# Optimizing a Trainium2 kernel written in Bass

```python
import numpy as np
import jax
import jax.numpy as jnp

def _softmax(x, axis=-1):
    return jax.nn.softmax(x, axis=axis)

def _gelu(x):
    return jax.nn.gelu(x, approximate=True)

def _silu(x):
    return jax.nn.silu(x)

def _sigmoid(x):
    return jax.nn.sigmoid(x)

def _layernorm(x, axis=-1, eps=1e-05):
    m = jnp.mean(x, axis=axis, keepdims=True)
    v = jnp.var(x, axis=axis, keepdims=True)
    return (x - m) / jnp.sqrt(v + eps)

def _scatter_add(tgt, idx, src, axis=0):
    return tgt.at[idx].add(src)

def _segment_sum(src, seg, n):
    return jax.ops.segment_sum(src, seg, n)
kernel_name = 'mk_perceiver_d4_seqx_r4_43c039'

def setup_inputs(seed: int=0):
    np.random.seed(seed)
    _w = jnp.asarray

    def _rec_inputs():
        import jax
        import jax.numpy as jnp
        _rk = jax.random.key(seed)
        x = -0.0002928 + 1 * jax.random.normal(jax.random.fold_in(_rk, 1), (2, 256, 256), jnp.float32)
        _lenS = 256 - jax.random.randint(jax.random.fold_in(_rk, 7), (2,), 0, max(1, 256 // 4) + 1, jnp.int32)
        _lenS2 = 4096 - jax.random.randint(jax.random.fold_in(_rk, 8), (2,), 0, max(1, 4096 // 4) + 1, jnp.int32)
        _ctx_1024P = jax.random.normal(jax.random.fold_in(_rk, 11), (2, 16, 256), jnp.float32)
        _ctx_1024c = jax.random.dirichlet(jax.random.fold_in(_rk, 511), 0.3 * jnp.ones((16,), jnp.float32), (2, 4096))
        _ctx_1024t = jnp.einsum('bsk,bkd->bsd', _ctx_1024c, _ctx_1024P)
        _ctx_1024t = _ctx_1024t * jax.lax.rsqrt(jnp.mean(jnp.square(_ctx_1024t)) + 1e-12) * 0.953939
        ctx_1024 = 4.13588e-05 + 0.999923 * (_ctx_1024t + 0.3 * jax.random.normal(jax.random.fold_in(_rk, 611), (2, 4096, 256), jnp.float32))
        _validS = jnp.arange(256)[None, :] < _lenS[:, None]
        _validS2 = jnp.arange(4096)[None, :] < _lenS2[:, None]
        _causal = jnp.tril(jnp.ones((256, 256), dtype=bool))
        mask_BxSxS2_bf0 = jnp.logical_not(jnp.ones((2, 256, 4096), dtype=bool))
        mask_BxSxS2_bk1 = jnp.broadcast_to(_validS2[:, None, :], (2, 256, 4096))
        mask_BxS2_ik1 = jnp.where(jnp.broadcast_to(_validS2[:, :], (2, 4096)), 1, 0).astype(jnp.int32)
        return (x, ctx_1024, mask_BxSxS2_bf0, mask_BxSxS2_bk1, mask_BxS2_ik1)
    x, ctx_1024, mask_BxSxS2_bf0, mask_BxSxS2_bk1, mask_BxS2_ik1 = _rec_inputs()

    def _L0_xattn_setup():
        import jax, jax.numpy as jnp
        import numpy as np
        HIDDEN = 256
        HEADS = 16
        D_K = HIDDEN // HEADS
        B, LQ, LKV = (4, 256, 512)
        NEG_INF = -1e+18
        key = jax.random.key(seed)
        ks = jax.random.split(key, 12)
        s = 1.0 / np.sqrt(HIDDEN)
        return {'tgt': jax.random.normal(ks[0], (B, LQ, HIDDEN), jnp.float32), 'memory': jax.random.normal(ks[1], (B, LKV, HIDDEN), jnp.float32), 'mask': jnp.zeros((B, LQ, LKV), dtype=bool), 'Wq': jax.random.normal(ks[2], (HIDDEN, HIDDEN), jnp.float32) * s, 'bq': jnp.zeros((HIDDEN,), jnp.float32), 'Wk': jax.random.normal(ks[3], (HIDDEN, HIDDEN), jnp.float32) * s, 'bk': jnp.zeros((HIDDEN,), jnp.float32), 'Wv': jax.random.normal(ks[4], (HIDDEN, HIDDEN), jnp.float32) * s, 'bv': jnp.zeros((HIDDEN,), jnp.float32), 'Wo': jax.random.normal(ks[5], (HIDDEN, HIDDEN), jnp.float32) * s, 'bo': jnp.zeros((HIDDEN,), jnp.float32)}
    _L0_xattn_all = _L0_xattn_setup()
    _L0_xattn_in = {k: v for k, v in _L0_xattn_all.items() if k in ('Wq', 'bq', 'Wk', 'bk', 'Wv', 'bv', 'Wo', 'bo')}
    del _L0_xattn_all

    def _L0_attn_setup():
        import jax, jax.numpy as jnp
        import numpy as np
        D_MODEL = 256
        N_HEADS = 16

        def get_freqs(seq, n_dim):
            inv = 1.0 / 10000.0 ** (jnp.arange(0, n_dim, 2, dtype=jnp.float32) / n_dim)
            pos = jnp.arange(seq, dtype=jnp.float32)
            return pos[:, None] * inv[None, :]

        def rope(x, freq):
            xf = x.astype(jnp.float32)
            x1 = xf[..., 0::2]
            x2 = xf[..., 1::2]
            cos = jnp.cos(freq)[None, :, None, :]
            sin = jnp.sin(freq)[None, :, None, :]
            r1 = x1 * cos - x2 * sin
            r2 = x1 * sin + x2 * cos
            out = jnp.stack([r1, r2], axis=-1).reshape(x.shape)
            return out.astype(x.dtype)
        key = jax.random.key(seed)
        k1, k2, k3, k4, k5 = jax.random.split(key, 5)
        batch, seq = (2, 512)
        x = jax.random.normal(k1, (batch, seq, D_MODEL), dtype=jnp.float16)
        scale = jnp.float16(0.02)
        qw = jax.random.normal(k2, (D_MODEL, D_MODEL), dtype=jnp.float16) * scale
        kw = jax.random.normal(k3, (D_MODEL, D_MODEL), dtype=jnp.float16) * scale
        vw = jax.random.normal(k4, (D_MODEL, D_MODEL), dtype=jnp.float16) * scale
        ow = jax.random.normal(k5, (D_MODEL, D_MODEL), dtype=jnp.float16) * scale
        return {'x': x, 'qw': qw, 'kw': kw, 'vw': vw, 'ow': ow}
    _L0_attn_all = _L0_attn_setup()
    _L0_attn_in = {k: v for k, v in _L0_attn_all.items() if k in ('qw', 'kw', 'vw', 'ow')}
    del _L0_attn_all

    def _L0_ffn_setup():
        import jax, jax.numpy as jnp
        import numpy as np
        TOP_K = 2

        def gelu(x):
            return jax.nn.gelu(x, approximate=False)
        key = jax.random.key(seed)
        ks = jax.random.split(key, 6)
        B, L, D, H, E, S = (4, 512, 256, 512, 8, 2)
        sd = 0.02
        return {'x': jax.random.normal(ks[0], (B, L, D), dtype=jnp.float32), 'router_w': jax.random.normal(ks[1], (D, E), dtype=jnp.float32) * sd, 'router_b': jnp.zeros((E,), dtype=jnp.float32), 'w1': jax.random.normal(ks[2], (E, D, H), dtype=jnp.float32) * sd, 'b1': jnp.zeros((E, H), dtype=jnp.float32), 'w2': jax.random.normal(ks[3], (E, H, D), dtype=jnp.float32) * sd, 'b2': jnp.zeros((E, D), dtype=jnp.float32), 'sw1': jax.random.normal(ks[4], (S, D, H), dtype=jnp.float32) * sd, 'sb1': jnp.zeros((S, H), dtype=jnp.float32), 'sw2': jax.random.normal(ks[5], (S, H, D), dtype=jnp.float32) * sd, 'sb2': jnp.zeros((S, D), dtype=jnp.float32)}
    _L0_ffn_all = _L0_ffn_setup()
    _L0_ffn_in = {k: v for k, v in _L0_ffn_all.items() if k in ('router_w', 'router_b', 'w1', 'b1', 'w2', 'b2', 'sw1', 'sb1', 'sw2', 'sb2')}
    del _L0_ffn_all

    def _L1_xattn_setup():
        import jax, jax.numpy as jnp
        import numpy as np
        DIM = 256
        HEADS = 16
        DIM_HEAD = 64
        INNER = HEADS * DIM_HEAD
        B, N = (2, 512)
        key = jax.random.key(seed)
        ks = jax.random.split(key, 8)
        q = jax.random.normal(ks[0], (B, N, DIM), dtype=jnp.float32)
        k = jax.random.normal(ks[1], (B, N, DIM), dtype=jnp.float32)
        v = jax.random.normal(ks[2], (B, N, DIM), dtype=jnp.float32)
        causal = jnp.triu(jnp.ones((N, N), dtype=jnp.bool_), k=1)
        mask = jnp.broadcast_to(causal, (B, N, N))
        s = 0.02
        Wq = jax.random.normal(ks[3], (DIM, INNER), dtype=jnp.float32) * s
        Wk = jax.random.normal(ks[4], (DIM, INNER), dtype=jnp.float32) * s
        Wv = jax.random.normal(ks[5], (DIM, INNER), dtype=jnp.float32) * s
        Wo = jax.random.normal(ks[6], (INNER, DIM), dtype=jnp.float32) * s
        bo = jnp.zeros((DIM,), dtype=jnp.float32)
        return {'q': q, 'k': k, 'v': v, 'mask': mask, 'Wq': Wq, 'Wk': Wk, 'Wv': Wv, 'Wo': Wo, 'bo': bo}
    _L1_xattn_all = _L1_xattn_setup()
    _L1_xattn_in = {k: v for k, v in _L1_xattn_all.items() if k in ('Wq', 'Wk', 'Wv', 'Wo', 'bo')}
    del _L1_xattn_all

    def _L1_attn_setup():
        import jax, jax.numpy as jnp
        import numpy as np
        import math
        N, S, E, H = (4, 1024, 256, 16)
        D = E // H
        key = jax.random.key(seed)
        ks = jax.random.split(key, 9)
        w = 1.0 / math.sqrt(E)
        mk = lambda k, shape: jax.random.normal(k, shape, jnp.float32) * w
        return {'x': jax.random.normal(ks[0], (N, S, E), jnp.float32), 'Wq': mk(ks[1], (E, E)), 'bq': mk(ks[2], (E,)), 'Wk': mk(ks[3], (E, E)), 'bk': mk(ks[4], (E,)), 'Wv': mk(ks[5], (E, E)), 'bv': mk(ks[6], (E,)), 'Wo': mk(ks[7], (E, E)), 'bo': mk(ks[8], (E,))}
    _L1_attn_all = _L1_attn_setup()
    _L1_attn_in = {k: v for k, v in _L1_attn_all.items() if k in ('Wq', 'bq', 'Wk', 'bk', 'Wv', 'bv', 'Wo', 'bo')}
    del _L1_attn_all

    def _L1_ffn_setup():
        import jax, jax.numpy as jnp
        import numpy as np
        D, H, E, K, S = (256, 512, 8, 2, 1)
        B, L = (4, 512)
        key = jax.random.key(seed)
        ks = jax.random.split(key, 9)
        std = 0.02
        return {'x': jax.random.normal(ks[0], (B, L, D), dtype=jnp.float32), 'router_w': jax.random.normal(ks[1], (E, D), dtype=jnp.float32) * std, 'experts_bias': jnp.zeros((E,), dtype=jnp.float32), 'w1': jax.random.normal(ks[2], (E, D, H), dtype=jnp.float32) * std, 'w3': jax.random.normal(ks[3], (E, D, H), dtype=jnp.float32) * std, 'w2': jax.random.normal(ks[4], (E, H, D), dtype=jnp.float32) * std, 'sw1': jax.random.normal(ks[5], (S, D, H), dtype=jnp.float32) * std, 'sw3': jax.random.normal(ks[6], (S, D, H), dtype=jnp.float32) * std, 'sw2': jax.random.normal(ks[7], (S, H, D), dtype=jnp.float32) * std}
    _L1_ffn_all = _L1_ffn_setup()
    _L1_ffn_in = {k: v for k, v in _L1_ffn_all.items() if k in ('router_w', 'experts_bias', 'w1', 'w3', 'w2', 'sw1', 'sw3', 'sw2')}
    del _L1_ffn_all

    def _L2_xattn_setup():
        import jax, jax.numpy as jnp
        import numpy as np
        EMBED_DIM = 256
        NUM_HEADS = 16
        HEAD_DIM = EMBED_DIM // NUM_HEADS
        key = jax.random.key(seed)
        ks = jax.random.split(key, 8)
        B, S, D = (2, 512, EMBED_DIM)
        scale = 1.0 / np.sqrt(D)
        return {'query': jax.random.normal(ks[0], (B, S, D), dtype=jnp.float32), 'key': jax.random.normal(ks[1], (B, S, D), dtype=jnp.float32), 'value': jax.random.normal(ks[2], (B, S, D), dtype=jnp.float32), 'Wq': jax.random.normal(ks[3], (D, D), dtype=jnp.float32) * scale, 'Wk': jax.random.normal(ks[4], (D, D), dtype=jnp.float32) * scale, 'Wv': jax.random.normal(ks[5], (D, D), dtype=jnp.float32) * scale, 'Wo': jax.random.normal(ks[6], (D, D), dtype=jnp.float32) * scale, 'attention_mask': jax.random.randint(ks[7], (B, S), 0, 2, dtype=jnp.int32)}
    _L2_xattn_all = _L2_xattn_setup()
    _L2_xattn_in = {k: v for k, v in _L2_xattn_all.items() if k in ('Wq', 'Wk', 'Wv', 'Wo')}
    del _L2_xattn_all

    def _L2_attn_setup():
        import jax, jax.numpy as jnp
        import numpy as np
        from jax import lax
        D_MODEL, D_STATE, EXPAND, K = (256, 16, 2, 4)
        D_INNER = D_MODEL * EXPAND
        B, L = (2, 512)

        def _selective_ssm(x, A_log, D_skip, W_delta, b_delta, W_B, W_C):
            A = -jnp.exp(A_log)
            delta = jax.nn.softplus(x @ W_delta + b_delta)
            Bm = x @ W_B
            Cm = x @ W_C
            h0 = jnp.zeros((x.shape[0], A.shape[0], A.shape[1]), x.dtype)

            def step(h, inp):
                d_t, x_t, B_t, C_t = inp
                dA = jnp.exp(d_t[..., None] * A)
                h = dA * h + (d_t * x_t)[..., None] * B_t[:, None, :]
                y_t = jnp.einsum('bdn,bn->bd', h, C_t)
                return (h, y_t)
            xs = (delta.transpose(1, 0, 2), x.transpose(1, 0, 2), Bm.transpose(1, 0, 2), Cm.transpose(1, 0, 2))
            _, ys = lax.scan(step, h0, xs)
            return ys.transpose(1, 0, 2) + x * D_skip
        key = jax.random.key(seed)
        ks = jax.random.split(key, 16)
        s = lambda fan_in: 1.0 / np.sqrt(fan_in)
        inp = {'x': jax.random.normal(ks[0], (B, L, D_MODEL), jnp.float32), 'W_in': jax.random.normal(ks[1], (D_MODEL, D_INNER), jnp.float32) * s(D_MODEL), 'b_in': jnp.zeros((D_INNER,), jnp.float32), 'W_gate': jax.random.normal(ks[2], (D_MODEL, D_INNER), jnp.float32) * s(D_MODEL), 'b_gate': jnp.zeros((D_INNER,), jnp.float32), 'conv_w': jax.random.normal(ks[3], (D_INNER, 1, K), jnp.float32) * s(K), 'conv_b': jnp.zeros((D_INNER,), jnp.float32), 'A_log': jnp.log(jnp.broadcast_to(jnp.arange(1, D_STATE + 1, dtype=jnp.float32), (D_INNER, D_STATE))), 'D_skip': jnp.ones((D_INNER,), jnp.float32), 'W_delta': jax.random.normal(ks[4], (D_INNER, D_INNER), jnp.float32) * s(D_INNER), 'b_delta': jnp.zeros((D_INNER,), jnp.float32), 'W_B': jax.random.normal(ks[5], (D_INNER, D_STATE), jnp.float32) * s(D_INNER), 'W_C': jax.random.normal(ks[6], (D_INNER, D_STATE), jnp.float32) * s(D_INNER), 'W_out': jax.random.normal(ks[7], (D_INNER, D_MODEL), jnp.float32) * s(D_INNER), 'b_out': jnp.zeros((D_MODEL,), jnp.float32)}
        return inp
    _L2_attn_all = _L2_attn_setup()
    _L2_attn_in = {k: v for k, v in _L2_attn_all.items() if k in ('W_in', 'b_in', 'W_gate', 'b_gate', 'conv_w', 'conv_b', 'A_log', 'D_skip', 'W_delta', 'b_delta', 'W_B', 'W_C', 'W_out', 'b_out')}
    del _L2_attn_all

    def _L2_ffn_setup():
        import jax, jax.numpy as jnp
        import numpy as np
        import math
        D_IN = 256
        FEATURES = (1024, 1024, 256)
        BATCH, SEQ = (8, 512)

        def _conn_dense(kernel_bool, x):
            w = jnp.where(kernel_bool, jnp.float32(1.0), jnp.float32(-1.0))
            return x @ w
        key = jax.random.key(seed)
        kx, kk0, kk1, kk2 = jax.random.split(key, 4)
        x = jax.random.normal(kx, (BATCH, SEQ, D_IN), dtype=jnp.float32)
        k0 = jax.random.randint(kk0, (2 * D_IN, FEATURES[0]), 0, 2).astype(jnp.bool_)
        k1 = jax.random.randint(kk1, (FEATURES[0], FEATURES[1]), 0, 2).astype(jnp.bool_)
        k2 = jax.random.randint(kk2, (FEATURES[1], FEATURES[2]), 0, 2).astype(jnp.bool_)
        s0 = jnp.asarray(1.0 / math.sqrt(2 * D_IN), dtype=jnp.float32)
        s1 = jnp.asarray(1.0 / math.sqrt(FEATURES[0]), dtype=jnp.float32)
        s2 = jnp.asarray(1.0 / math.sqrt(FEATURES[1]), dtype=jnp.float32)
        return {'x': x, 'k0': k0, 'k1': k1, 'k2': k2, 's0': s0, 's1': s1, 's2': s2}
    _L2_ffn_all = _L2_ffn_setup()
    _L2_ffn_in = {k: v for k, v in _L2_ffn_all.items() if k in ('k0', 'k1', 'k2', 's0', 's1', 's2')}
    del _L2_ffn_all

    def _L3_xattn_setup():
        import jax, jax.numpy as jnp
        import numpy as np
        B, TQ, TV, H = (8, 512, 512, 256)
        LN_EPS = 1e-05
        key = jax.random.key(seed)
        k1, k2, k3, k4 = jax.random.split(key, 4)
        query = jax.random.normal(k1, (B, TQ, H), dtype=jnp.float32)
        value = jax.random.normal(k2, (B, TV, H), dtype=jnp.float32)
        bound = 1.0 / np.sqrt(2 * H)
        W = jax.random.uniform(k3, (H, 2 * H), minval=-bound, maxval=bound, dtype=jnp.float32)
        b = jax.random.uniform(k4, (H,), minval=-bound, maxval=bound, dtype=jnp.float32)
        gamma = jnp.ones((H,), dtype=jnp.float32)
        beta = jnp.zeros((H,), dtype=jnp.float32)
        return {'query': query, 'value': value, 'W': W, 'b': b, 'gamma': gamma, 'beta': beta}
    _L3_xattn_all = _L3_xattn_setup()
    _L3_xattn_in = {k: v for k, v in _L3_xattn_all.items() if k in ('W', 'b', 'gamma', 'beta')}
    del _L3_xattn_all

    def _L3_attn_setup():
        import jax, jax.numpy as jnp
        import numpy as np
        EMBED_DIM = 256
        NUM_HEADS = 16
        HEAD_DIM = EMBED_DIM // NUM_HEADS
        BATCH = 2
        SEQ = 512
        NEG_INF = float('-inf')
        key = jax.random.key(seed)
        k1, k2, k3, k4, k5 = jax.random.split(key, 5)
        return {'query': jax.random.normal(k1, (BATCH, SEQ, EMBED_DIM), dtype=jnp.float32), 'key': jax.random.normal(k2, (BATCH, SEQ, EMBED_DIM), dtype=jnp.float32), 'value': jax.random.normal(k3, (BATCH, SEQ, EMBED_DIM), dtype=jnp.float32), 'in_proj_weight': jax.random.normal(k4, (3 * EMBED_DIM, EMBED_DIM), dtype=jnp.float32) * (1.0 / np.sqrt(EMBED_DIM)), 'out_proj_weight': jax.random.normal(k5, (EMBED_DIM, EMBED_DIM), dtype=jnp.float32) * (1.0 / np.sqrt(EMBED_DIM))}
    _L3_attn_all = _L3_attn_setup()
    _L3_attn_in = {k: v for k, v in _L3_attn_all.items() if k in ('key', 'value', 'in_proj_weight', 'out_proj_weight')}
    del _L3_attn_all

    def _L3_ffn_setup():
        import jax, jax.numpy as jnp
        import numpy as np
        EPS = 1e-08

        def _ste(x, q):
            return x + jax.lax.stop_gradient(q - x)

        def quant_act_uint8(x):
            s = jax.lax.stop_gradient(jnp.maximum(jnp.max(x), EPS)) / 255.0
            q = jnp.clip(jnp.round(x / s), 0.0, 255.0) * s
            return (_ste(x, q), s)

        def quant_weight_int8_perchannel(w):
            s = jax.lax.stop_gradient(jnp.maximum(jnp.max(jnp.abs(w), axis=1, keepdims=True), EPS)) / 127.0
            q = jnp.clip(jnp.round(w / s), -128.0, 127.0) * s
            return (_ste(w, q), s[:, 0])

        def quant_bias_int32(b, s_in, s_w):
            s = jax.lax.stop_gradient(s_in * s_w)
            q = jnp.round(b / s) * s
            return _ste(b, q)

        def quant_linear(x, w, b):
            xq, s_in = quant_act_uint8(x)
            wq, s_w = quant_weight_int8_perchannel(w)
            bq = quant_bias_int32(b, s_in, s_w)
            return jnp.einsum('btd,fd->btf', xq, wq) + bq
        key = jax.random.key(seed)
        k1, k2, k3, k4, k5 = jax.random.split(key, 5)
        B, S, D, F = (4, 512, 256, 1024)
        return {'x': jax.random.normal(k1, (B, S, D), dtype=jnp.float32), 'w1': jax.random.normal(k2, (F, D), dtype=jnp.float32) * (1.0 / np.sqrt(D)), 'b1': jax.random.normal(k3, (F,), dtype=jnp.float32) * 0.01, 'w2': jax.random.normal(k4, (D, F), dtype=jnp.float32) * (1.0 / np.sqrt(F)), 'b2': jax.random.normal(k5, (D,), dtype=jnp.float32) * 0.01}
    _L3_ffn_all = _L3_ffn_setup()
    _L3_ffn_in = {k: v for k, v in _L3_ffn_all.items() if k in ('w1', 'b1', 'w2', 'b2')}
    del _L3_ffn_all
    return {'x': x, 'ctx_1024': ctx_1024, 'mask_BxSxS2_bf0': mask_BxSxS2_bf0, 'mask_BxSxS2_bk1': mask_BxSxS2_bk1, 'mask_BxS2_ik1': mask_BxS2_ik1, 'L0_xattn_Wq': _L0_xattn_in['Wq'], 'L0_xattn_bq': _L0_xattn_in['bq'], 'L0_xattn_Wk': _L0_xattn_in['Wk'], 'L0_xattn_bk': _L0_xattn_in['bk'], 'L0_xattn_Wv': _L0_xattn_in['Wv'], 'L0_xattn_bv': _L0_xattn_in['bv'], 'L0_xattn_Wo': _L0_xattn_in['Wo'], 'L0_xattn_bo': _L0_xattn_in['bo'], 'L0_attn_qw': _L0_attn_in['qw'], 'L0_attn_kw': _L0_attn_in['kw'], 'L0_attn_vw': _L0_attn_in['vw'], 'L0_attn_ow': _L0_attn_in['ow'], 'L0_ffn_router_w': _L0_ffn_in['router_w'], 'L0_ffn_router_b': _L0_ffn_in['router_b'], 'L0_ffn_w1': _L0_ffn_in['w1'], 'L0_ffn_b1': _L0_ffn_in['b1'], 'L0_ffn_w2': _L0_ffn_in['w2'], 'L0_ffn_b2': _L0_ffn_in['b2'], 'L0_ffn_sw1': _L0_ffn_in['sw1'], 'L0_ffn_sb1': _L0_ffn_in['sb1'], 'L0_ffn_sw2': _L0_ffn_in['sw2'], 'L0_ffn_sb2': _L0_ffn_in['sb2'], 'L1_xattn_Wq': _L1_xattn_in['Wq'], 'L1_xattn_Wk': _L1_xattn_in['Wk'], 'L1_xattn_Wv': _L1_xattn_in['Wv'], 'L1_xattn_Wo': _L1_xattn_in['Wo'], 'L1_xattn_bo': _L1_xattn_in['bo'], 'L1_attn_Wq': _L1_attn_in['Wq'], 'L1_attn_bq': _L1_attn_in['bq'], 'L1_attn_Wk': _L1_attn_in['Wk'], 'L1_attn_bk': _L1_attn_in['bk'], 'L1_attn_Wv': _L1_attn_in['Wv'], 'L1_attn_bv': _L1_attn_in['bv'], 'L1_attn_Wo': _L1_attn_in['Wo'], 'L1_attn_bo': _L1_attn_in['bo'], 'L1_ffn_router_w': _L1_ffn_in['router_w'], 'L1_ffn_experts_bias': _L1_ffn_in['experts_bias'], 'L1_ffn_w1': _L1_ffn_in['w1'], 'L1_ffn_w3': _L1_ffn_in['w3'], 'L1_ffn_w2': _L1_ffn_in['w2'], 'L1_ffn_sw1': _L1_ffn_in['sw1'], 'L1_ffn_sw3': _L1_ffn_in['sw3'], 'L1_ffn_sw2': _L1_ffn_in['sw2'], 'L2_xattn_Wq': _L2_xattn_in['Wq'], 'L2_xattn_Wk': _L2_xattn_in['Wk'], 'L2_xattn_Wv': _L2_xattn_in['Wv'], 'L2_xattn_Wo': _L2_xattn_in['Wo'], 'L2_attn_W_in': _L2_attn_in['W_in'], 'L2_attn_b_in': _L2_attn_in['b_in'], 'L2_attn_W_gate': _L2_attn_in['W_gate'], 'L2_attn_b_gate': _L2_attn_in['b_gate'], 'L2_attn_conv_w': _L2_attn_in['conv_w'], 'L2_attn_conv_b': _L2_attn_in['conv_b'], 'L2_attn_A_log': _L2_attn_in['A_log'], 'L2_attn_D_skip': _L2_attn_in['D_skip'], 'L2_attn_W_delta': _L2_attn_in['W_delta'], 'L2_attn_b_delta': _L2_attn_in['b_delta'], 'L2_attn_W_B': _L2_attn_in['W_B'], 'L2_attn_W_C': _L2_attn_in['W_C'], 'L2_attn_W_out': _L2_attn_in['W_out'], 'L2_attn_b_out': _L2_attn_in['b_out'], 'L2_ffn_k0': _L2_ffn_in['k0'], 'L2_ffn_k1': _L2_ffn_in['k1'], 'L2_ffn_k2': _L2_ffn_in['k2'], 'L2_ffn_s0': _L2_ffn_in['s0'], 'L2_ffn_s1': _L2_ffn_in['s1'], 'L2_ffn_s2': _L2_ffn_in['s2'], 'L3_xattn_W': _L3_xattn_in['W'], 'L3_xattn_b': _L3_xattn_in['b'], 'L3_xattn_gamma': _L3_xattn_in['gamma'], 'L3_xattn_beta': _L3_xattn_in['beta'], 'L3_attn_key': _L3_attn_in['key'], 'L3_attn_value': _L3_attn_in['value'], 'L3_attn_in_proj_weight': _L3_attn_in['in_proj_weight'], 'L3_attn_out_proj_weight': _L3_attn_in['out_proj_weight'], 'L3_ffn_w1': _L3_ffn_in['w1'], 'L3_ffn_b1': _L3_ffn_in['b1'], 'L3_ffn_w2': _L3_ffn_in['w2'], 'L3_ffn_b2': _L3_ffn_in['b2']}

def reference(x, ctx_1024, mask_BxSxS2_bf0, mask_BxSxS2_bk1, mask_BxS2_ik1, L0_xattn_Wq, L0_xattn_bq, L0_xattn_Wk, L0_xattn_bk, L0_xattn_Wv, L0_xattn_bv, L0_xattn_Wo, L0_xattn_bo, L0_attn_qw, L0_attn_kw, L0_attn_vw, L0_attn_ow, L0_ffn_router_w, L0_ffn_router_b, L0_ffn_w1, L0_ffn_b1, L0_ffn_w2, L0_ffn_b2, L0_ffn_sw1, L0_ffn_sb1, L0_ffn_sw2, L0_ffn_sb2, L1_xattn_Wq, L1_xattn_Wk, L1_xattn_Wv, L1_xattn_Wo, L1_xattn_bo, L1_attn_Wq, L1_attn_bq, L1_attn_Wk, L1_attn_bk, L1_attn_Wv, L1_attn_bv, L1_attn_Wo, L1_attn_bo, L1_ffn_router_w, L1_ffn_experts_bias, L1_ffn_w1, L1_ffn_w3, L1_ffn_w2, L1_ffn_sw1, L1_ffn_sw3, L1_ffn_sw2, L2_xattn_Wq, L2_xattn_Wk, L2_xattn_Wv, L2_xattn_Wo, L2_attn_W_in, L2_attn_b_in, L2_attn_W_gate, L2_attn_b_gate, L2_attn_conv_w, L2_attn_conv_b, L2_attn_A_log, L2_attn_D_skip, L2_attn_W_delta, L2_attn_b_delta, L2_attn_W_B, L2_attn_W_C, L2_attn_W_out, L2_attn_b_out, L2_ffn_k0, L2_ffn_k1, L2_ffn_k2, L2_ffn_s0, L2_ffn_s1, L2_ffn_s2, L3_xattn_W, L3_xattn_b, L3_xattn_gamma, L3_xattn_beta, L3_attn_key, L3_attn_value, L3_attn_in_proj_weight, L3_attn_out_proj_weight, L3_ffn_w1, L3_ffn_b1, L3_ffn_w2, L3_ffn_b2):
    import jax
    import jax.numpy as jnp

    def _L0_xattn_ref(tgt, memory, mask, Wq, bq, Wk, bk, Wv, bv, Wo, bo):
        import jax, jax.numpy as jnp
        import numpy as np
        HIDDEN = 256
        HEADS = 16
        D_K = HIDDEN // HEADS
        B, LQ, LKV = (4, 256, 512)
        NEG_INF = -1e+18
        b = tgt.shape[0]

        def heads(x):
            return x.reshape(b, -1, HEADS, D_K).transpose(0, 2, 1, 3)
        q = heads(tgt @ Wq + bq) / jnp.sqrt(jnp.asarray(D_K, tgt.dtype))
        k = heads(memory @ Wk + bk)
        v = heads(memory @ Wv + bv)
        scores = jnp.einsum('bhqd,bhkd->bhqk', q, k)
        scores = jnp.where(mask[:, None, :, :], NEG_INF, scores)
        attn = jax.nn.softmax(scores, axis=-1)
        ctx = jnp.einsum('bhqk,bhkd->bhqd', attn, v)
        ctx = ctx.transpose(0, 2, 1, 3).reshape(b, -1, HIDDEN)
        return ctx @ Wo + bo

    def _L0_attn_ref(x, qw, kw, vw, ow):
        import jax, jax.numpy as jnp
        import numpy as np
        D_MODEL = 256
        N_HEADS = 16

        def get_freqs(seq, n_dim):
            inv = 1.0 / 10000.0 ** (jnp.arange(0, n_dim, 2, dtype=jnp.float32) / n_dim)
            pos = jnp.arange(seq, dtype=jnp.float32)
            return pos[:, None] * inv[None, :]

        def rope(x, freq):
            xf = x.astype(jnp.float32)
            x1 = xf[..., 0::2]
            x2 = xf[..., 1::2]
            cos = jnp.cos(freq)[None, :, None, :]
            sin = jnp.sin(freq)[None, :, None, :]
            r1 = x1 * cos - x2 * sin
            r2 = x1 * sin + x2 * cos
            out = jnp.stack([r1, r2], axis=-1).reshape(x.shape)
            return out.astype(x.dtype)
        batch, seq, dim = x.shape
        n_heads = N_HEADS
        n_dim = dim // n_heads
        Q = (x @ qw).reshape(batch, seq, n_heads, n_dim)
        K = (x @ kw).reshape(batch, seq, n_heads, n_dim)
        V = (x @ vw).reshape(batch, seq, n_heads, n_dim)
        freq = get_freqs(seq, n_dim)
        Q = rope(Q, freq)
        K = rope(K, freq)
        Q = jnp.transpose(Q, (0, 2, 1, 3))
        K = jnp.transpose(K, (0, 2, 1, 3))
        V = jnp.transpose(V, (0, 2, 1, 3))
        score = Q @ jnp.swapaxes(K, -1, -2) / jnp.sqrt(jnp.float16(dim))
        score = score.astype(jnp.float32)
        mask = jnp.tril(jnp.ones((1, 1, seq, seq), dtype=jnp.float32))
        score = score - 10000000000.0 * (1.0 - mask)
        weights = jax.nn.softmax(score, axis=-1)
        attn = weights @ V.astype(jnp.float32)
        merged = jnp.transpose(attn, (0, 2, 1, 3)).reshape(batch, seq, dim)
        out = merged @ ow.astype(jnp.float32)
        return out

    def _L0_ffn_ref(x, router_w, router_b, w1, b1, w2, b2, sw1, sb1, sw2, sb2):
        import jax, jax.numpy as jnp
        import numpy as np
        TOP_K = 2

        def gelu(x):
            return jax.nn.gelu(x, approximate=False)
        B, L, D = x.shape
        E = router_b.shape[0]
        S = sw1.shape[0]
        xf = x.reshape(-1, D)
        sh = gelu(jnp.einsum('nd,sdh->snh', xf, sw1) + sb1[:, None, :])
        shared_out = (jnp.einsum('snh,shd->nd', sh, sw2) + sb2.sum(0)) / S
        gates = xf @ router_w + router_b
        topv, topi = jax.lax.top_k(gates, TOP_K)
        probs = jax.nn.softmax(topv, axis=-1)
        comb = jnp.einsum('nke,nk->ne', jax.nn.one_hot(topi, E, dtype=xf.dtype), probs)
        h = gelu(jnp.einsum('nd,edh->enh', xf, w1) + b1[:, None, :])
        y = jnp.einsum('enh,ehd->end', h, w2) + b2[:, None, :]
        moe_out = jnp.einsum('ne,end->nd', comb, y)
        return (shared_out + moe_out).reshape(B, L, D)

    def _L1_xattn_ref(q, k, v, mask, Wq, Wk, Wv, Wo, bo):
        import jax, jax.numpy as jnp
        import numpy as np
        DIM = 256
        HEADS = 16
        DIM_HEAD = 64
        INNER = HEADS * DIM_HEAD
        B, N = (2, 512)
        h, d = (HEADS, DIM_HEAD)
        scale = d ** (-0.5)
        b, n, _ = q.shape

        def heads_split(x):
            return x.reshape(b, -1, h, d).transpose(0, 2, 1, 3)
        qh = heads_split(q @ Wq)
        kh = heads_split(k @ Wk)
        vh = heads_split(v @ Wv)
        dots = jnp.einsum('bhid,bhjd->bhij', qh, kh) * scale
        mask_value = -jnp.finfo(dots.dtype).max
        dots = jnp.where(mask[:, None, :, :], mask_value, dots)
        attn = jax.nn.softmax(dots, axis=-1)
        out = jnp.einsum('bhij,bhjd->bhid', attn, vh)
        out = out.transpose(0, 2, 1, 3).reshape(b, n, h * d)
        out = out @ Wo + bo
        return out

    def _L1_attn_ref(x, Wq, bq, Wk, bk, Wv, bv, Wo, bo):
        import jax, jax.numpy as jnp
        import numpy as np
        import math
        N, S, E, H = (4, 1024, 256, 16)
        D = E // H
        n, s, e = x.shape
        h, d = (H, D)
        scale = 1.0 / math.sqrt(d)

        def proj(W, b):
            y = jnp.einsum('nse,fe->nsf', x, W) + b
            return y.reshape(n, s, h, d).transpose(0, 2, 1, 3)
        Q = proj(Wq, bq)
        K = proj(Wk, bk)
        V = proj(Wv, bv)
        scores = jnp.einsum('nqhd,nkhd->nhqk', Q, K) * scale
        attn = jax.nn.softmax(scores, axis=-1)
        out = jnp.einsum('nhql,nlhd->nqhd', attn, V)
        out = out.reshape(n, s, e)
        return jnp.einsum('nse,fe->nsf', out, Wo) + bo

    def _L1_ffn_ref(x, router_w, experts_bias, w1, w3, w2, sw1, sw3, sw2):
        import jax, jax.numpy as jnp
        import numpy as np
        D, H, E, K, S = (256, 512, 8, 2, 1)
        B, L = (4, 512)
        b, l, d = x.shape
        xf = x.reshape(-1, d)
        sg = jnp.einsum('td,sdh->tsh', xf, sw1)
        su = jnp.einsum('td,sdh->tsh', xf, sw3)
        shared_out = jnp.einsum('tsh,shd->td', jax.nn.silu(sg) * su, sw2)
        logits = xf @ router_w.T + experts_bias
        rw, sel = jax.lax.top_k(logits, K)
        rw = jax.nn.softmax(rw.astype(jnp.float32), axis=-1).astype(x.dtype)
        cw = (jax.nn.one_hot(sel, E, dtype=x.dtype) * rw[..., None]).sum(axis=1)
        g = jnp.einsum('td,edh->teh', xf, w1)
        u = jnp.einsum('td,edh->teh', xf, w3)
        eo = jax.nn.silu(g) * u
        moe_out = jnp.einsum('te,teh,ehd->td', cw, eo, w2)
        return (moe_out + shared_out).reshape(b, l, d)

    def _L2_xattn_ref(query, key, value, Wq, Wk, Wv, Wo, attention_mask):
        import jax, jax.numpy as jnp
        import numpy as np
        EMBED_DIM = 256
        NUM_HEADS = 16
        HEAD_DIM = EMBED_DIM // NUM_HEADS
        B, Sq, D = query.shape
        Sk = key.shape[1]
        H, hd = (NUM_HEADS, HEAD_DIM)
        q = (query @ Wq).reshape(B, Sq, H, hd).transpose(0, 2, 1, 3)
        k = (key @ Wk).reshape(B, Sk, H, hd).transpose(0, 2, 1, 3)
        v = (value @ Wv).reshape(B, Sk, H, hd).transpose(0, 2, 1, 3)
        scores = jnp.einsum('bhqd,bhkd->bhqk', q, k) / jnp.sqrt(jnp.float32(hd))
        mask = attention_mask[:, None, None, :]
        scores = jnp.where(mask == 0, -jnp.inf, scores)
        weights = jax.nn.softmax(scores, axis=-1)
        out = jnp.einsum('bhqk,bhkd->bhqd', weights, v)
        out = out.transpose(0, 2, 1, 3).reshape(B, Sq, D)
        return out @ Wo

    def _L2_attn_ref(x, W_in, b_in, W_gate, b_gate, conv_w, conv_b, A_log, D_skip, W_delta, b_delta, W_B, W_C, W_out, b_out):
        import jax, jax.numpy as jnp
        import numpy as np
        from jax import lax
        D_MODEL, D_STATE, EXPAND, K = (256, 16, 2, 4)
        D_INNER = D_MODEL * EXPAND
        B, L = (2, 512)

        def _selective_ssm(x, A_log, D_skip, W_delta, b_delta, W_B, W_C):
            A = -jnp.exp(A_log)
            delta = jax.nn.softplus(x @ W_delta + b_delta)
            Bm = x @ W_B
            Cm = x @ W_C
            h0 = jnp.zeros((x.shape[0], A.shape[0], A.shape[1]), x.dtype)

            def step(h, inp):
                d_t, x_t, B_t, C_t = inp
                dA = jnp.exp(d_t[..., None] * A)
                h = dA * h + (d_t * x_t)[..., None] * B_t[:, None, :]
                y_t = jnp.einsum('bdn,bn->bd', h, C_t)
                return (h, y_t)
            xs = (delta.transpose(1, 0, 2), x.transpose(1, 0, 2), Bm.transpose(1, 0, 2), Cm.transpose(1, 0, 2))
            _, ys = lax.scan(step, h0, xs)
            return ys.transpose(1, 0, 2) + x * D_skip
        xz = x @ W_in + b_in
        x_gate = x @ W_gate + b_gate
        x_conv = lax.conv_general_dilated(xz.transpose(0, 2, 1), conv_w, window_strides=(1,), padding=[(K - 1, 0)], dimension_numbers=('NCH', 'OIH', 'NCH'), feature_group_count=D_INNER)
        x_conv = x_conv.transpose(0, 2, 1) + conv_b
        act = jax.nn.silu(x_conv)
        ssm_out = _selective_ssm(act, A_log, D_skip, W_delta, b_delta, W_B, W_C)
        gated = ssm_out * jax.nn.silu(x_gate)
        return gated @ W_out + b_out

    def _L2_ffn_ref(x, k0, k1, k2, s0, s1, s2):
        import jax, jax.numpy as jnp
        import numpy as np
        import math
        D_IN = 256
        FEATURES = (1024, 1024, 256)
        BATCH, SEQ = (8, 512)

        def _conn_dense(kernel_bool, x):
            w = jnp.where(kernel_bool, jnp.float32(1.0), jnp.float32(-1.0))
            return x @ w
        h = jnp.concatenate([x, -x], axis=-1)
        h = s0 * _conn_dense(k0, h)
        h = jax.nn.relu(h) * 2
        h = s1 * _conn_dense(k1, h)
        h = jax.nn.relu(h) * 2
        h = s2 * _conn_dense(k2, h)
        return h

    def _L3_xattn_ref(query, value, W, b, gamma, beta):
        import jax, jax.numpy as jnp
        import numpy as np
        B, TQ, TV, H = (8, 512, 512, 256)
        LN_EPS = 1e-05
        score = jnp.einsum('bqh,bvh->bqv', query, value)
        attn = jax.nn.softmax(score, axis=-1)
        context = jnp.einsum('bqv,bvh->bqh', attn, value)
        combined = jnp.concatenate((context, query), axis=2)
        proj = jnp.einsum('bqk,hk->bqh', combined, W) + b
        mean = jnp.mean(proj, axis=-1, keepdims=True)
        var = jnp.mean(jnp.square(proj - mean), axis=-1, keepdims=True)
        out = (proj - mean) * jax.lax.rsqrt(var + LN_EPS) * gamma + beta
        return out

    def _L3_attn_ref(query, key, value, in_proj_weight, out_proj_weight):
        import jax, jax.numpy as jnp
        import numpy as np
        EMBED_DIM = 256
        NUM_HEADS = 16
        HEAD_DIM = EMBED_DIM // NUM_HEADS
        BATCH = 2
        SEQ = 512
        NEG_INF = float('-inf')
        B, T, E = query.shape
        H, D = (NUM_HEADS, HEAD_DIM)
        projected = jnp.einsum('bte,fe->btf', query, in_proj_weight)
        packed = projected.reshape(B, T, 3, H, D).transpose(0, 3, 2, 1, 4)
        q, k, v = (packed[:, :, 0], packed[:, :, 1], packed[:, :, 2])
        q = q / jnp.sqrt(jnp.asarray(D, dtype=q.dtype))
        attention = jnp.einsum('bhtd,bhkd->bhtk', q, k)
        qpos = jnp.arange(T)[:, None]
        kpos = jnp.arange(T)[None, :]
        mask = jnp.where(qpos - kpos >= 0, 0.0, NEG_INF).astype(attention.dtype)
        attention = attention + mask[None, None]
        activation = jax.nn.softmax(attention, axis=-1)
        x = jnp.einsum('bhtk,bhkd->bhtd', activation, v)
        x = x.transpose(0, 2, 1, 3).reshape(B, T, E)
        out = jnp.einsum('bte,fe->btf', x, out_proj_weight)
        return out

    def _L3_ffn_ref(x, w1, b1, w2, b2):
        import jax, jax.numpy as jnp
        import numpy as np
        EPS = 1e-08

        def _ste(x, q):
            return x + jax.lax.stop_gradient(q - x)

        def quant_act_uint8(x):
            s = jax.lax.stop_gradient(jnp.maximum(jnp.max(x), EPS)) / 255.0
            q = jnp.clip(jnp.round(x / s), 0.0, 255.0) * s
            return (_ste(x, q), s)

        def quant_weight_int8_perchannel(w):
            s = jax.lax.stop_gradient(jnp.maximum(jnp.max(jnp.abs(w), axis=1, keepdims=True), EPS)) / 127.0
            q = jnp.clip(jnp.round(w / s), -128.0, 127.0) * s
            return (_ste(w, q), s[:, 0])

        def quant_bias_int32(b, s_in, s_w):
            s = jax.lax.stop_gradient(s_in * s_w)
            q = jnp.round(b / s) * s
            return _ste(b, q)

        def quant_linear(x, w, b):
            xq, s_in = quant_act_uint8(x)
            wq, s_w = quant_weight_int8_perchannel(w)
            bq = quant_bias_int32(b, s_in, s_w)
            return jnp.einsum('btd,fd->btf', xq, wq) + bq
        h = jax.nn.relu(quant_linear(x, w1, b1))
        return quant_linear(h, w2, b2)
    x = x + _L0_xattn_ref(_layernorm(x, axis=-1), ctx_1024, mask_BxSxS2_bf0, L0_xattn_Wq, L0_xattn_bq, L0_xattn_Wk, L0_xattn_bk, L0_xattn_Wv, L0_xattn_bv, L0_xattn_Wo, L0_xattn_bo)
    x = x + _L0_attn_ref(_layernorm(x, axis=-1), L0_attn_qw, L0_attn_kw, L0_attn_vw, L0_attn_ow)
    x = x + _L0_ffn_ref(_layernorm(x, axis=-1), L0_ffn_router_w, L0_ffn_router_b, L0_ffn_w1, L0_ffn_b1, L0_ffn_w2, L0_ffn_b2, L0_ffn_sw1, L0_ffn_sb1, L0_ffn_sw2, L0_ffn_sb2)
    x = x + _L1_xattn_ref(_layernorm(x, axis=-1), ctx_1024, ctx_1024, mask_BxSxS2_bk1, L1_xattn_Wq, L1_xattn_Wk, L1_xattn_Wv, L1_xattn_Wo, L1_xattn_bo)
    x = x + _L1_attn_ref(_layernorm(x, axis=-1), L1_attn_Wq, L1_attn_bq, L1_attn_Wk, L1_attn_bk, L1_attn_Wv, L1_attn_bv, L1_attn_Wo, L1_attn_bo)
    x = x + _L1_ffn_ref(_layernorm(x, axis=-1), L1_ffn_router_w, L1_ffn_experts_bias, L1_ffn_w1, L1_ffn_w3, L1_ffn_w2, L1_ffn_sw1, L1_ffn_sw3, L1_ffn_sw2)
    x = x + _L2_xattn_ref(_layernorm(x, axis=-1), ctx_1024, ctx_1024, L2_xattn_Wq, L2_xattn_Wk, L2_xattn_Wv, L2_xattn_Wo, mask_BxS2_ik1)
    x = x + _L2_attn_ref(_layernorm(x, axis=-1), L2_attn_W_in, L2_attn_b_in, L2_attn_W_gate, L2_attn_b_gate, L2_attn_conv_w, L2_attn_conv_b, L2_attn_A_log, L2_attn_D_skip, L2_attn_W_delta, L2_attn_b_delta, L2_attn_W_B, L2_attn_W_C, L2_attn_W_out, L2_attn_b_out)
    x = x + _L2_ffn_ref(_layernorm(x, axis=-1), L2_ffn_k0, L2_ffn_k1, L2_ffn_k2, L2_ffn_s0, L2_ffn_s1, L2_ffn_s2)
    x = x + _L3_xattn_ref(_layernorm(x, axis=-1), ctx_1024, L3_xattn_W, L3_xattn_b, L3_xattn_gamma, L3_xattn_beta)
    x = x + _L3_attn_ref(_layernorm(x, axis=-1), L3_attn_key, L3_attn_value, L3_attn_in_proj_weight, L3_attn_out_proj_weight)
    x = x + _L3_ffn_ref(_layernorm(x, axis=-1), L3_ffn_w1, L3_ffn_b1, L3_ffn_w2, L3_ffn_b2)
    return x

_drawn_inputs = setup_inputs


def setup_inputs(seed=0):
    import zlib

    import numpy as np

    out = dict(_drawn_inputs(seed))
    spreads = {'L0_xattn_bq': (0.0, 0.1),
     'L0_xattn_bk': (0.0, 2.0),
     'L0_xattn_bv': (0.0, 0.1),
     'L0_xattn_bo': (0.0, 0.1),
     'L0_ffn_router_b': (0.0, 0.1),
     'L0_ffn_b1': (0.0, 0.289),
     'L0_ffn_b2': (0.0, 0.1),
     'L0_ffn_sb1': (0.0, 0.293),
     'L0_ffn_sb2': (0.0, 0.1),
     'L1_xattn_bo': (0.0, 0.1),
     'L1_ffn_experts_bias': (0.0, 0.497),
     'L2_attn_b_in': (0.0, 0.1),
     'L2_attn_b_gate': (0.0, 0.1),
     'L2_attn_conv_b': (0.0, 0.1),
     'L2_attn_D_skip': (1.0, 0.2),
     'L2_attn_b_delta': (0.0, 0.325),
     'L2_attn_b_out': (0.0, 0.1),
     'L3_xattn_gamma': (1.0, 0.2),
     'L3_xattn_beta': (0.0, 0.1)}
    factors = {'L0_attn_qw': 8.0,
     'L0_attn_kw': 8.0,
     'L1_xattn_Wq': 8.0,
     'L1_xattn_Wk': 8.0,
     'L1_ffn_router_w': 3.183,
     'L1_ffn_w2': 2.682,
     'L3_xattn_b': 3.712,
     'L3_ffn_b1': 22.083,
     'L3_ffn_b2': 8.0}
    for name, (base, spread) in spreads.items():
        noise = np.random.default_rng([zlib.crc32(name.encode()), seed]).standard_normal(out[name].shape)
        drawn = base * np.exp(spread * noise) if base else spread * noise
        out[name] = jnp.asarray(drawn.astype(out[name].dtype))
    for name, factor in factors.items():
        out[name] = (out[name] * factor).astype(out[name].dtype)
    return out
```

```python
import concourse.bass as bass
import numpy as np
from concourse import mybir
from contextlib import ExitStack, contextmanager

LAYERS = (0, 1, 2, 3, 4, 5, 6, 7, 8, 9, 10, 11)

F32 = mybir.dt.float32
BF16 = mybir.dt.bfloat16
F16 = mybir.dt.float16
U8 = mybir.dt.uint8
I32 = mybir.dt.int32
ALU = mybir.AluOpType
ACT = mybir.ActivationFunctionType
AX = mybir.AxisListType

B, S, D = 2, 256, 256
SK = 4096
P = 128
NT = B * S // P
QT = S // P
DC = D // P
MASKED = -1e30
EPS = 1e-5


class Stage:

    number = 0

    def __init__(self, nc):
        self.nc, self.stack, self.sems = nc, ExitStack(), []

    def own(self, name):
        Stage.number += 1
        return f"{name}_{Stage.number}"

    def __enter__(self):
        self.stack.__enter__()
        return self

    def sb(self, name, shape, dt=F32):
        return self.stack.enter_context(self.nc.sbuf_tensor(self.own(name), shape, dt))

    def ps(self, name, shape, dt=F32):
        return self.stack.enter_context(self.nc.psum_tensor(self.own(name), shape, dt))

    def sem(self, name):
        s = self.nc.alloc_semaphore(self.own(name))
        self.sems.append(s)
        return s

    def __exit__(self, *a):
        r = self.stack.__exit__(*a)
        if a[0] is None:
            self.nc.clear_and_free_semaphores(self.sems)
            self.nc.all_engine_barrier()
        return r


def setup_stage(nc, R, x):
    with Stage(nc) as st:
        loaded, zeroed, made = st.sem("x_loaded"), st.sem("ident_zeroed"), st.sem("ident_made")
        with nc.Block() as block:

            @block.sync
            def _(sp):
                sp.dma_start(R.x[:, :, :], x).then_inc(loaded, 16)
                sp.wait_ge(loaded, 16)

            @block.gpsimd
            def _(pool):
                pool.memset(R.identf[:, :], 0.0).then_inc(zeroed, 1)
                pool.memset(R.onesf[:, :], 1.0).then_inc(zeroed, 1)
                pool.wait_ge(zeroed, 2)
                pool.affine_select(out=R.identf[:, :], in_=R.identf[:, :], compare_op=ALU.not_equal, fill=1.0,
                                   base=0, pattern=[[-1, P]], channel_multiplier=1).then_inc(made, 1)

            @block.vector
            def _(dve):
                dve.wait_ge(made, 1)
                dve.tensor_copy(R.identb[:, :], R.identf[:, :]).then_inc(made, 1)


def norm_stage(nc, R):
    with Stage(nc) as st:
        stats = st.sb("stats", [P, NT, 6])
        mv = st.sb("mean_var", [P, NT, 2])
        rstd = st.sb("rstd", [P, NT])
        tp = st.ps("tp", [P, DC, NT * P])
        done = st.sem("dve_step")
        rooted, normed, turned = st.sem("rooted"), st.sem("normed"), st.sem("turned")
        with nc.Block() as block:

            @block.vector
            def _(dve):
                for t in range(NT):
                    dve.bn_stats(stats[:, t, :], R.x[:, t, :]).then_inc(done, 1)
                for t in range(NT):
                    dve.wait_ge(done, t + 1)
                    dve.bn_aggr(mv[:, t, :], stats[:, t, :]).then_inc(done, 1)
                dve.wait_ge(done, 2 * NT)
                dve.tensor_scalar(rstd[:, :], mv[:, :, 1], EPS, None, ALU.add).then_inc(done, 1)
                dve.wait_ge(rooted, 1)
                dve.reciprocal(rstd[:, :], rstd[:, :]).then_inc(done, 1)
                dve.wait_ge(done, 2 * NT + 2)
                for t in range(NT):
                    dve.tensor_scalar(R.xn[:, t, :], R.x[:, t, :], mv[:, t, 0:1], rstd[:, t:t + 1],
                                      ALU.subtract, ALU.mult).then_inc(normed, 1)
                dve.wait_ge(turned, DC * NT)
                dve.tensor_copy(R.xnT[:, 0, :], tp[:, 0, :])

            @block.scalar
            def _(act):
                act.wait_ge(done, 2 * NT + 1)
                act.activation(rstd[:, :], rstd[:, :], ACT.Sqrt).then_inc(rooted, 1)
                act.wait_ge(turned, DC * NT)
                act.activation(R.xnT[:, 1, :], tp[:, 1, :], ACT.Copy)

            @block.tensor
            def _(pe):
                for t in range(NT):
                    pe.wait_ge(normed, t + 1)
                    for c in range(DC):
                        pe.transpose(tp[:, c, t * P:(t + 1) * P], R.xn[:, t, c * P:(c + 1) * P],
                                     R.identf[:, :]).then_inc(turned, 1)


def add_projected_stage(nc, R, src, width, w, brow):
    C = width // P
    with Stage(nc) as st:
        srcT = st.sb("srcT", [P, C, NT * P])
        wt = st.sb("w_out", [P, C, D], w.dtype)
        wf = st.sb("w_out_f", [P, C, D]) if w.dtype != F32 else wt
        bt = st.sb("b_out", [P, D])
        tp = [st.ps("tp", [P, NT * P]) for _ in range(2)]
        acc = [st.ps("acc", [P, D]) for _ in range(2)]
        loaded, widened, turned, kept = st.sem("w_loaded"), st.sem("w_widened"), st.sem("turned"), st.sem("srcT_kept")
        made, added, added_bias = st.sem("product_made"), st.sem("product_added"), st.sem("bias_added")
        n_loads = 2 if brow is not None else 1
        with nc.Block() as block:

            @block.sync
            def _(sp):
                sp.dma_start(wt[:, :, :], w).then_inc(loaded, 16)
                if brow is not None:
                    sp.dma_start(bt[:, :], brow).then_inc(loaded, 16)

            @block.tensor
            def _(pe):
                for c in range(C):
                    if c >= 2:
                        pe.wait_ge(kept, c - 1)
                    for t in range(NT):
                        last = pe.transpose(tp[c % 2][:, t * P:(t + 1) * P], src[:, t, c * P:(c + 1) * P],
                                            R.identf[:, :])
                    last.then_inc(turned, 1)
                pe.wait_ge(kept, C)
                pe.wait_ge(widened, 1)
                for t in range(NT):
                    if t >= 2:
                        pe.wait_ge(added, t - 1)
                    for c in range(C):
                        last = pe.matmul(acc[t % 2][:, :], srcT[:, c, t * P:(t + 1) * P], wf[:, c, :],
                                         start=(c == 0), stop=(c == C - 1))
                    last.then_inc(made, 1)

            @block.scalar
            def _(act):
                for c in range(C):
                    act.wait_ge(turned, c + 1)
                    act.activation(srcT[:, c, :], tp[c % 2][:, :], ACT.Copy).then_inc(kept, 1)

            @block.vector
            def _(dve):
                dve.wait_ge(loaded, 16 * n_loads)
                if w.dtype != F32:
                    dve.tensor_copy(wf[:, :, :], wt[:, :, :]).then_inc(widened, 1)
                else:
                    dve.engine_nop().then_inc(widened, 1)
                if brow is not None:
                    for t in range(NT):
                        dve.tensor_tensor(R.x[:, t, :], R.x[:, t, :], bt[:, :], ALU.add).then_inc(added_bias, 1)
                for t in range(NT):
                    if brow is not None:
                        dve.wait_ge(added_bias, t + 1)
                    dve.wait_ge(made, t + 1)
                    dve.tensor_tensor(R.x[:, t, :], R.x[:, t, :], acc[t % 2][:, :], ALU.add).then_inc(added, 1)


def pack_offsets(hg, d, rope):
    vw = hg * (d + 1)
    names = [("wk", DC * P), ("wq", DC * P), ("wv", DC * vw)]
    if rope:
        names += [("wks", DC * P), ("wqs", DC * P)]
    names += [("kb", 1), ("qb", P), ("vb", vw)]
    at, out = 0, {}
    for n, w in names:
        out[n] = (at, at + w)
        at += w
    return out, at


def attention_stage(nc, R, out_tok, pack, nk, hg, d, scale, ctxT=None, masks=None, key_mask=None, rope=None):
    G = 16 // hg
    VW = hg * (d + 1)
    KR = d + (2 if key_mask is not None else 1)
    HS = P // hg
    KW = min(512, nk)
    KC = nk // KW
    NKT = nk // P
    VP = 4 if nk > 512 else NKT
    VG = NKT // VP
    RW = QT * S if nk == S else 1024
    EK = 4 if nk > 512 else NKT
    EC = NKT // EK
    EU = hg * EC
    SCW = EK * S
    OFF, WF = pack_offsets(hg, d, rope is not None)
    if nk == S:
        units = [(j, [(q, 0, nk, q * nk) for q in range(QT)], 0) for j in range(hg)]
        parts = 1
    else:
        parts = nk // 1024
        units = [(j, [(q, k * 1024 + h * 512, 512, h * 512) for h in range(2)], k)
                 for j in range(hg) for q in range(QT) for k in range(parts)]
    MU = len(units)
    U = KC + VG + 3
    VQ = VG + 3

    with Stage(nc) as st:
        KT = st.sb("KT", [P, nk])
        V = st.sb("V", [P, NKT, VW])
        wt = st.sb("w_pack", [P, WF])
        narrow = pack.dtype != F32
        wl = st.sb("w_pack_half", [P, WF], pack.dtype) if narrow else wt
        qsrc = st.sb("qsrc", [P, DC, S])
        kvsrc = st.sb("ctxT", [P, DC, nk]) if ctxT is not None else qsrc
        qtok = st.sb("q_tok", [P, QT, P])
        QTt = st.sb("QT", [P, S])
        mx = st.sb("max_parts", [P, QT, hg, parts])
        rsum = st.sb("sum_recip", [P, QT, hg])
        PT = [st.sb("probsT", [P, SCW]) for _ in range(3)]
        big = st.ps("scores", [P, 2, 1024])
        pj = st.ps("proj", [P, 2, 512])
        pv = st.ps("weighted", [P, QT, 512])
        if masks is not None:
            m8 = [st.sb("mask_words", [P, QT * nk // 4], I32) for _ in range(2)]
            mq, mk = [st.sb("mask_add", [P, QT * nk], BF16) for _ in range(2)]
        if key_mask is not None:
            km = st.sb("key_mask", [1, nk], I32)
            kadd = st.sb("key_add", [1, nk])
            sel = st.sb("mask_row_sel", [1, P])
        if rope is not None:
            rk = st.sb("rope_k", [P, 2, S])
            rq = st.sb("rope_q", [P, 2, QT, P])
            ra = st.sb("rope_a", [P, S])
            rb = st.sb("rope_b", [P, S])

        def W(n, c=None, w=None):
            a, z = OFF[n]
            return wt[:, a:z] if c is None else wt[:, a + c * w:a + (c + 1) * w]

        w_loaded, b_loaded, const_loaded = st.sem("w_loaded"), st.sem("batch_loaded"), st.sem("const_loaded")
        src_ready, step, widened = st.sem("src_ready"), st.sem("dve_step"), st.sem("w_widened")
        proj_made, k_kept, vq_kept = st.sem("proj_made"), st.sem("keys_kept"), st.sem("vq_kept")
        s_made, s_read, maxed = st.sem("scores_made"), st.sem("scores_read"), st.sem("maxed")
        st_made, exp_done, pv_done = st.sem("scoresT_made"), st.sem("exp_done"), st.sem("weighted_done")
        normed = st.sem("normalised")
        n_b = (1 if ctxT is not None else 0) + (2 if masks is not None else 0) + (1 if key_mask is not None else 0)
        n_const = (1 if key_mask is not None else 0) + (2 if rope is not None else 0)
        SRC = 1 + (2 if masks is not None else 0) + (1 if key_mask is not None else 0)
        STEPS = 1 + (3 if rope is not None else 0)
        if rope is not None:
            STEPS = 5

        with nc.Block() as block:

            @block.gpsimd
            def _(pool):
                if key_mask is not None:
                    pool.dma_start(sel[:, :], key_mask[1]).then_inc(const_loaded, 16)
                if rope is not None:
                    pool.dma_start(rk[:, :, :], rope[0]).then_inc(const_loaded, 16)
                    pool.dma_start(rq[:, :, :, :], rope[1]).then_inc(const_loaded, 16)
                with pool.Fori(0, B) as b:
                    if n_b:
                        pool.wait_ge(pv_done, b * (G * EU) + 1)
                        pool.wait_ge(src_ready, b * SRC + 1)
                    if ctxT is not None:
                        pool.dma_start(kvsrc[:, :, :], ctxT[bass.ds(b, 1)].rearrange("o p c k -> (o p) c k"))\
                          .then_inc(b_loaded, 16)
                    if masks is not None:
                        for n in range(2):
                            pool.dma_start(m8[n][:, :], masks[n][bass.ds(b, 1)].rearrange("o p k -> (o p) k"))\
                              .then_inc(b_loaded, 16)
                    if key_mask is not None:
                        pool.dma_start(km[:, :], key_mask[0][bass.ds(b, 1), :]).then_inc(b_loaded, 16)
                    with pool.Fori(0, G) as g:
                        pool.wait_ge(maxed, b * G + g + 1)
                        pool.dma_start(wl[:, :], pack[bass.ds(g, 1)].rearrange("o p w -> (o p) w"))\
                          .then_inc(w_loaded, 16)

            @block.tensor
            def _(pe):
                pe.sem_inc(pv_done, 1)
                if n_const:
                    pe.wait_ge(const_loaded, 16 * n_const)
                with pe.Fori(0, B) as b:
                    with pe.Fori(0, G) as g:
                        it = b * G + g
                        if n_b:
                            pe.wait_ge(b_loaded, b * (16 * n_b) + 16 * n_b)
                        pe.wait_ge(src_ready, b * SRC + SRC + 1)
                        if narrow:
                            pe.wait_ge(widened, it + 1)
                        else:
                            pe.wait_ge(w_loaded, it * 16 + 16)

                        def buffer_free(n):
                            if n < 2:
                                return
                            if n - 2 < KC:
                                pe.wait_ge(k_kept, it * KC + (n - 1))
                            else:
                                pe.wait_ge(vq_kept, it * VQ + (n - 1 - KC))

                        for n in range(KC):
                            buffer_free(n)
                            o = pj[:, n % 2, 0:KW]
                            for c in range(DC):
                                last = pe.matmul(o, W("wk", c, P), kvsrc[:, c, n * KW:(n + 1) * KW],
                                                 start=(c == 0), stop=(c == DC - 1 and key_mask is None))
                            if key_mask is not None:
                                last = pe.matmul(o, sel[:, :], kadd[:, n * KW:(n + 1) * KW], start=False, stop=True)
                            if rope is not None:
                                for c in range(DC):
                                    last = pe.matmul(pj[:, n % 2, S:2 * S], W("wks", c, P), kvsrc[:, c, :],
                                                     start=(c == 0), stop=(c == DC - 1))
                            last.then_inc(proj_made, 1)
                        for v in range(VG):
                            n = KC + v
                            buffer_free(n)
                            for i in range(VP):
                                k0 = (v * VP + i) * P
                                for c in range(DC):
                                    last = pe.matmul(pj[:, n % 2, i * VW:(i + 1) * VW], kvsrc[:, c, k0:k0 + P],
                                                     W("wv", c, VW), start=(c == 0), stop=(c == DC - 1))
                            last.then_inc(proj_made, 1)
                        n = KC + VG
                        buffer_free(n)
                        for q in range(QT):
                            for r, name in enumerate(["wq"] + ["wqs"] * (rope is not None)):
                                o = r * S + q * P
                                for c in range(DC):
                                    last = pe.matmul(pj[:, n % 2, o:o + P], qsrc[:, c, q * P:(q + 1) * P],
                                                     W(name, c, P), start=(c == 0), stop=(c == DC - 1))
                        last.then_inc(proj_made, 1)

                        def turn_queries(n):
                            pe.wait_ge(vq_kept, it * VQ + VG + (n - KC - VG))
                            for q in range(QT):
                                last = pe.transpose(pj[:, n % 2, q * P:(q + 1) * P], qtok[:, q, :], R.identf[:, :])
                            last.then_inc(proj_made, 1)

                        turn_queries(KC + VG + 1)
                        pe.wait_ge(k_kept, it * KC + KC)
                        pe.wait_ge(vq_kept, it * VQ + VG + 2)
                        pe.wait_ge(exp_done, it * EU + 1)
                        for u, (j, cells, _) in enumerate(units):
                            if u >= 2:
                                pe.wait_ge(s_read, it * MU + (u - 1))
                            for q, k0, w, o in cells:
                                out = big[:, u % 2, o:o + w]
                                if masks is not None:
                                    pe.matmul(out, R.identb[:, :], mq[:, q * nk + k0:q * nk + k0 + w],
                                              start=True, stop=False)
                                last = pe.matmul(out, QTt[j * HS:j * HS + KR, q * P:(q + 1) * P],
                                                 KT[j * HS:j * HS + KR, k0:k0 + w],
                                                 start=(masks is None), stop=True)
                            last.then_inc(s_made, 1)
                        pe.wait_ge(maxed, it + 1 + 1)
                        turn_queries(KC + VG + 2)
                        pe.wait_ge(vq_kept, it * VQ + VQ)

                        def weigh(e):
                            j, e0 = e // EC, e % EC
                            pe.wait_ge(exp_done, it * EU + (e + 1) + 1)
                            if e == 0:
                                pe.wait_ge(normed, it + 1)
                            for i in range(EK):
                                kt = e0 * EK + i
                                for q in range(QT):
                                    last = pe.matmul(pv[:, q, j * (d + 1):(j + 1) * (d + 1)],
                                                     PT[e % 3][:, i * S + q * P:i * S + (q + 1) * P],
                                                     V[:, kt, j * (d + 1):(j + 1) * (d + 1)],
                                                     start=(kt == 0), stop=(kt == NKT - 1))
                            last.then_inc(pv_done, 1)

                        for e in range(EU):
                            j, e0 = e // EC, e % EC
                            if e >= 2:
                                pe.wait_ge(exp_done, it * EU + (e - 1) + 1)
                            for h in range(EK // 2):
                                bank = big[:, e % 2, h * 512:(h + 1) * 512]
                                if masks is not None:
                                    k0 = (e0 * EK + 2 * h) * S
                                    pe.matmul(bank, R.identb[:, :], mk[:, k0:k0 + 512], start=True, stop=False)
                                for i in range(2):
                                    kt = e0 * EK + 2 * h + i
                                    last = pe.matmul(bank[:, i * S:(i + 1) * S],
                                                     KT[j * HS:j * HS + KR, kt * P:(kt + 1) * P],
                                                     QTt[j * HS:j * HS + KR, :],
                                                     start=(masks is None), stop=(masks is None or i == 1))
                            last.then_inc(st_made, 1)
                            if e >= 1:
                                weigh(e - 1)
                        weigh(EU - 1)

            @block.scalar
            def _(act):
                act.sem_inc(exp_done, 1)
                with act.Fori(0, B) as b:
                    with act.Fori(0, G) as g:
                        it = b * G + g
                        if rope is None:
                            for n in range(KC):
                                act.wait_ge(proj_made, it * U + (n + 1))
                                act.activation(KT[:, n * KW:(n + 1) * KW], pj[:, n % 2, 0:KW], ACT.Identity,
                                               bias=W("kb")).then_inc(k_kept, 1)
                        for e in range(EU):
                            act.wait_ge(st_made, it * EU + (e + 1))
                            if e < 3:
                                act.wait_ge(pv_done, it * EU + 1)
                            else:
                                act.wait_ge(pv_done, it * EU + (e - 2) + 1)
                            act.activation(PT[e % 3][:, :], big[:, e % 2, 0:SCW], ACT.Exp, scale=scale)\
                               .then_inc(exp_done, 1)

            @block.vector
            def _(dve):
                dve.sem_inc(src_ready, 1)
                dve.sem_inc(step, 1)
                dve.sem_inc(maxed, 1)
                dve.sem_inc(normed, 1)
                if n_const:
                    dve.wait_ge(const_loaded, 16 * n_const)
                with dve.Fori(0, B) as b:
                    dve.wait_ge(pv_done, b * (G * EU) + 1)
                    dve.tensor_copy(qsrc[:, :, :], R.xnT[:, :, bass.ds(b * S, S)]).then_inc(src_ready, 1)
                    if n_b:
                        dve.wait_ge(b_loaded, b * (16 * n_b) + 16 * n_b)
                    if masks is not None:
                        for src8, add in zip(m8, (mq, mk)):
                            dve.tensor_scalar(add[:, :], src8[:, :].bitcast(U8), MASKED, None, ALU.mult).then_inc(src_ready, 1)
                    if key_mask is not None:
                        dve.tensor_scalar(kadd[:, :], km[:, :], 0.0, MASKED, ALU.is_equal, ALU.mult)\
                           .then_inc(src_ready, 1)
                    with dve.Fori(0, G) as g:
                        it = b * G + g
                        if narrow:
                            dve.wait_ge(w_loaded, it * 16 + 16)
                            dve.tensor_copy(wt[:, :], wl[:, :]).then_inc(widened, 1)
                            dve.wait_ge(widened, it + 1)
                        if rope is not None:
                            dve.wait_ge(proj_made, it * U + 1)
                            dve.wait_ge(step, it * STEPS + 1)
                            dve.tensor_tensor(ra[:, :], pj[:, 0, 0:S], rk[:, 0, :], ALU.mult).then_inc(step, 1)
                            dve.tensor_tensor(rb[:, :], pj[:, 0, S:2 * S], rk[:, 1, :], ALU.mult).then_inc(step, 1)
                            dve.wait_ge(step, it * STEPS + 2 + 1)
                            dve.scalar_tensor_tensor(out=KT[:, :], in0=ra[:, :], scalar=W("kb"), in1=rb[:, :],
                                                     op0=ALU.add, op1=ALU.add).then_inc(k_kept, 1)
                        for v in range(VG):
                            n = KC + v
                            dve.wait_ge(proj_made, it * U + (n + 1))
                            dve.tensor_tensor(V[:, v * VP:(v + 1) * VP, :],
                                              pj[:, n % 2, 0:VP * VW].rearrange("p (k w) -> p k w", k=VP),
                                              W("vb").unsqueeze(1).broadcast_to([P, VP, VW]), ALU.add)\
                               .then_inc(vq_kept, 1)
                        n = KC + VG
                        dve.wait_ge(proj_made, it * U + (n + 1))
                        if rope is None:
                            dve.tensor_tensor(qtok[:, :, :],
                                              pj[:, n % 2, 0:S].rearrange("p (q w) -> p q w", q=QT),
                                              W("qb").unsqueeze(1).broadcast_to([P, QT, P]), ALU.add)\
                               .then_inc(vq_kept, 1)
                        else:
                            dve.wait_ge(k_kept, it + 1)
                            dve.tensor_tensor(ra[:, :], pj[:, n % 2, 0:S],
                                              rq[:, 0, :, :].rearrange("p q w -> p (q w)"), ALU.mult).then_inc(step, 1)
                            dve.tensor_tensor(rb[:, :], pj[:, n % 2, S:2 * S],
                                              rq[:, 1, :, :].rearrange("p q w -> p (q w)"), ALU.mult).then_inc(step, 1)
                            dve.wait_ge(step, it * STEPS + 4 + 1)
                            dve.tensor_tensor(qtok[:, :, :].rearrange("p q w -> p (q w)"), ra[:, :], rb[:, :],
                                              ALU.add).then_inc(vq_kept, 1)
                        n += 1
                        dve.wait_ge(proj_made, it * U + (n + 1))
                        dve.tensor_copy(QTt[:, :], pj[:, n % 2, 0:S]).then_inc(vq_kept, 1)
                        for u, (j, cells, part) in enumerate(units):
                            dve.wait_ge(s_made, it * MU + (u + 1))
                            if nk == S:
                                dve.tensor_reduce(mx[:, :, j, 0], big[:, u % 2, 0:RW].rearrange(
                                    "p (q k) -> p q k", q=QT), AX.X, ALU.max).then_inc(s_read, 1)
                            else:
                                dve.tensor_reduce(mx[:, cells[0][0], j, part:part + 1], big[:, u % 2, 0:RW],
                                                  AX.X, ALU.max).then_inc(s_read, 1)
                        dve.wait_ge(s_read, it * MU + MU)
                        dve.tensor_reduce(qtok[:, :, :].rearrange("p q (j s) -> p q j s", j=hg)[:, :, :, d],
                                          mx[:, :, :, :], AX.X, ALU.max, negate=True).then_inc(maxed, 1)
                        n += 1
                        dve.wait_ge(proj_made, it * U + (n + 1))
                        dve.tensor_copy(QTt[:, :], pj[:, n % 2, 0:S]).then_inc(vq_kept, 1)
                        dve.wait_ge(pv_done, it * EU + EU + 1)
                        pvv = pv[:, :, 0:VW].rearrange("p q (j w) -> p q j w", j=hg)
                        dve.wait_ge(normed, it + 1)
                        dve.reciprocal(rsum[:, :, :], pvv[:, :, :, d]).then_inc(step, 1)
                        dve.wait_ge(step, it * STEPS + STEPS + 1)
                        for q in range(QT):
                            o = out_tok[:, bass.ds(b * QT + q, 1), bass.ds(g * (hg * d), hg * d)]
                            ins = dve.tensor_tensor(o.rearrange("p o (j w) -> p (o j) w", j=hg),
                                                    pvv[:, q, :, 0:d],
                                                    rsum[:, q, :].unsqueeze(2).broadcast_to([P, hg, d]), ALU.mult)
                        ins.then_inc(normed, 1)


def head_mix_stage(nc, R, dram, scratch):
    H, d = 16, 16
    with Stage(nc) as st:
        w = st.sb("w_qkv", [P, DC, 3 * D])
        bias = st.sb("b_qkv", [P, 3 * D])
        qkv = [st.sb("qkv", [P, 3 * D]) for _ in range(2)]
        prod = st.sb("products", [P, H, H, d])
        sc = st.sb("scores", [P, H, H])
        ex = st.sb("exps", [P, H, H])
        mx, sm = st.sb("max", [P, H]), st.sb("sum", [P, H])
        o = [st.sb("mixed", [P, H, d]) for _ in range(2)]
        ps = [st.ps("qkv_ps", [P, 2, 512]) for _ in range(2)]
        loaded, made, kept, step = st.sem("w_loaded"), st.sem("qkv_made"), st.sem("qkv_kept"), st.sem("dve_step")
        shifted, exped, mixed = st.sem("shifted"), st.sem("exp_done"), st.sem("mixed")
        stored = [st.sem("stored") for _ in range(2)]
        with nc.Block() as block:

            @block.sync
            def _(sp):
                sp.dma_start(w[:, :, :], dram["w4"]).then_inc(loaded, 16)
                sp.dma_start(bias[:, :], dram["b4"]).then_inc(loaded, 16)
                for t in range(NT):
                    b, q = t // QT, t % QT
                    sp.wait_ge(mixed, t + 1)
                    sp.dma_start(scratch[b, :, q * P:(q + 1) * P, :].rearrange("h s d -> s h d"),
                                 o[t % 2][:, :, :]).then_inc(stored[t % 2], 16)
                for s in stored:
                    sp.wait_ge(s, 16 * NT // 2)

            @block.tensor
            def _(pe):
                pe.wait_ge(loaded, 32)
                for t in range(NT):
                    if t >= 2:
                        pe.wait_ge(kept, t - 1)
                    for h, (c0, c1) in enumerate(((0, 512), (512, 768))):
                        for c in range(DC):
                            last = pe.matmul(ps[t % 2][:, h, 0:c1 - c0], R.xnT[:, c, t * P:(t + 1) * P],
                                             w[:, c, c0:c1], start=(c == 0), stop=(c == DC - 1))
                    last.then_inc(made, 1)

            @block.scalar
            def _(act):
                for t in range(NT):
                    act.wait_ge(shifted, t + 1)
                    act.activation(ex[:, :, :], sc[:, :, :], ACT.Exp, scale=0.25).then_inc(exped, 1)

            @block.vector
            def _(dve):
                dve.wait_ge(loaded, 32)
                n = 0
                for t in range(NT):
                    a = qkv[t % 2]
                    dve.wait_ge(made, t + 1)
                    flat = ps[t % 2][:, :, :].rearrange("p a b -> p (a b)")[:, 0:3 * D]
                    dve.tensor_tensor(a[:, :], flat, bias[:, :], ALU.add).then_inc(kept, 1)
                    q, k, v = (a[:, i * D:(i + 1) * D].rearrange("p (h d) -> p h d", h=H) for i in range(3))
                    dve.wait_ge(kept, t + 1)
                    dve.tensor_tensor(prod[:, :, :, :], q.unsqueeze(2).broadcast_to([P, H, H, d]),
                                      k.unsqueeze(1).broadcast_to([P, H, H, d]), ALU.mult).then_inc(step, 1)
                    dve.wait_ge(step, n + 1)
                    dve.tensor_reduce(sc[:, :, :], prod[:, :, :, :], AX.X, ALU.add).then_inc(step, 1)
                    dve.wait_ge(step, n + 2)
                    dve.tensor_reduce(mx[:, :], sc[:, :, :], AX.X, ALU.max).then_inc(step, 1)
                    dve.wait_ge(step, n + 3)
                    dve.tensor_tensor(sc[:, :, :], sc[:, :, :], mx[:, :].unsqueeze(2).broadcast_to([P, H, H]),
                                      ALU.subtract).then_inc(shifted, 1)
                    dve.wait_ge(exped, t + 1)
                    dve.tensor_reduce(sm[:, :], ex[:, :, :], AX.X, ALU.add).then_inc(step, 1)
                    dve.tensor_tensor(prod[:, :, :, :], ex[:, :, :].unsqueeze(2).broadcast_to([P, H, d, H]),
                                      v.rearrange("p h d -> p d h").unsqueeze(1).broadcast_to([P, H, d, H]),
                                      ALU.mult).then_inc(step, 1)
                    dve.wait_ge(step, n + 5)
                    dve.reciprocal(sm[:, :], sm[:, :]).then_inc(step, 1)
                    if t >= 2:
                        dve.wait_ge(stored[t % 2], 16 * (t // 2))
                    dve.tensor_reduce(o[t % 2][:, :, :], prod[:, :, :, :], AX.X, ALU.add).then_inc(step, 1)
                    n += 7
                    dve.wait_ge(step, n)
                    dve.tensor_tensor(o[t % 2][:, :, :], o[t % 2][:, :, :],
                                      sm[:, :].unsqueeze(2).broadcast_to([P, H, d]), ALU.mult).then_inc(mixed, 1)


def reload_stage(nc, att, scratch):
    with Stage(nc) as st:
        loaded = st.sem("reloaded")
        with nc.Block() as block:

            @block.sync
            def _(sp):
                flat = scratch.rearrange("b h s d -> (b h s d)").rearrange("(t p m) -> p t m", p=P, m=D)
                sp.dma_start(att[:, :, :], flat).then_inc(loaded, 16)
                sp.wait_ge(loaded, 16)


def experts_stage(nc, R, dram, layer, E, func, shared_weight):
    NE, HT = 8, 4
    gated = layer == 5
    rw_d, rb_d = dram[f"rw{layer}"], dram[f"rb{layer}"]
    w1_d, w2_d = dram[f"e1_{layer}"], dram[f"e2_{layer}"]
    with Stage(nc) as st:
        rw, rb, desc = st.sb("router_w", [P, DC, NE]), st.sb("router_b", [P, NE]), st.sb("descending", [P, NE])
        lg, l2, tmp = st.sb("logits", [P, NT, NE]), st.sb("logits2", [P, NT, NE]), st.sb("tie", [P, NT, NE])
        one = [st.sb("one_hot", [P, NT, NE]) for _ in range(2)]
        top = [st.sb("top", [P, NT]) for _ in range(2)]
        tie = st.sb("tie_max", [P, NT])
        pr = [st.sb("prob", [P, NT]) for _ in range(2)]
        comb = st.sb("weights", [P, NT, E])
        cur = [st.sb("weight_now", [P, NT]) for _ in range(2)]
        w1, w2 = st.sb("w1", [P, DC, HT * P]), st.sb("w2", [P, HT, D])
        w3 = st.sb("w3", [P, DC, HT * P]) if gated else None
        b1 = None if gated else st.sb("b1", [P, HT])
        hs = [st.sb("h_silu", [P, NT * P]) for _ in range(2)] if gated else None
        hT = st.sb("hT", [P, HT, NT * P])
        h_ps = [st.ps("h_ps", [P, NT * P]) for _ in range(2)]
        u_ps = [st.ps("u_ps", [P, NT * P]) for _ in range(2)] if gated else None
        y_ps = [st.ps("y_ps", [P, 512]) for _ in range(2)]
        r_ps = st.ps("router_ps", [P, NT, NE])
        if not gated:
            b2, combT = st.sb("b2", [E, D]), st.sb("weightsT", [E, NT * P])
            c_ps = st.ps("weightsT_ps", [E, NT * P])
        r_loaded, routed, step, e2s = st.sem("router_loaded"), st.sem("routed"), st.sem("dve_step"), st.sem("exp_done")
        turned, bias_made = st.sem("turned"), st.sem("bias_made")
        w1_loaded, w2_loaded = st.sem("w1_loaded"), st.sem("w2_loaded")
        h_made, silu_done, h_kept = st.sem("h_made"), st.sem("silu_done"), st.sem("h_kept")
        y_made, y_added, cur_ready = st.sem("y_made"), st.sem("y_added"), st.sem("weight_ready")
        own = st.sem("routing_step")
        NL1 = 2
        NR = 3 if gated else 4
        YB = 0 if gated else NT

        with nc.Block() as block:

            @block.sync
            def _(sp):
                sp.dma_start(rw[:, :, :], rw_d).then_inc(r_loaded, 16)
                sp.dma_start(rb[:, :], rb_d).then_inc(r_loaded, 16)
                sp.dma_start(desc[:, :], dram["descending"]).then_inc(r_loaded, 16)
                if not gated:
                    sp.dma_start(b2[:, :], dram["b2_2"]).then_inc(r_loaded, 16)

            @block.gpsimd
            def _(pool):
                with pool.Fori(0, E) as e:
                    pool.wait_ge(h_kept, e * HT + 1)
                    pool.dma_start(w1[:, :, :], w1_d[bass.ds(e, 1)].rearrange("o p c h -> (o p) c h"))\
                        .then_inc(w1_loaded, 16)
                    if gated:
                        pool.dma_start(w3[:, :, :], dram["e3_5"][bass.ds(e, 1)].rearrange("o p c h -> (o p) c h"))\
                            .then_inc(w1_loaded, 16)
                    else:
                        pool.dma_start(b1[:, :], dram["b1_2"][bass.ds(e, 1)].rearrange("o p h -> (o p) h"))\
                            .then_inc(w1_loaded, 16)

            @block.tensor
            def _(pe):
                pe.sem_inc(y_made, 1)
                pe.wait_ge(r_loaded, 16 * NR)
                for t in range(NT):
                    for c in range(DC):
                        last = pe.matmul(r_ps[:, t, :], R.xnT[:, c, t * P:(t + 1) * P], rw[:, c, :],
                                         start=(c == 0), stop=(c == DC - 1))
                last.then_inc(turned, 1)
                if not gated:
                    pe.wait_ge(routed, 1)
                    for t in range(NT):
                        last = pe.transpose(c_ps[:, t * P:(t + 1) * P], comb[:, t, :], R.identf[:, :])
                    last.then_inc(turned, 1)
                    pe.wait_ge(bias_made, 1)
                    for t in range(NT):
                        if t >= 2:
                            pe.wait_ge(y_added, t)
                        pe.matmul(y_ps[t % 2][:, 0:D], combT[:, t * P:(t + 1) * P], b2[:, :],
                                  start=True, stop=True).then_inc(turned, 1)
                with pe.Fori(0, E) as e:
                    pe.wait_ge(w1_loaded, e * (16 * NL1) + 16 * NL1)
                    for f in range(HT):
                        if f >= 2:
                            pe.wait_ge(h_kept, e * HT + f)
                        else:
                            pe.wait_ge(h_kept, e * HT + 1)
                        for w, ps in ((w1, h_ps), (w3, u_ps)):
                            if w is not None:
                                for c in range(DC):
                                    last = pe.matmul(ps[f % 2][:, :], w[:, c, f * P:(f + 1) * P], R.xnT[:, c, :],
                                                     start=(c == 0), stop=(c == DC - 1))
                        last.then_inc(h_made, 1)
                    pe.wait_ge(h_kept, e * HT + HT + 1)
                    pe.wait_ge(w2_loaded, e * 16 + 16)
                    for t in range(NT):
                        pe.wait_ge(y_added, e * NT + (YB + 1 + max(t - 1, 0)))
                        for f in range(HT):
                            last = pe.matmul(y_ps[t % 2][:, 0:D], hT[:, f, t * P:(t + 1) * P], w2[:, f, :],
                                             start=(f == 0), stop=(f == HT - 1))
                        last.then_inc(y_made, 1)

            @block.scalar
            def _(act):
                act.wait_ge(step, 1)
                act.activation(pr[1][:, :], pr[1][:, :], ACT.Exp).then_inc(e2s, 1)
                if not gated:
                    act.sem_inc(h_kept, 1)
                    act.wait_ge(turned, 2)
                    act.activation(combT[:, :], c_ps[:, :], ACT.Copy).then_inc(bias_made, 1)
                with act.Fori(0, E) as e:
                    act.wait_ge(y_made, e * NT + 1)
                    act.dma_start(w2[:, :, :], w2_d[bass.ds(e, 1)].rearrange("o p h m -> (o p) h m"))\
                       .then_inc(w2_loaded, 16)
                    for f in range(HT):
                        act.wait_ge(h_made, e * HT + (f + 1))
                        if gated:
                            act.wait_ge(h_kept, e * HT + max(f - 1, 0) + 1)
                            act.activation(hs[f % 2][:, :], h_ps[f % 2][:, :], func).then_inc(silu_done, 1)
                        else:
                            act.wait_ge(y_made, e * NT + 1)
                            act.activation(hT[:, f, :], h_ps[f % 2][:, :], func, bias=b1[:, f:f + 1])\
                               .then_inc(h_kept, 1)

            @block.vector
            def _(dve):
                dve.sem_inc(y_added, 1)
                dve.sem_inc(cur_ready, 1)
                if gated:
                    dve.sem_inc(h_kept, 1)

                def over(v):
                    return v[:, :].unsqueeze(2).broadcast_to([P, NT, NE])

                def row(v):
                    return v[:, :].unsqueeze(1).broadcast_to([P, NT, NE])

                n = 0
                dve.wait_ge(r_loaded, 16 * NR)
                dve.wait_ge(turned, 1)
                dve.tensor_tensor(lg[:, :, :], r_ps[:, :, :], row(rb), ALU.add).then_inc(own, 1)
                for k, src in enumerate((lg, l2)):
                    n += 1
                    dve.wait_ge(own, n)
                    dve.tensor_reduce(top[k][:, :], src[:, :, :], AX.X, ALU.max).then_inc(own, 1)
                    n += 1
                    dve.wait_ge(own, n)
                    dve.tensor_tensor(tmp[:, :, :], src[:, :, :], over(top[k]), ALU.is_equal).then_inc(own, 1)
                    n += 1
                    dve.wait_ge(own, n)
                    dve.tensor_tensor(tmp[:, :, :], tmp[:, :, :], row(desc), ALU.mult).then_inc(own, 1)
                    n += 1
                    dve.wait_ge(own, n)
                    dve.tensor_reduce(tie[:, :], tmp[:, :, :], AX.X, ALU.max).then_inc(own, 1)
                    n += 1
                    dve.wait_ge(own, n)
                    dve.tensor_tensor(one[k][:, :, :], tmp[:, :, :], over(tie), ALU.is_equal).then_inc(own, 1)
                    if k == 0:
                        n += 1
                        dve.wait_ge(own, n)
                        dve.scalar_tensor_tensor(out=l2[:, :, :].rearrange("p t e -> p (t e)"),
                                                 in0=one[0][:, :, :].rearrange("p t e -> p (t e)"), scalar=MASKED,
                                                 in1=lg[:, :, :].rearrange("p t e -> p (t e)"),
                                                 op0=ALU.mult, op1=ALU.add).then_inc(own, 1)
                dve.tensor_tensor(pr[1][:, :], top[1][:, :], top[0][:, :], ALU.subtract).then_inc(step, 1)
                dve.wait_ge(e2s, 1)
                dve.tensor_scalar(pr[0][:, :], pr[1][:, :], 1.0, None, ALU.add).then_inc(own, 1)
                n += 2
                dve.wait_ge(own, n)
                dve.reciprocal(pr[0][:, :], pr[0][:, :]).then_inc(own, 1)
                n += 1
                dve.wait_ge(own, n)
                dve.tensor_tensor(pr[1][:, :], pr[1][:, :], pr[0][:, :], ALU.mult).then_inc(own, 1)
                dve.tensor_tensor(one[0][:, :, :], one[0][:, :, :], over(pr[0]), ALU.mult).then_inc(own, 1)
                n += 2
                dve.wait_ge(own, n)
                dve.tensor_tensor(one[1][:, :, :], one[1][:, :, :], over(pr[1]), ALU.mult).then_inc(own, 1)
                dve.memset(comb[:, :, NE:E], shared_weight).then_inc(own, 1)
                n += 2
                dve.wait_ge(own, n)
                dve.tensor_tensor(comb[:, :, 0:NE], one[0][:, :, :], one[1][:, :, :], ALU.add).then_inc(routed, 1)
                if not gated:
                    for t in range(NT):
                        dve.wait_ge(turned, 3 + t)
                        dve.tensor_tensor(R.x[:, t, :], R.x[:, t, :], y_ps[t % 2][:, 0:D], ALU.add)\
                           .then_inc(y_added, 1)
                dve.wait_ge(routed, 1)
                with dve.Fori(0, E) as e:
                    if gated:
                        for f in range(HT):
                            dve.wait_ge(silu_done, e * HT + (f + 1))
                            dve.tensor_tensor(hT[:, f, :], hs[f % 2][:, :], u_ps[f % 2][:, :], ALU.mult)\
                               .then_inc(h_kept, 1)
                    dve.wait_ge(y_added, e * NT + (YB + 1))
                    dve.tensor_copy(cur[0][:, :], comb[:, :, bass.ds(e, 1)].rearrange("p t o -> p (t o)"))\
                       .then_inc(cur_ready, 1)
                    dve.wait_ge(cur_ready, e + 2)
                    for t in range(NT):
                        dve.wait_ge(y_made, e * NT + (t + 2))
                        dve.scalar_tensor_tensor(out=R.x[:, t, :], in0=y_ps[t % 2][:, 0:D], scalar=cur[0][:, t:t + 1],
                                                 in1=R.x[:, t, :], op0=ALU.mult, op1=ALU.add).then_inc(y_added, 1)


def signs_stage(nc, R, dram):
    HT = 8
    with Stage(nc) as st:
        k0 = st.sb("k0_words", [P, 2 * DC, HT * P // 4], I32)
        k1 = st.sb("k1_words", [P, HT, HT * P // 4], I32)
        k2 = st.sb("k2_words", [P, HT, D // 4], I32)
        w0 = st.sb("w0", [P, DC, HT * P])
        w1 = st.sb("w1", [P, HT, HT * P])
        w2 = st.sb("w2", [P, HT, D])
        sc = st.sb("scales", [P, 3])
        h1, h2 = st.sb("h1T", [P, HT, NT * P]), st.sb("h2T", [P, HT, NT * P])
        ps = [st.ps("h_ps", [P, NT * P]) for _ in range(4)]
        y_ps = [st.ps("y_ps", [P, 512]) for _ in range(2)]
        loaded, widened, made, kept = st.sem("loaded"), st.sem("widened"), st.sem("h_made"), st.sem("h_kept")
        y_made, y_added, differed = st.sem("y_made"), st.sem("y_added"), st.sem("differed")
        with nc.Block() as block:

            @block.sync
            def _(sp):
                sp.dma_start(k0[:, :, :], dram["k0"]).then_inc(loaded, 16)
                sp.dma_start(sc[:, :], dram["signs_scales"]).then_inc(loaded, 16)
                sp.dma_start(k1[:, :, :], dram["k1"]).then_inc(loaded, 16)
                sp.dma_start(k2[:, :, :], dram["k2"]).then_inc(loaded, 16)

            @block.vector
            def _(dve):
                dve.wait_ge(loaded, 64)
                a = k0[:, :, :].bitcast(U8)
                dve.tensor_tensor(w0[:, :, :], a[:, 0:DC, :], a[:, DC:2 * DC, :], ALU.subtract).then_inc(differed, 1)
                dve.wait_ge(differed, 1)
                dve.tensor_scalar(w0[:, :, :], w0[:, :, :], 4.0, None, ALU.mult).then_inc(widened, 1)
                dve.tensor_scalar(w1[:, :, :], k1[:, :, :].bitcast(U8), 4.0, -2.0, ALU.mult, ALU.add)\
                   .then_inc(widened, 1)
                dve.tensor_scalar(w2[:, :, :], k2[:, :, :].bitcast(U8), 2.0, -1.0, ALU.mult, ALU.add)\
                   .then_inc(widened, 1)
                for t in range(NT):
                    dve.wait_ge(y_made, t + 1)
                    dve.scalar_tensor_tensor(out=R.x[:, t, :], in0=y_ps[t % 2][:, 0:D], scalar=sc[:, 2:3],
                                             in1=R.x[:, t, :], op0=ALU.mult, op1=ALU.add).then_inc(y_added, 1)

            @block.tensor
            def _(pe):
                n = 0
                for w, src, C, ready in ((w0, R.xnT, DC, 1), (w1, h1, HT, 2)):
                    pe.wait_ge(widened, ready)
                    for f in range(HT):
                        if n >= 4:
                            pe.wait_ge(kept, n - 3)
                        if C == HT and f == 0:
                            pe.wait_ge(kept, HT)
                        for c in range(C):
                            last = pe.matmul(ps[n % 4][:, :], w[:, c, f * P:(f + 1) * P], src[:, c, :],
                                             start=(c == 0), stop=(c == C - 1))
                        last.then_inc(made, 1)
                        n += 1
                pe.wait_ge(widened, 3)
                pe.wait_ge(kept, 2 * HT)
                for t in range(NT):
                    if t >= 2:
                        pe.wait_ge(y_added, t - 1)
                    for c in range(HT):
                        last = pe.matmul(y_ps[t % 2][:, 0:D], h2[:, c, t * P:(t + 1) * P], w2[:, c, :],
                                         start=(c == 0), stop=(c == HT - 1))
                    last.then_inc(y_made, 1)

            @block.scalar
            def _(act):
                act.wait_ge(loaded, 64)
                for n in range(2 * HT):
                    act.wait_ge(made, n + 1)
                    h = h1 if n < HT else h2
                    act.activation(h[:, n % HT, :], ps[n % 4][:, :], ACT.Relu,
                                   scale=sc[:, n // HT:n // HT + 1]).then_inc(kept, 1)


def context_stage(nc, R, att, ctxT_d, ctx_d):
    NKT, EK = SK // P, 4
    EU = NKT // EK
    parts = SK // 1024
    VW = D + 1
    with Stage(nc) as st:
        KT = st.sb("ctxT", [P, DC, SK])
        V = st.sb("ctx_ones", [P, NKT, VW])
        mx = st.sb("max_parts", [P, QT, parts])
        neg = st.sb("neg_max", [P, QT])
        nrow = st.sb("neg_max_row", [1, S])
        rsum = st.sb("sum_recip", [P, QT])
        PT = [st.sb("probsT", [P, EK * S]) for _ in range(3)]
        big = st.ps("scores", [P, 2, 1024])
        pv = st.ps("weighted", [P, QT, 512])
        rp = st.ps("row_ps", [1, S])
        loaded, ones_set = st.sem("loaded"), st.sem("ones_set")
        s_made, s_read, maxed, turned, row_kept = (st.sem(n) for n in (
            "scores_made", "scores_read", "maxed", "turned", "row_kept"))
        st_made, exp_done, pv_done, summed, normed = (st.sem(n) for n in (
            "scoresT_made", "exp_done", "weighted_done", "summed", "normalised"))
        MU = QT * parts
        with nc.Block() as block:

            @block.sync
            def _(sp):
                for b in range(B):
                    if b:
                        sp.wait_ge(pv_done, b * EU)
                    sp.dma_start(KT[:, :, :], ctxT_d[b]).then_inc(loaded, 16)
                    sp.dma_start(V[:, :, 0:D], ctx_d[b]).then_inc(loaded, 16)

            @block.gpsimd
            def _(pool):
                pool.memset(V[:, :, D:VW], 1.0).then_inc(ones_set, 1)

            @block.tensor
            def _(pe):
                pe.wait_ge(ones_set, 1)
                for b in range(B):
                    pe.wait_ge(loaded, (b + 1) * 32)
                    u = b * MU
                    if b:
                        pe.wait_ge(exp_done, b * EU)
                    for q in range(QT):
                        for k in range(parts):
                            if u % MU >= 2:
                                pe.wait_ge(s_read, u - 1)
                            for h in range(2):
                                k0 = k * 1024 + h * 512
                                for c in range(DC):
                                    last = pe.matmul(big[:, u % 2, h * 512:(h + 1) * 512],
                                                     R.xnT[:, c, b * S + q * P:b * S + (q + 1) * P],
                                                     KT[:, c, k0:k0 + 512], start=(c == 0), stop=(c == DC - 1))
                            last.then_inc(s_made, 1)
                            u += 1
                    pe.wait_ge(maxed, b + 1)
                    for q in range(QT):
                        last = pe.transpose(rp[:, q * P:(q + 1) * P], neg[:, q:q + 1], R.identf[:, :])
                    last.then_inc(turned, 1)
                    pe.wait_ge(row_kept, b + 1)

                    def weigh(e):
                        pe.wait_ge(exp_done, b * EU + e + 1)
                        if e == 0 and b:
                            pe.wait_ge(normed, b)
                        for i in range(EK):
                            kt = e * EK + i
                            for q in range(QT):
                                last = pe.matmul(pv[:, q, 0:VW], PT[e % 3][:, i * S + q * P:i * S + (q + 1) * P],
                                                 V[:, kt, :], start=(kt == 0), stop=(kt == NKT - 1))
                        last.then_inc(pv_done, 1)

                    for e in range(EU):
                        if e >= 2:
                            pe.wait_ge(exp_done, b * EU + e - 1)
                        for i in range(EK):
                            kt = e * EK + i
                            o = big[:, e % 2, i * S:(i + 1) * S]
                            for c in range(DC):
                                pe.matmul(o, KT[:, c, kt * P:(kt + 1) * P], R.xnT[:, c, b * S:(b + 1) * S],
                                          start=(c == 0), stop=False)
                            last = pe.matmul(o, R.onesf[0:1, :], nrow[:, :], start=False, stop=True)
                        last.then_inc(st_made, 1)
                        if e >= 1:
                            weigh(e - 1)
                    weigh(EU - 1)

            @block.scalar
            def _(act):
                for e in range(B * EU):
                    act.wait_ge(st_made, e + 1)
                    if e >= 3:
                        act.wait_ge(pv_done, e - 2)
                    act.activation(PT[e % EU % 3][:, :], big[:, e % 2, :], ACT.Exp).then_inc(exp_done, 1)

            @block.vector
            def _(dve):
                for b in range(B):
                    for u in range(MU):
                        dve.wait_ge(s_made, b * MU + u + 1)
                        dve.tensor_reduce(mx[:, u // parts, u % parts:u % parts + 1], big[:, u % 2, :],
                                          AX.X, ALU.max).then_inc(s_read, 1)
                    dve.wait_ge(s_read, (b + 1) * MU)
                    dve.tensor_reduce(neg[:, :], mx[:, :, :], AX.X, ALU.max, negate=True).then_inc(maxed, 1)
                    dve.wait_ge(turned, b + 1)
                    dve.tensor_copy(nrow[:, :], rp[:, :]).then_inc(row_kept, 1)
                    dve.wait_ge(pv_done, (b + 1) * EU)
                    dve.reciprocal(rsum[:, :], pv[:, :, D]).then_inc(summed, 1)
                    dve.wait_ge(summed, b + 1)
                    for q in range(QT):
                        ins = dve.tensor_scalar(att[:, b * QT + q, :], pv[:, q, 0:D], rsum[:, q:q + 1], None, ALU.mult)
                    ins.then_inc(normed, 1)


def combine_stage(nc, R, att, dram):
    with Stage(nc) as st:
        w, rowp = st.sb("w_comb", [P, 2 * DC, D]), st.sb("b_gamma_beta", [P, 3, D])
        aT = st.sb("attT", [P, DC, NT * P])
        y = st.sb("y", [P, NT, D])
        stats, mv, rstd = st.sb("stats", [P, NT, 6]), st.sb("mean_var", [P, NT, 2]), st.sb("rstd", [P, NT])
        tp = [st.ps("tp", [P, NT * P]) for _ in range(DC)]
        acc = [st.ps("acc", [P, 512]) for _ in range(NT)]
        loaded, turned, kept, made, step, rooted = (st.sem(n) for n in (
            "loaded", "turned", "kept", "made", "dve_step", "rooted"))
        with nc.Block() as block:

            @block.sync
            def _(sp):
                sp.dma_start(w[:, :, :], dram["w9"]).then_inc(loaded, 16)
                sp.dma_start(rowp[:, :, :], dram["r9"]).then_inc(loaded, 16)

            @block.tensor
            def _(pe):
                for c in range(DC):
                    for t in range(NT):
                        last = pe.transpose(tp[c][:, t * P:(t + 1) * P], att[:, t, c * P:(c + 1) * P], R.identf[:, :])
                    last.then_inc(turned, 1)
                pe.wait_ge(kept, DC)
                pe.wait_ge(loaded, 32)
                for t in range(NT):
                    for c in range(2 * DC):
                        src = aT if c < DC else R.xnT
                        last = pe.matmul(acc[t][:, 0:D], src[:, c % DC, t * P:(t + 1) * P], w[:, c, :],
                                         start=(c == 0), stop=(c == 2 * DC - 1))
                    last.then_inc(made, 1)

            @block.scalar
            def _(act):
                for c in range(DC):
                    act.wait_ge(turned, c + 1)
                    act.activation(aT[:, c, :], tp[c][:, :], ACT.Copy).then_inc(kept, 1)
                act.wait_ge(step, 3 * NT + 1)
                act.activation(rstd[:, :], rstd[:, :], ACT.Sqrt).then_inc(rooted, 1)

            @block.vector
            def _(dve):
                dve.wait_ge(loaded, 32)
                for t in range(NT):
                    dve.wait_ge(made, t + 1)
                    dve.tensor_tensor(y[:, t, :], acc[t][:, 0:D], rowp[:, 0, :], ALU.add).then_inc(step, 1)
                for t in range(NT):
                    dve.wait_ge(step, t + 1)
                    dve.bn_stats(stats[:, t, :], y[:, t, :]).then_inc(step, 1)
                for t in range(NT):
                    dve.wait_ge(step, NT + t + 1)
                    dve.bn_aggr(mv[:, t, :], stats[:, t, :]).then_inc(step, 1)
                dve.wait_ge(step, 3 * NT)
                dve.tensor_scalar(rstd[:, :], mv[:, :, 1], EPS, None, ALU.add).then_inc(step, 1)
                dve.wait_ge(rooted, 1)
                dve.reciprocal(rstd[:, :], rstd[:, :]).then_inc(step, 1)
                n = 3 * NT + 2
                dve.wait_ge(step, n)
                for t in range(NT):
                    dve.tensor_scalar(y[:, t, :], y[:, t, :], mv[:, t, 0:1], rstd[:, t:t + 1],
                                      ALU.subtract, ALU.mult).then_inc(step, 1)
                for k, op in ((1, ALU.mult), (2, ALU.add)):
                    for t in range(NT):
                        n += 1
                        dve.wait_ge(step, n)
                        dve.tensor_tensor(y[:, t, :], y[:, t, :], rowp[:, k, :], op).then_inc(step, 1)
                for t in range(NT):
                    n += 1
                    dve.wait_ge(step, n)
                    dve.tensor_tensor(R.x[:, t, :], R.x[:, t, :], y[:, t, :], ALU.add)


def quantised_stage(nc, R, dram):
    HT = 8
    MAGIC = 1.5 * 2.0 ** 23
    SMALL = 1e-8
    with Stage(nc) as st:
        w1, w2 = st.sb("w1", [P, HT, D]), st.sb("w2", [P, DC, HT * P])
        b1, b2 = st.sb("b1", [P, HT]), st.sb("b2", [P, DC])
        w1q, w2q = st.sb("w1q", [P, HT, D], BF16), st.sb("w2q", [P, DC, HT * P], BF16)
        w1T, w2T = st.sb("w1qT", [P, DC, HT * P], BF16), st.sb("w2qT", [P, HT, D], BF16)
        s1, s2, i1, i2 = (st.sb(n, [P, w]) for n, w in (("s1", HT), ("s2", DC), ("i1", HT), ("i2", DC)))
        c1, c2 = st.sb("bq1", [P, HT]), st.sb("bq2", [P, DC])
        pm, gm, gs, gi = (st.sb(n, [P, 2]) for n in ("part_max", "all_max", "in_scale", "in_inverse"))
        grow = st.sb("max_row", [1, 2])
        xq = st.sb("xq", [P, DC, NT * P], BF16)
        h, hq = st.sb("h", [P, HT, NT * P]), st.sb("hq", [P, HT, NT * P], BF16)
        yT = st.sb("yT", [P, DC, NT * P])
        wp = [st.ps("w_turned", [P, 1024], BF16) for _ in range(2)]
        tp = st.ps("max_turned", [P, 512])
        ps = [st.ps("h_ps", [P, NT * P]) for _ in range(3)]
        yp = [st.ps("y_turned", [P, 512]) for _ in range(2)]
        loaded, step, wq_ready, w_turned, w_kept = (st.sem(n) for n in (
            "loaded", "dve_step", "w_quantised", "w_turned", "w_kept"))
        maxed, m_turned, row_ready, x_ready, made, kept, bias_ready = (st.sem(n) for n in (
            "maxed", "max_turned", "max_row_ready", "x_quantised", "made", "kept", "bias_ready"))
        out_turned, part = st.sem("out_turned"), st.sem("h_part_max")
        with nc.Block() as block:

            @block.sync
            def _(sp):
                sp.dma_start(w1[:, :, :], dram["w11_1"]).then_inc(loaded, 16)
                sp.dma_start(b1[:, :], dram["b11_1"]).then_inc(loaded, 16)
                sp.dma_start(w2[:, :, :], dram["w11_2"]).then_inc(loaded, 16)
                sp.dma_start(b2[:, :], dram["b11_2"]).then_inc(loaded, 16)

            @block.vector
            def _(dve):
                n = 0

                def did(ins):
                    nonlocal n
                    ins.then_inc(step, 1)
                    n += 1

                def round_to(out, src, inverse, low, high):
                    did(dve.tensor_scalar(src, src, inverse, MAGIC, ALU.mult, ALU.add))
                    dve.wait_ge(step, n)
                    did(dve.tensor_scalar(src, src, -MAGIC, low, ALU.add, ALU.max))
                    dve.wait_ge(step, n)
                    return dve.tensor_scalar(out, src, high, None, ALU.min)

                def weights(w, wq, s, inv, count):
                    did(dve.tensor_reduce(s[:, :], w[:, :, :], AX.X, ALU.max, apply_absolute_value=True))
                    dve.wait_ge(step, n)
                    did(dve.tensor_scalar(s[:, :], s[:, :], SMALL, 1.0 / 127.0, ALU.max, ALU.mult))
                    dve.wait_ge(step, n)
                    did(dve.reciprocal(inv[:, :], s[:, :]))
                    dve.wait_ge(step, n)
                    for f in range(count):
                        round_to(wq[:, f, :], w[:, f, :], inv[:, f:f + 1], -128.0, 127.0).then_inc(wq_ready, 1)

                def input_scale(k):
                    dve.wait_ge(m_turned, 2 * k + 1)
                    dve.tensor_reduce(grow[:, k:k + 1], tp[0:1, 0:P], AX.X, ALU.max).then_inc(row_ready, 1)
                    dve.wait_ge(m_turned, 2 * k + 2)
                    did(dve.tensor_scalar(gs[:, k:k + 1], tp[:, P:P + 1], SMALL, 1.0 / 255.0, ALU.max, ALU.mult))
                    dve.wait_ge(step, n)
                    did(dve.reciprocal(gi[:, k:k + 1], gs[:, k:k + 1]))
                    dve.wait_ge(step, n)

                def bias(s, inv, b, c, k):
                    did(dve.tensor_scalar(s[:, :], s[:, :], gs[:, k:k + 1], None, ALU.mult))
                    dve.wait_ge(step, n)
                    did(dve.reciprocal(inv[:, :], s[:, :]))
                    dve.wait_ge(step, n)
                    did(dve.tensor_tensor(c[:, :], b[:, :], inv[:, :], ALU.mult))
                    dve.wait_ge(step, n)
                    did(dve.tensor_scalar(c[:, :], c[:, :], MAGIC, -MAGIC, ALU.add, ALU.add))
                    dve.wait_ge(step, n)
                    dve.tensor_tensor(c[:, :], c[:, :], s[:, :], ALU.mult).then_inc(bias_ready, 1)

                dve.tensor_reduce(pm[:, 0:1], R.xnT[:, :, :], AX.XY, ALU.max).then_inc(maxed, 1)
                dve.wait_ge(loaded, 64)
                weights(w1, w1q, s1, i1, HT)
                input_scale(0)
                for c in range(DC):
                    round_to(xq[:, c, :], R.xnT[:, c, :], gi[:, 0:1], 0.0, 255.0).then_inc(x_ready, 1)
                bias(s1, i1, b1, c1, 0)
                weights(w2, w2q, s2, i2, DC)
                dve.wait_ge(kept, HT)
                dve.tensor_reduce(pm[:, 1:2], h[:, :, :], AX.XY, ALU.max).then_inc(maxed, 1)
                input_scale(1)
                for c in range(HT):
                    round_to(hq[:, c, :], h[:, c, :], gi[:, 1:2], 0.0, 255.0).then_inc(x_ready, 1)
                bias(s2, i2, b2, c2, 1)
                for t in range(NT):
                    dve.wait_ge(out_turned, t // 2 * 2 + 2)
                    dve.tensor_tensor(R.x[:, t, :], R.x[:, t, :], yp[t // 2][:, (t % 2) * D:(t % 2 + 1) * D], ALU.add)

            @block.tensor
            def _(pe):
                def all_max(k):
                    pe.wait_ge(maxed, k + 1)
                    pe.transpose(tp[0:1, 0:P], pm[:, k:k + 1], R.identf[:, :]).then_inc(m_turned, 1)
                    pe.wait_ge(row_ready, k + 1)
                    pe.matmul(tp[:, P:P + 1], R.onesf[0:1, :], grow[:, k:k + 1], start=True, stop=True)\
                      .then_inc(m_turned, 1)

                all_max(0)
                for c in range(DC):
                    pe.wait_ge(wq_ready, HT)
                    for f in range(HT):
                        last = pe.transpose(wp[c][:, f * P:(f + 1) * P], w1q[:, f, c * P:(c + 1) * P], R.identb[:, :])
                    last.then_inc(w_turned, 1)
                pe.wait_ge(w_kept, 2)
                pe.wait_ge(x_ready, DC)
                for f in range(HT):
                    if f >= 3:
                        pe.wait_ge(kept, f - 2)
                    for c in range(DC):
                        last = pe.matmul(ps[f % 3][:, :], w1T[:, c, f * P:(f + 1) * P], xq[:, c, :],
                                         start=(c == 0), stop=(c == DC - 1))
                    last.then_inc(made, 1)
                pe.wait_ge(wq_ready, HT + DC)
                for o in range(2):
                    for f in range(4):
                        for c in range(DC):
                            last = pe.transpose(wp[o][:, f * D + c * P:f * D + (c + 1) * P],
                                                w2q[:, c, (4 * o + f) * P:(4 * o + f + 1) * P], R.identb[:, :])
                    last.then_inc(w_turned, 1)
                pe.wait_ge(kept, HT)
                all_max(1)
                pe.wait_ge(w_kept, 4)
                pe.wait_ge(x_ready, DC + HT)
                for o in range(DC):
                    for f in range(HT):
                        last = pe.matmul(ps[o][:, :], w2T[:, f, o * P:(o + 1) * P], hq[:, f, :],
                                         start=(f == 0), stop=(f == HT - 1))
                    last.then_inc(made, 1)
                pe.wait_ge(kept, HT + DC)
                for t in range(NT):
                    for o in range(DC):
                        last = pe.transpose(yp[t // 2][:, (t % 2) * D + o * P:(t % 2) * D + (o + 1) * P],
                                            yT[:, o, t * P:(t + 1) * P], R.identf[:, :])
                    last.then_inc(out_turned, 1)

            @block.scalar
            def _(act):
                for c in range(DC):
                    act.wait_ge(w_turned, c + 1)
                    act.activation(w1T[:, c, :], wp[c][:, :], ACT.Copy).then_inc(w_kept, 1)
                act.wait_ge(bias_ready, 1)
                for f in range(HT):
                    act.wait_ge(made, f + 1)
                    act.activation(h[:, f, :], ps[f % 3][:, :], ACT.Relu, bias=c1[:, f:f + 1],
                                   scale=s1[:, f:f + 1]).then_inc(kept, 1)
                for o in range(2):
                    act.wait_ge(w_turned, 3 + o)
                    act.activation(w2T[:, 4 * o:4 * (o + 1), :], wp[o][:, :].rearrange("p (f m) -> p f m", f=4),
                                   ACT.Copy).then_inc(w_kept, 1)
                act.wait_ge(bias_ready, 2)
                for o in range(DC):
                    act.wait_ge(made, HT + o + 1)
                    act.activation(yT[:, o, :], ps[o][:, :], ACT.Identity, bias=c2[:, o:o + 1],
                                   scale=s2[:, o:o + 1]).then_inc(kept, 1)


def mamba_stages(nc, R, dram):
    CT, NS, K = 4, 16, 4
    T = NT * P
    bc_d = nc.dram_tensor("bc_rows", [2 * NS, T], F32, kind="Internal").ap()
    with ExitStack() as keep:
        def sb(name, shape, dt=F32):
            return keep.enter_context(nc.sbuf_tensor("ssm_" + name, shape, dt))

        actT, gate, delta, dx = (sb(n, [P, CT, T]) for n in ("act", "gate", "delta", "dx"))
        yT, A = sb("y", [P, CT, T]), sb("A", [P, CT, NS])
        cols = sb("cols", [P, CT, 9])
        BI, BG, CB, BD, DS, TAP = 0, 1, 2, 3, 4, 5
        wd = sb("w_delta", [P, CT, CT * P])
        wbc = sb("w_bc", [P, CT, 2 * NS])

        with Stage(nc) as st:
            win, wg = st.sb("w_in", [P, DC, CT * P]), st.sb("w_gate", [P, DC, CT * P])
            xz = st.sb("xz", [P, CT, B, K - 1 + S])
            cv = st.sb("conv", [P, CT, T])
            ps = [st.ps("ps", [P, T]) for _ in range(4)]
            loaded, made, xz_kept, conv, gate_kept, acted, zeroed = (st.sem(n) for n in (
                "loaded", "made", "xz_kept", "conv_step", "gate_kept", "acted", "zeroed"))
            with nc.Block() as block:

                @block.sync
                def _(sp):
                    sp.dma_start(cols[:, :, :], dram["s_cols"]).then_inc(loaded, 16)
                    sp.dma_start(win[:, :, :], dram["s_win"]).then_inc(loaded, 16)
                    sp.dma_start(wg[:, :, :], dram["s_wgate"]).then_inc(loaded, 16)
                    sp.dma_start(A[:, :, :], dram["s_alog"]).then_inc(loaded, 16)
                    sp.dma_start(wd[:, :, :], dram["s_wdelta"]).then_inc(loaded, 16)
                    sp.dma_start(wbc[:, :, :], dram["s_wbc"]).then_inc(loaded, 16)

                @block.gpsimd
                def _(pool):
                    pool.memset(xz[:, :, :, 0:K - 1], 0.0).then_inc(zeroed, 1)

                @block.tensor
                def _(pe):
                    pe.wait_ge(loaded, 96)
                    for n in range(2 * CT):
                        w, f = (win, n) if n < CT else (wg, n - CT)
                        if n >= 4:
                            pe.wait_ge(xz_kept, n - 3)
                        for c in range(DC):
                            last = pe.matmul(ps[n % 4][:, :], w[:, c, f * P:(f + 1) * P], R.xnT[:, c, :],
                                             start=(c == 0), stop=(c == DC - 1))
                        last.then_inc(made, 1)

                @block.vector
                def _(dve):
                    dve.wait_ge(zeroed, 1)
                    for f in range(CT):
                        dve.wait_ge(xz_kept, f + 1)
                        dst = cv[:, f, :].rearrange("p (b s) -> p b s", b=B)
                        for k in range(K):
                            src = xz[:, f, :, k:k + S]
                            tap = cols[:, f, TAP + k:TAP + k + 1]
                            if k == 0:
                                dve.tensor_scalar(dst, src, tap, None, ALU.mult).then_inc(conv, 1)
                            else:
                                dve.wait_ge(conv, f * K + k)
                                dve.scalar_tensor_tensor(out=dst, in0=src, scalar=tap, in1=dst,
                                                         op0=ALU.mult, op1=ALU.add).then_inc(conv, 1)

                @block.scalar
                def _(act):
                    for f in range(CT):
                        act.wait_ge(made, f + 1)
                        act.activation(xz[:, f, :, K - 1:K - 1 + S], ps[f][:, :].rearrange("p (b s) -> p b s", b=B),
                                       ACT.Identity, bias=cols[:, f, BI:BI + 1]).then_inc(xz_kept, 1)
                    for f in range(CT):
                        act.wait_ge(made, CT + f + 1)
                        act.activation(gate[:, f, :], ps[f][:, :], ACT.Silu, bias=cols[:, f, BG:BG + 1])
                    for f in range(CT):
                        act.wait_ge(conv, (f + 1) * K)
                        act.activation(actT[:, f, :], cv[:, f, :], ACT.Silu, bias=cols[:, f, CB:CB + 1])
                    act.activation(A[:, :, :], A[:, :, :], ACT.Exp).then_inc(acted, 1)

        with Stage(nc) as st:
            z, ez = st.sb("z", [P, CT, T]), st.sb("ez", [P, CT, T])
            bc = st.sb("bc", [2 * NS, T])
            ps = [st.ps("ps", [P, T]) for _ in range(CT)]
            bp = st.ps("bc_ps", [2 * NS, T])
            made, kept, lned, step, bc_made, stored = (st.sem(n) for n in (
                "made", "z_kept", "ln_done", "dve_step", "bc_kept", "bc_stored"))
            with nc.Block() as block:

                @block.tensor
                def _(pe):
                    for c in range(CT):
                        last = pe.matmul(bp[:, :], wbc[:, c, :], actT[:, c, :], start=(c == 0), stop=(c == CT - 1))
                    last.then_inc(made, 1)
                    for f in range(CT):
                        for c in range(CT):
                            last = pe.matmul(ps[f][:, :], wd[:, c, f * P:(f + 1) * P], actT[:, c, :],
                                             start=(c == 0), stop=(c == CT - 1))
                        last.then_inc(made, 1)

                @block.sync
                def _(sp):
                    sp.wait_ge(bc_made, 1)
                    sp.dma_start(bc_d, bc[:, :]).then_inc(stored, 16)
                    sp.wait_ge(stored, 16)

                @block.scalar
                def _(act):
                    act.wait_ge(made, 1)
                    act.activation(bc[:, :], bp[:, :], ACT.Copy).then_inc(bc_made, 1)
                    for f in range(CT):
                        act.wait_ge(made, f + 2)
                        act.activation(z[:, f, :], ps[f][:, :], ACT.Identity, bias=cols[:, f, BD:BD + 1])\
                           .then_inc(kept, 1)
                    act.wait_ge(kept, CT)
                    act.activation(ez[:, :, :], z[:, :, :], ACT.Abs).then_inc(kept, 1)
                    act.wait_ge(kept, CT + 1)
                    act.activation(ez[:, :, :], ez[:, :, :], ACT.Exp, scale=-1.0).then_inc(kept, 1)
                    act.wait_ge(kept, CT + 2)
                    act.activation(ez[:, :, :], ez[:, :, :], ACT.Ln, bias=1.0).then_inc(lned, 1)

                @block.vector
                def _(dve):
                    dve.tensor_scalar(A[:, :, :], A[:, :, :], -1.0, None, ALU.mult)
                    dve.wait_ge(lned, 1)
                    dve.tensor_scalar(delta[:, :, :], z[:, :, :], 0.0, None, ALU.max).then_inc(step, 1)
                    dve.wait_ge(step, 1)
                    dve.tensor_tensor(delta[:, :, :], delta[:, :, :], ez[:, :, :], ALU.add).then_inc(step, 1)
                    dve.wait_ge(step, 2)
                    dve.tensor_tensor(dx[:, :, :], delta[:, :, :], actT[:, :, :], ALU.mult)

        with Stage(nc) as st:
            bcb = st.sb("bc_all", [P, 2 * NS, T])
            dA, dB = ([st.sb(n, [P, T]) for _ in range(2)] for n in ("dA", "dBx"))
            hh, hc = ([st.sb(n, [P, T]) for _ in range(2)] for n in ("h", "hC"))
            zero = st.sb("zero", [P, T])
            An = st.sb("A_now", [P, CT])
            yp = [st.ps("y_ps", [P, T]) for _ in range(CT)]
            loaded, a_ready, da, db, scanned, hc_ready, summed = (st.sem(n) for n in (
                "bc_loaded", "A_ready", "dA_ready", "dBx_ready", "scanned", "hC_ready", "summed"))
            cleared = st.sem("cleared")
            with nc.Block() as block:

                @block.sync
                def _(sp):
                    sp.dma_start(bcb[:, :, :], bc_d.partition_broadcast(P)).then_inc(loaded, 16)
                    sp.wait_ge(loaded, 16)

                @block.scalar
                def _(act):
                    act.sem_inc(a_ready, 1)
                    act.sem_inc(da, 1)
                    with act.Fori(0, NS) as n:
                        act.wait_ge(da, n * CT + 1)
                        act.activation(An[:, :], A[:, :, bass.ds(n, 1)].rearrange("p c o -> p (c o)"), ACT.Copy)\
                           .then_inc(a_ready, 1)
                        act.wait_ge(a_ready, n + 2)
                        for i in range(CT):
                            act.wait_ge(scanned, n * CT + (1 + max(i - 1, 0)))
                            act.activation(dA[i % 2][:, :], delta[:, i, :], ACT.Exp, scale=An[:, i:i + 1])\
                               .then_inc(da, 1)

                @block.vector
                def _(dve):
                    dve.memset(zero[:, :], 0.0).then_inc(cleared, 1)
                    dve.sem_inc(scanned, 1)
                    dve.sem_inc(hc_ready, 1)
                    dve.wait_ge(loaded, 16)
                    with dve.Fori(0, NS) as n:
                        for i in range(CT):
                            dve.tensor_tensor(dB[i % 2][:, :], dx[:, i, :],
                                              bcb[:, bass.ds(n, 1), :].rearrange("p o t -> p (o t)"), ALU.mult)\
                               .then_inc(db, 1)
                            dve.wait_ge(da, n * CT + (i + 2))
                            dve.wait_ge(db, n * CT + (i + 1))
                            dve.wait_ge(hc_ready, n * CT + (1 + max(i - 1, 0)))
                            for b in range(B):
                                s = slice(b * S, (b + 1) * S)
                                ins = dve.tensor_tensor_scan(hh[i % 2][:, s], dA[i % 2][:, s], dB[i % 2][:, s],
                                                             0.0, ALU.mult, ALU.add)
                            ins.then_inc(scanned, 1)
                            dve.wait_ge(scanned, n * CT + (i + 2))
                            dve.wait_ge(summed, n * CT + (1 + max(i - 1, 0)))
                            dve.tensor_tensor(hc[i % 2][:, :], hh[i % 2][:, :],
                                              bcb[:, bass.ds(n + NS, 1), :].rearrange("p o t -> p (o t)"),
                                              ALU.mult).then_inc(hc_ready, 1)

                @block.tensor
                def _(pe):
                    pe.wait_ge(cleared, 1)
                    for i in range(CT):
                        last = pe.matmul(yp[i][:, :], R.identf[:, :], zero[:, :], start=True, stop=False,
                                         skip_group_check=True)
                    last.then_inc(summed, 1)
                    with pe.Fori(0, NS) as n:
                        for i in range(CT):
                            pe.wait_ge(hc_ready, n * CT + (i + 2))
                            pe.matmul(yp[i][:, :], R.identf[:, :], hc[i % 2][:, :], start=False, stop=False,
                                      skip_group_check=True).then_inc(summed, 1)
                    for i in range(CT):
                        pe.matmul(yp[i][:, :], R.identf[:, :], zero[:, :], start=False, stop=True,
                                  skip_group_check=True).then_inc(summed, 1)

            with nc.Block() as block:

                @block.vector
                def _(dve):
                    for i in range(CT):
                        dve.scalar_tensor_tensor(out=yT[:, i, :], in0=actT[:, i, :], scalar=cols[:, i, DS:DS + 1],
                                                 in1=yp[i][:, :], op0=ALU.mult, op1=ALU.add).then_inc(cleared, 1)
                    for i in range(CT):
                        dve.wait_ge(cleared, i + 2)
                        dve.tensor_tensor(yT[:, i, :], yT[:, i, :], gate[:, i, :], ALU.mult)

        with Stage(nc) as st:
            wo, bo = st.sb("w_out", [P, CT, D]), st.sb("b_out", [P, D])
            ps = [st.ps("ps", [P, 512]) for _ in range(NT)]
            loaded, made, biased = st.sem("loaded"), st.sem("made"), st.sem("biased")
            with nc.Block() as block:

                @block.sync
                def _(sp):
                    sp.dma_start(wo[:, :, :], dram["s_wout"]).then_inc(loaded, 16)
                    sp.dma_start(bo[:, :], dram["s_bout"]).then_inc(loaded, 16)

                @block.tensor
                def _(pe):
                    pe.wait_ge(loaded, 32)
                    for t in range(NT):
                        for c in range(CT):
                            last = pe.matmul(ps[t][:, 0:D], yT[:, c, t * P:(t + 1) * P], wo[:, c, :],
                                             start=(c == 0), stop=(c == CT - 1))
                        last.then_inc(made, 1)

                @block.vector
                def _(dve):
                    dve.wait_ge(loaded, 32)
                    for t in range(NT):
                        dve.tensor_tensor(R.x[:, t, :], R.x[:, t, :], bo[:, :], ALU.add).then_inc(biased, 1)
                    for t in range(NT):
                        dve.wait_ge(biased, t + 1)
                        dve.wait_ge(made, t + 1)
                        dve.tensor_tensor(R.x[:, t, :], R.x[:, t, :], ps[t][:, 0:D], ALU.add)


class Resident:
    pass


def build(nc, dram, out):
    R = Resident()
    Stage.number = 0
    with ExitStack() as keep:
        def sb(name, shape, dt=F32):
            return keep.enter_context(nc.sbuf_tensor(name, shape, dt))

        R.x, R.xn = sb("x_res", [P, NT, D]), sb("xn", [P, NT, D])
        R.xnT = sb("xnT", [P, DC, NT * P])
        R.identf, R.identb, R.onesf = sb("identf", [P, P]), sb("identb", [P, P], BF16), sb("onesf", [P, P])
        R.stored = nc.alloc_semaphore("out_stored")
        setup_stage(nc, R, dram["x"])

        def attend(layer, width, nk, hg, d, scale, out_bias, **how):
            norm_stage(nc, R)
            with nc.sbuf_tensor(f"att{layer}", [P, NT, width], F32) as att:
                attention_stage(nc, R, att, dram[f"w{layer}"], nk, hg, d, scale, **how)
                add_projected_stage(nc, R, att, width, dram[f"o{layer}"], dram[f"ob{layer}"] if out_bias else None)

        causal = (dram["causal_q"], dram["causal_k"])
        if 0 in LAYERS:
            attend(0, D, SK, 4, 16, 0.25, True, ctxT=dram["ctxT"], masks=(dram["m0q"], dram["m0k"]))
        if 1 in LAYERS:
            attend(1, D, S, 4, 16, 1.0 / 16, False, masks=causal, rope=(dram["rope_k"], dram["rope_q"]))
        if 2 in LAYERS:
            norm_stage(nc, R)
            experts_stage(nc, R, dram, 2, 10, ACT.Gelu, 0.5)
        if 3 in LAYERS:
            attend(3, 1024, SK, 1, 64, 0.125, True, ctxT=dram["ctxT"], masks=(dram["m3q"], dram["m3k"]))
        if 4 in LAYERS:
            scratch = nc.dram_tensor("mixed_heads", [B, 16, S, 16], F32, kind="Internal").ap()
            norm_stage(nc, R)
            head_mix_stage(nc, R, dram, scratch)
            with nc.sbuf_tensor("att4", [P, NT, D], F32) as att:
                reload_stage(nc, att, scratch)
                add_projected_stage(nc, R, att, D, dram["o4"], dram["ob4"])
        if 5 in LAYERS:
            norm_stage(nc, R)
            experts_stage(nc, R, dram, 5, 9, ACT.Silu, 1.0)
        if 6 in LAYERS:
            attend(6, D, SK, 4, 16, 0.25, False, ctxT=dram["ctxT"], key_mask=(dram["m6"], dram["key_sel"]))
        if 7 in LAYERS:
            norm_stage(nc, R)
            mamba_stages(nc, R, dram)
        if 8 in LAYERS:
            norm_stage(nc, R)
            signs_stage(nc, R, dram)
        if 9 in LAYERS:
            norm_stage(nc, R)
            with nc.sbuf_tensor("att9", [P, NT, D], F32) as att:
                context_stage(nc, R, att, dram["ctxT"], dram["ctx"])
                combine_stage(nc, R, att, dram)
        if 10 in LAYERS:
            attend(10, D, S, 4, 16, 0.25, False, masks=causal)
        if 11 in LAYERS:
            norm_stage(nc, R)
            quantised_stage(nc, R, dram)
        store_stage(nc, R, out)


def store_stage(nc, R, out):
    with nc.Block() as block:

        @block.sync
        def _(sp):
            sp.dma_start(out, R.x[:, :, :]).then_inc(R.stored, 16)
            sp.wait_ge(R.stored, 16)



def kernel(**inputs):
    import concourse.bacc as bacc
    from concourse.bass_utils import run_bass_kernel_spmd as run

    a = {k: np.asarray(v) for k, v in inputs.items()}
    nc = bacc.Bacc("TRN2", target_bir_lowering=False, num_devices=1)
    arrays, dram = {}, {}

    def give(name, v):
        v = np.ascontiguousarray(v)
        arrays["in_" + name] = v
        dram[name] = nc.dram_tensor("in_" + name, v.shape, mybir.dt.from_np(v.dtype), kind="ExternalInput").ap()

    def rows(w):
        return w.reshape(-1, P, w.shape[-1]).transpose(1, 0, 2)

    def spread(v):
        return np.broadcast_to(v.reshape(1, -1), (P, v.size))

    def pack(wk, wq, wv, bk, bq, bv, hg, d, rope=False):
        off, wf = pack_offsets(hg, d, rope)
        hs, vw, dt = P // hg, hg * (d + 1), wk.dtype
        out = np.zeros((16 // hg, P, wf), np.float32 if dt == np.float32 else dt)
        swap = np.arange(d) ^ 1
        for g in range(16 // hg):
            for j in range(hg):
                c = slice((g * hg + j) * d, (g * hg + j + 1) * d)
                for name, w, perm in (("wk", wk, None), ("wq", wq, None), ("wks", wk, swap), ("wqs", wq, swap)):
                    if name in off:
                        a0, a1 = off[name]
                        part = w[:, c] if perm is None else w[:, c][:, perm]
                        out[g, :, a0:a1].reshape(P, DC, P)[:, :, j * hs:j * hs + d] = rows(part)
                a0, a1 = off["wv"]
                out[g, :, a0:a1].reshape(P, DC, vw)[:, :, j * (d + 1):j * (d + 1) + d] = rows(wv[:, c])
                kb, qb, vb = off["kb"][0], off["qb"][0], off["vb"][0]
                if bk is not None:
                    out[g, j * hs:j * hs + d, kb] = bk[c]
                    out[g, :, qb + j * hs:qb + j * hs + d] = bq[c]
                    out[g, :, vb + j * (d + 1):vb + j * (d + 1) + d] = bv[c]
                out[g, j * hs + d, kb] = 1.0
                out[g, :, vb + j * (d + 1) + d] = 1.0
                if hs > d + 1:
                    out[g, :, qb + j * hs + d + 1] = 1.0
        return out

    def words(m):
        return np.ascontiguousarray(m).view(np.int32)

    def both_masks(m):
        m = m.view(np.uint8)
        nk = m.shape[2]
        return (m.reshape(B, QT, P, nk).transpose(0, 2, 1, 3).reshape(B, P, QT * nk),
                m.reshape(B, S, nk // P, P).transpose(0, 3, 2, 1).reshape(B, P, nk // P * S))

    def rope_tables():
        inv = (np.float32(1.0) / np.float32(10000.0) ** (np.arange(0, 16, 2, dtype=np.float32) / np.float32(16))).astype(np.float32)
        freq = (np.arange(S, dtype=np.float32)[:, None] * inv[None, :]).astype(np.float32)
        cos, sin = np.zeros((S, P), np.float32), np.zeros((S, P), np.float32)
        for j in range(4):
            for odd in range(2):
                c = slice(32 * j + odd, 32 * j + 16, 2)
                cos[:, c] = np.cos(freq)
                sin[:, c] = np.sin(freq) if odd else -np.sin(freq)
        return cos, sin

    give("x", rows(a["x"].reshape(B * S, D)))
    ctx = a["ctx_1024"]
    give("ctxT", ctx.reshape(B, SK, DC, P).transpose(0, 3, 2, 1))
    for n, m in zip(("m0q", "m0k"), both_masks(a["mask_BxSxS2_bf0"])):
        give(n, words(m))
    for n, m in zip(("m3q", "m3k"), both_masks(a["mask_BxSxS2_bk1"])):
        give(n, words(m))
    later = np.arange(S)[None, :] > np.arange(S)[:, None]
    for n, m in zip(("causal_q", "causal_k"), both_masks(np.broadcast_to(later, (B, S, S)).copy())):
        give(n, words(m))
    give("m6", a["mask_BxS2_ik1"])
    sel = np.zeros((1, P), np.float32)
    sel[0, 17::32] = 1.0
    give("key_sel", sel)
    cos, sin = rope_tables()
    give("rope_k", np.stack([cos.T, sin.T], 1))
    give("rope_q", np.stack([rows(cos), rows(sin)], 1))

    xw = ("Wk", "Wq", "Wv", "bk", "bq", "bv")
    give("w0", pack(*[a["L0_xattn_" + n] for n in xw], 4, 16))
    give("o0", rows(a["L0_xattn_Wo"]))
    give("ob0", spread(a["L0_xattn_bo"]))
    give("w1", pack(a["L0_attn_kw"], a["L0_attn_qw"], a["L0_attn_vw"], None, None, None, 4, 16, rope=True))
    give("o1", rows(a["L0_attn_ow"]))
    give("w3", pack(*[a["L1_xattn_" + n] for n in xw[:3]], None, None, None, 1, 64))
    give("o3", rows(a["L1_xattn_Wo"]))
    give("ob3", spread(a["L1_xattn_bo"]))
    give("w4", rows(np.concatenate([a["L1_attn_" + n].T for n in ("Wq", "Wk", "Wv")], 1)))
    give("b4", spread(np.concatenate([a["L1_attn_" + n] for n in ("bq", "bk", "bv")])))
    give("o4", rows(a["L1_attn_Wo"].T))
    give("ob4", spread(a["L1_attn_bo"]))
    give("w6", pack(*[a["L2_xattn_" + n] for n in xw[:3]], None, None, None, 4, 16))
    give("o6", rows(a["L2_xattn_Wo"]))
    w = a["L3_attn_in_proj_weight"]
    give("w10", pack(w[D:2 * D].T, w[:D].T, w[2 * D:].T, None, None, None, 4, 16))
    give("o10", rows(a["L3_attn_out_proj_weight"].T))

    def all_experts(routed, shared):
        w = np.concatenate([routed, shared], 0)
        return w.reshape(len(w), -1, P, w.shape[2]).transpose(0, 2, 1, 3)

    give("descending", spread(np.arange(8, 0, -1).astype(np.float32)))
    give("rw2", rows(a["L0_ffn_router_w"]))
    give("rb2", spread(a["L0_ffn_router_b"]))
    give("e1_2", all_experts(a["L0_ffn_w1"], a["L0_ffn_sw1"]))
    give("e2_2", all_experts(a["L0_ffn_w2"], a["L0_ffn_sw2"]))
    give("b1_2", np.concatenate([a["L0_ffn_b1"], a["L0_ffn_sb1"]]).reshape(10, 4, P).transpose(0, 2, 1))
    give("b2_2", np.concatenate([a["L0_ffn_b2"], a["L0_ffn_sb2"]]))
    give("rw5", rows(a["L1_ffn_router_w"].T))
    give("rb5", spread(a["L1_ffn_experts_bias"]))
    give("e1_5", all_experts(a["L1_ffn_w1"], a["L1_ffn_sw1"]))
    give("e3_5", all_experts(a["L1_ffn_w3"], a["L1_ffn_sw3"]))
    give("e2_5", all_experts(a["L1_ffn_w2"], a["L1_ffn_sw2"]))

    for k in ("k0", "k1", "k2"):
        give(k, words(rows(a["L2_ffn_" + k].view(np.uint8))))
    give("signs_scales", spread(np.stack([a["L2_ffn_s0"], a["L2_ffn_s1"], a["L2_ffn_s2"]])))

    give("ctx", ctx.reshape(B, SK // P, P, D).transpose(0, 2, 1, 3))
    give("w9", rows(a["L3_xattn_W"].T))
    r9 = np.stack([a["L3_xattn_b"], a["L3_xattn_gamma"], a["L3_xattn_beta"]])
    give("r9", np.broadcast_to(r9[None], (P, 3, D)))

    give("w11_1", rows(a["L3_ffn_w1"]))
    give("w11_2", rows(a["L3_ffn_w2"]))
    give("b11_1", a["L3_ffn_b1"].reshape(8, P).T)
    give("b11_2", a["L3_ffn_b2"].reshape(DC, P).T)

    m = {k[8:]: v for k, v in a.items() if k.startswith("L2_attn_")}
    tiles = [m[k].reshape(4, P).T for k in ("b_in", "b_gate", "conv_b", "b_delta", "D_skip")]
    taps = m["conv_w"].reshape(4, P, 4).transpose(1, 0, 2)
    give("s_cols", np.concatenate([np.stack(tiles, 2), taps], 2))
    give("s_win", rows(m["W_in"]))
    give("s_wgate", rows(m["W_gate"]))
    give("s_alog", rows(m["A_log"]))
    give("s_wdelta", rows(m["W_delta"]))
    give("s_wbc", rows(np.concatenate([m["W_B"], m["W_C"]], 1)))
    give("s_wout", rows(m["W_out"]))
    give("s_bout", spread(m["b_out"]))

    out = nc.dram_tensor("out_x", (P, NT, D), F32, kind="ExternalOutput").ap()
    build(nc, dram, out)
    r = run(nc, [arrays], core_ids=[0])
    got = r.results[0]["out_x"]
    return got.transpose(1, 0, 2).reshape(B, S, D)
```

```python
import concourse.bass as bass
import numpy as np
from concourse import mybir
from contextlib import ExitStack, contextmanager

LAYERS = (0, 1, 2, 3, 4, 5, 6, 7, 8, 9, 10, 11)

F32 = mybir.dt.float32
BF16 = mybir.dt.bfloat16
F16 = mybir.dt.float16
U8 = mybir.dt.uint8
I32 = mybir.dt.int32
ALU = mybir.AluOpType
ACT = mybir.ActivationFunctionType
AX = mybir.AxisListType

B, S, D = 2, 256, 256
SK = 4096
P = 128
NT = B * S // P
QT = S // P
DC = D // P
MASKED = -1e30
EPS = 1e-5


class Stage:

    number = 0

    def __init__(self, nc):
        self.nc, self.stack, self.sems = nc, ExitStack(), []

    def own(self, name):
        Stage.number += 1
        return f"{name}_{Stage.number}"

    def __enter__(self):
        self.stack.__enter__()
        return self

    def sb(self, name, shape, dt=F32):
        return self.stack.enter_context(self.nc.sbuf_tensor(self.own(name), shape, dt))

    def ps(self, name, shape, dt=F32):
        return self.stack.enter_context(self.nc.psum_tensor(self.own(name), shape, dt))

    def sem(self, name):
        s = self.nc.alloc_semaphore(self.own(name))
        self.sems.append(s)
        return s

    def __exit__(self, *a):
        r = self.stack.__exit__(*a)
        if a[0] is None:
            self.nc.clear_and_free_semaphores(self.sems)
            self.nc.all_engine_barrier()
        return r


def setup_stage(nc, R, x):
    with Stage(nc) as st:
        loaded, zeroed, made = st.sem("x_loaded"), st.sem("ident_zeroed"), st.sem("ident_made")
        with nc.Block() as block:

            @block.sync
            def _(sp):
                sp.dma_start(R.x[:, :, :], x).then_inc(loaded, 16)
                sp.wait_ge(loaded, 16)

            @block.gpsimd
            def _(pool):
                pool.memset(R.identf[:, :], 0.0).then_inc(zeroed, 1)
                pool.memset(R.onesf[:, :], 1.0).then_inc(zeroed, 1)
                pool.wait_ge(zeroed, 2)
                pool.affine_select(out=R.identf[:, :], in_=R.identf[:, :], compare_op=ALU.not_equal, fill=1.0,
                                   base=0, pattern=[[-1, P]], channel_multiplier=1).then_inc(made, 1)

            @block.vector
            def _(dve):
                dve.wait_ge(made, 1)
                dve.tensor_copy(R.identb[:, :], R.identf[:, :]).then_inc(made, 1)


def norm_stage(nc, R):
    with Stage(nc) as st:
        stats = st.sb("stats", [P, NT, 6])
        mv = st.sb("mean_var", [P, NT, 2])
        rstd = st.sb("rstd", [P, NT])
        tp = st.ps("tp", [P, DC, NT * P])
        done = st.sem("dve_step")
        rooted, normed, turned = st.sem("rooted"), st.sem("normed"), st.sem("turned")
        with nc.Block() as block:

            @block.vector
            def _(dve):
                for t in range(NT):
                    dve.bn_stats(stats[:, t, :], R.x[:, t, :]).then_inc(done, 1)
                for t in range(NT):
                    dve.wait_ge(done, t + 1)
                    dve.bn_aggr(mv[:, t, :], stats[:, t, :]).then_inc(done, 1)
                dve.wait_ge(done, 2 * NT)
                dve.tensor_scalar(rstd[:, :], mv[:, :, 1], EPS, None, ALU.add).then_inc(done, 1)
                dve.wait_ge(rooted, 1)
                dve.reciprocal(rstd[:, :], rstd[:, :]).then_inc(done, 1)
                dve.wait_ge(done, 2 * NT + 2)
                for t in range(NT):
                    dve.tensor_scalar(R.xn[:, t, :], R.x[:, t, :], mv[:, t, 0:1], rstd[:, t:t + 1],
                                      ALU.subtract, ALU.mult).then_inc(normed, 1)
                dve.wait_ge(turned, DC * NT)
                dve.tensor_copy(R.xnT[:, 0, :], tp[:, 0, :])

            @block.scalar
            def _(act):
                act.wait_ge(done, 2 * NT + 1)
                act.activation(rstd[:, :], rstd[:, :], ACT.Sqrt).then_inc(rooted, 1)
                act.wait_ge(turned, DC * NT)
                act.activation(R.xnT[:, 1, :], tp[:, 1, :], ACT.Copy)

            @block.tensor
            def _(pe):
                for t in range(NT):
                    pe.wait_ge(normed, t + 1)
                    for c in range(DC):
                        pe.transpose(tp[:, c, t * P:(t + 1) * P], R.xn[:, t, c * P:(c + 1) * P],
                                     R.identf[:, :]).then_inc(turned, 1)


def add_projected_stage(nc, R, src, width, w, brow):
    C = width // P
    with Stage(nc) as st:
        srcT = st.sb("srcT", [P, C, NT * P])
        wt = st.sb("w_out", [P, C, D], w.dtype)
        wf = st.sb("w_out_f", [P, C, D]) if w.dtype != F32 else wt
        bt = st.sb("b_out", [P, D])
        tp = [st.ps("tp", [P, NT * P]) for _ in range(2)]
        acc = [st.ps("acc", [P, D]) for _ in range(2)]
        loaded, widened, turned, kept = st.sem("w_loaded"), st.sem("w_widened"), st.sem("turned"), st.sem("srcT_kept")
        made, added, added_bias = st.sem("product_made"), st.sem("product_added"), st.sem("bias_added")
        n_loads = 2 if brow is not None else 1
        with nc.Block() as block:

            @block.sync
            def _(sp):
                sp.dma_start(wt[:, :, :], w).then_inc(loaded, 16)
                if brow is not None:
                    sp.dma_start(bt[:, :], brow).then_inc(loaded, 16)

            @block.tensor
            def _(pe):
                for c in range(C):
                    if c >= 2:
                        pe.wait_ge(kept, c - 1)
                    for t in range(NT):
                        last = pe.transpose(tp[c % 2][:, t * P:(t + 1) * P], src[:, t, c * P:(c + 1) * P],
                                            R.identf[:, :])
                    last.then_inc(turned, 1)
                pe.wait_ge(kept, C)
                pe.wait_ge(widened, 1)
                for t in range(NT):
                    if t >= 2:
                        pe.wait_ge(added, t - 1)
                    for c in range(C):
                        last = pe.matmul(acc[t % 2][:, :], srcT[:, c, t * P:(t + 1) * P], wf[:, c, :],
                                         start=(c == 0), stop=(c == C - 1))
                    last.then_inc(made, 1)

            @block.scalar
            def _(act):
                for c in range(C):
                    act.wait_ge(turned, c + 1)
                    act.activation(srcT[:, c, :], tp[c % 2][:, :], ACT.Copy).then_inc(kept, 1)

            @block.vector
            def _(dve):
                dve.wait_ge(loaded, 16 * n_loads)
                if w.dtype != F32:
                    dve.tensor_copy(wf[:, :, :], wt[:, :, :]).then_inc(widened, 1)
                else:
                    dve.engine_nop().then_inc(widened, 1)
                if brow is not None:
                    for t in range(NT):
                        dve.tensor_tensor(R.x[:, t, :], R.x[:, t, :], bt[:, :], ALU.add).then_inc(added_bias, 1)
                for t in range(NT):
                    if brow is not None:
                        dve.wait_ge(added_bias, t + 1)
                    dve.wait_ge(made, t + 1)
                    dve.tensor_tensor(R.x[:, t, :], R.x[:, t, :], acc[t % 2][:, :], ALU.add).then_inc(added, 1)


def pack_offsets(hg, d, rope):
    vw = hg * (d + 1)
    names = [("wk", DC * P), ("wq", DC * P), ("wv", DC * vw)]
    if rope:
        names += [("wks", DC * P), ("wqs", DC * P)]
    names += [("kb", 1), ("qb", P), ("vb", vw)]
    at, out = 0, {}
    for n, w in names:
        out[n] = (at, at + w)
        at += w
    return out, at


def attention_stage(nc, R, out_tok, pack, nk, hg, d, scale, ctxT=None, masks=None, key_mask=None, rope=None):
    G = 16 // hg
    VW = hg * (d + 1)
    KR = d + (2 if key_mask is not None else 1)
    HS = P // hg
    KW = min(512, nk)
    KC = nk // KW
    NKT = nk // P
    VP = 4 if nk > 512 else NKT
    VG = NKT // VP
    RW = QT * S if nk == S else 1024
    EK = 4 if nk > 512 else NKT
    EC = NKT // EK
    EU = hg * EC
    SCW = EK * S
    OFF, WF = pack_offsets(hg, d, rope is not None)
    if nk == S:
        units = [(j, [(q, 0, nk, q * nk) for q in range(QT)], 0) for j in range(hg)]
        parts = 1
    else:
        parts = nk // 1024
        units = [(j, [(q, k * 1024 + h * 512, 512, h * 512) for h in range(2)], k)
                 for j in range(hg) for q in range(QT) for k in range(parts)]
    MU = len(units)
    U = KC + VG + 3
    VQ = VG + 3

    with Stage(nc) as st:
        KT = st.sb("KT", [P, nk])
        V = st.sb("V", [P, NKT, VW])
        wt = st.sb("w_pack", [P, WF])
        narrow = pack.dtype != F32
        wl = st.sb("w_pack_half", [P, WF], pack.dtype) if narrow else wt
        qsrc = st.sb("qsrc", [P, DC, S])
        kvsrc = st.sb("ctxT", [P, DC, nk]) if ctxT is not None else qsrc
        qtok = st.sb("q_tok", [P, QT, P])
        QTt = st.sb("QT", [P, S])
        mx = st.sb("max_parts", [P, QT, hg, parts])
        rsum = st.sb("sum_recip", [P, QT, hg])
        PT = [st.sb("probsT", [P, SCW]) for _ in range(3)]
        big = st.ps("scores", [P, 2, 1024])
        pj = st.ps("proj", [P, 2, 512])
        pv = st.ps("weighted", [P, QT, 512])
        if masks is not None:
            m8 = [st.sb("mask_words", [P, QT * nk // 4], I32) for _ in range(2)]
            mq, mk = [st.sb("mask_add", [P, QT * nk], BF16) for _ in range(2)]
        if key_mask is not None:
            km = st.sb("key_mask", [1, nk], I32)
            kadd = st.sb("key_add", [1, nk])
            sel = st.sb("mask_row_sel", [1, P])
        if rope is not None:
            rk = st.sb("rope_k", [P, 2, S])
            rq = st.sb("rope_q", [P, 2, QT, P])
            ra = st.sb("rope_a", [P, S])
            rb = st.sb("rope_b", [P, S])

        def W(n, c=None, w=None):
            a, z = OFF[n]
            return wt[:, a:z] if c is None else wt[:, a + c * w:a + (c + 1) * w]

        w_loaded, b_loaded, const_loaded = st.sem("w_loaded"), st.sem("batch_loaded"), st.sem("const_loaded")
        src_ready, step, widened = st.sem("src_ready"), st.sem("dve_step"), st.sem("w_widened")
        proj_made, k_kept, vq_kept = st.sem("proj_made"), st.sem("keys_kept"), st.sem("vq_kept")
        s_made, s_read, maxed = st.sem("scores_made"), st.sem("scores_read"), st.sem("maxed")
        st_made, exp_done, pv_done = st.sem("scoresT_made"), st.sem("exp_done"), st.sem("weighted_done")
        normed = st.sem("normalised")
        n_b = (1 if ctxT is not None else 0) + (2 if masks is not None else 0) + (1 if key_mask is not None else 0)
        n_const = (1 if key_mask is not None else 0) + (2 if rope is not None else 0)
        SRC = 1 + (2 if masks is not None else 0) + (1 if key_mask is not None else 0)
        STEPS = 1 + (3 if rope is not None else 0)
        if rope is not None:
            STEPS = 5

        with nc.Block() as block:

            @block.gpsimd
            def _(pool):
                if key_mask is not None:
                    pool.dma_start(sel[:, :], key_mask[1]).then_inc(const_loaded, 16)
                if rope is not None:
                    pool.dma_start(rk[:, :, :], rope[0]).then_inc(const_loaded, 16)
                    pool.dma_start(rq[:, :, :, :], rope[1]).then_inc(const_loaded, 16)
                with pool.Fori(0, B) as b:
                    if n_b:
                        pool.wait_ge(pv_done, b * (G * EU) + 1)
                        pool.wait_ge(src_ready, b * SRC + 1)
                    if ctxT is not None:
                        pool.dma_start(kvsrc[:, :, :], ctxT[bass.ds(b, 1)].rearrange("o p c k -> (o p) c k"))\
                          .then_inc(b_loaded, 16)
                    if masks is not None:
                        for n in range(2):
                            pool.dma_start(m8[n][:, :], masks[n][bass.ds(b, 1)].rearrange("o p k -> (o p) k"))\
                              .then_inc(b_loaded, 16)
                    if key_mask is not None:
                        pool.dma_start(km[:, :], key_mask[0][bass.ds(b, 1), :]).then_inc(b_loaded, 16)
                    with pool.Fori(0, G) as g:
                        pool.wait_ge(maxed, b * G + g + 1)
                        pool.dma_start(wl[:, :], pack[bass.ds(g, 1)].rearrange("o p w -> (o p) w"))\
                          .then_inc(w_loaded, 16)

            @block.tensor
            def _(pe):
                pe.sem_inc(pv_done, 1)
                if n_const:
                    pe.wait_ge(const_loaded, 16 * n_const)
                with pe.Fori(0, B) as b:
                    with pe.Fori(0, G) as g:
                        it = b * G + g
                        if n_b:
                            pe.wait_ge(b_loaded, b * (16 * n_b) + 16 * n_b)
                        pe.wait_ge(src_ready, b * SRC + SRC + 1)
                        if narrow:
                            pe.wait_ge(widened, it + 1)
                        else:
                            pe.wait_ge(w_loaded, it * 16 + 16)

                        def buffer_free(n):
                            if n < 2:
                                return
                            if n - 2 < KC:
                                pe.wait_ge(k_kept, it * KC + (n - 1))
                            else:
                                pe.wait_ge(vq_kept, it * VQ + (n - 1 - KC))

                        for n in range(KC):
                            buffer_free(n)
                            o = pj[:, n % 2, 0:KW]
                            for c in range(DC):
                                last = pe.matmul(o, W("wk", c, P), kvsrc[:, c, n * KW:(n + 1) * KW],
                                                 start=(c == 0), stop=(c == DC - 1 and key_mask is None))
                            if key_mask is not None:
                                last = pe.matmul(o, sel[:, :], kadd[:, n * KW:(n + 1) * KW], start=False, stop=True)
                            if rope is not None:
                                for c in range(DC):
                                    last = pe.matmul(pj[:, n % 2, S:2 * S], W("wks", c, P), kvsrc[:, c, :],
                                                     start=(c == 0), stop=(c == DC - 1))
                            last.then_inc(proj_made, 1)
                        for v in range(VG):
                            n = KC + v
                            buffer_free(n)
                            for i in range(VP):
                                k0 = (v * VP + i) * P
                                for c in range(DC):
                                    last = pe.matmul(pj[:, n % 2, i * VW:(i + 1) * VW], kvsrc[:, c, k0:k0 + P],
                                                     W("wv", c, VW), start=(c == 0), stop=(c == DC - 1))
                            last.then_inc(proj_made, 1)
                        n = KC + VG
                        buffer_free(n)
                        for q in range(QT):
                            for r, name in enumerate(["wq"] + ["wqs"] * (rope is not None)):
                                o = r * S + q * P
                                for c in range(DC):
                                    last = pe.matmul(pj[:, n % 2, o:o + P], qsrc[:, c, q * P:(q + 1) * P],
                                                     W(name, c, P), start=(c == 0), stop=(c == DC - 1))
                        last.then_inc(proj_made, 1)

                        def turn_queries(n):
                            pe.wait_ge(vq_kept, it * VQ + VG + (n - KC - VG))
                            for q in range(QT):
                                last = pe.transpose(pj[:, n % 2, q * P:(q + 1) * P], qtok[:, q, :], R.identf[:, :])
                            last.then_inc(proj_made, 1)

                        turn_queries(KC + VG + 1)
                        pe.wait_ge(k_kept, it * KC + KC)
                        pe.wait_ge(vq_kept, it * VQ + VG + 2)
                        pe.wait_ge(exp_done, it * EU + 1)
                        for u, (j, cells, _) in enumerate(units):
                            if u >= 2:
                                pe.wait_ge(s_read, it * MU + (u - 1))
                            for q, k0, w, o in cells:
                                out = big[:, u % 2, o:o + w]
                                if masks is not None:
                                    pe.matmul(out, R.identb[:, :], mq[:, q * nk + k0:q * nk + k0 + w],
                                              start=True, stop=False)
                                last = pe.matmul(out, QTt[j * HS:j * HS + KR, q * P:(q + 1) * P],
                                                 KT[j * HS:j * HS + KR, k0:k0 + w],
                                                 start=(masks is None), stop=True)
                            last.then_inc(s_made, 1)
                        pe.wait_ge(maxed, it + 1 + 1)
                        turn_queries(KC + VG + 2)
                        pe.wait_ge(vq_kept, it * VQ + VQ)

                        def weigh(e):
                            j, e0 = e // EC, e % EC
                            pe.wait_ge(exp_done, it * EU + (e + 1) + 1)
                            if e == 0:
                                pe.wait_ge(normed, it + 1)
                            for i in range(EK):
                                kt = e0 * EK + i
                                for q in range(QT):
                                    last = pe.matmul(pv[:, q, j * (d + 1):(j + 1) * (d + 1)],
                                                     PT[e % 3][:, i * S + q * P:i * S + (q + 1) * P],
                                                     V[:, kt, j * (d + 1):(j + 1) * (d + 1)],
                                                     start=(kt == 0), stop=(kt == NKT - 1))
                            last.then_inc(pv_done, 1)

                        for e in range(EU):
                            j, e0 = e // EC, e % EC
                            if e >= 2:
                                pe.wait_ge(exp_done, it * EU + (e - 1) + 1)
                            for h in range(EK // 2):
                                bank = big[:, e % 2, h * 512:(h + 1) * 512]
                                if masks is not None:
                                    k0 = (e0 * EK + 2 * h) * S
                                    pe.matmul(bank, R.identb[:, :], mk[:, k0:k0 + 512], start=True, stop=False)
                                for i in range(2):
                                    kt = e0 * EK + 2 * h + i
                                    last = pe.matmul(bank[:, i * S:(i + 1) * S],
                                                     KT[j * HS:j * HS + KR, kt * P:(kt + 1) * P],
                                                     QTt[j * HS:j * HS + KR, :],
                                                     start=(masks is None), stop=(masks is None or i == 1))
                            last.then_inc(st_made, 1)
                            if e >= 1:
                                weigh(e - 1)
                        weigh(EU - 1)

            @block.scalar
            def _(act):
                act.sem_inc(exp_done, 1)
                with act.Fori(0, B) as b:
                    with act.Fori(0, G) as g:
                        it = b * G + g
                        if rope is None:
                            for n in range(KC):
                                act.wait_ge(proj_made, it * U + (n + 1))
                                act.activation(KT[:, n * KW:(n + 1) * KW], pj[:, n % 2, 0:KW], ACT.Identity,
                                               bias=W("kb")).then_inc(k_kept, 1)
                        for e in range(EU):
                            act.wait_ge(st_made, it * EU + (e + 1))
                            if e < 3:
                                act.wait_ge(pv_done, it * EU + 1)
                            else:
                                act.wait_ge(pv_done, it * EU + (e - 2) + 1)
                            act.activation(PT[e % 3][:, :], big[:, e % 2, 0:SCW], ACT.Exp, scale=scale)\
                               .then_inc(exp_done, 1)

            @block.vector
            def _(dve):
                dve.sem_inc(src_ready, 1)
                dve.sem_inc(step, 1)
                dve.sem_inc(maxed, 1)
                dve.sem_inc(normed, 1)
                if n_const:
                    dve.wait_ge(const_loaded, 16 * n_const)
                with dve.Fori(0, B) as b:
                    dve.wait_ge(pv_done, b * (G * EU) + 1)
                    dve.tensor_copy(qsrc[:, :, :], R.xnT[:, :, bass.ds(b * S, S)]).then_inc(src_ready, 1)
                    if n_b:
                        dve.wait_ge(b_loaded, b * (16 * n_b) + 16 * n_b)
                    if masks is not None:
                        for src8, add in zip(m8, (mq, mk)):
                            dve.tensor_scalar(add[:, :], src8[:, :].bitcast(U8), MASKED, None, ALU.mult).then_inc(src_ready, 1)
                    if key_mask is not None:
                        dve.tensor_scalar(kadd[:, :], km[:, :], 0.0, MASKED, ALU.is_equal, ALU.mult)\
                           .then_inc(src_ready, 1)
                    with dve.Fori(0, G) as g:
                        it = b * G + g
                        if narrow:
                            dve.wait_ge(w_loaded, it * 16 + 16)
                            dve.tensor_copy(wt[:, :], wl[:, :]).then_inc(widened, 1)
                            dve.wait_ge(widened, it + 1)
                        if rope is not None:
                            dve.wait_ge(proj_made, it * U + 1)
                            dve.wait_ge(step, it * STEPS + 1)
                            dve.tensor_tensor(ra[:, :], pj[:, 0, 0:S], rk[:, 0, :], ALU.mult).then_inc(step, 1)
                            dve.tensor_tensor(rb[:, :], pj[:, 0, S:2 * S], rk[:, 1, :], ALU.mult).then_inc(step, 1)
                            dve.wait_ge(step, it * STEPS + 2 + 1)
                            dve.scalar_tensor_tensor(out=KT[:, :], in0=ra[:, :], scalar=W("kb"), in1=rb[:, :],
                                                     op0=ALU.add, op1=ALU.add).then_inc(k_kept, 1)
                        for v in range(VG):
                            n = KC + v
                            dve.wait_ge(proj_made, it * U + (n + 1))
                            dve.tensor_tensor(V[:, v * VP:(v + 1) * VP, :],
                                              pj[:, n % 2, 0:VP * VW].rearrange("p (k w) -> p k w", k=VP),
                                              W("vb").unsqueeze(1).broadcast_to([P, VP, VW]), ALU.add)\
                               .then_inc(vq_kept, 1)
                        n = KC + VG
                        dve.wait_ge(proj_made, it * U + (n + 1))
                        if rope is None:
                            dve.tensor_tensor(qtok[:, :, :],
                                              pj[:, n % 2, 0:S].rearrange("p (q w) -> p q w", q=QT),
                                              W("qb").unsqueeze(1).broadcast_to([P, QT, P]), ALU.add)\
                               .then_inc(vq_kept, 1)
                        else:
                            dve.wait_ge(k_kept, it + 1)
                            dve.tensor_tensor(ra[:, :], pj[:, n % 2, 0:S],
                                              rq[:, 0, :, :].rearrange("p q w -> p (q w)"), ALU.mult).then_inc(step, 1)
                            dve.tensor_tensor(rb[:, :], pj[:, n % 2, S:2 * S],
                                              rq[:, 1, :, :].rearrange("p q w -> p (q w)"), ALU.mult).then_inc(step, 1)
                            dve.wait_ge(step, it * STEPS + 4 + 1)
                            dve.tensor_tensor(qtok[:, :, :].rearrange("p q w -> p (q w)"), ra[:, :], rb[:, :],
                                              ALU.add).then_inc(vq_kept, 1)
                        n += 1
                        dve.wait_ge(proj_made, it * U + (n + 1))
                        dve.tensor_copy(QTt[:, :], pj[:, n % 2, 0:S]).then_inc(vq_kept, 1)
                        for u, (j, cells, part) in enumerate(units):
                            dve.wait_ge(s_made, it * MU + (u + 1))
                            if nk == S:
                                dve.tensor_reduce(mx[:, :, j, 0], big[:, u % 2, 0:RW].rearrange(
                                    "p (q k) -> p q k", q=QT), AX.X, ALU.max).then_inc(s_read, 1)
                            else:
                                dve.tensor_reduce(mx[:, cells[0][0], j, part:part + 1], big[:, u % 2, 0:RW],
                                                  AX.X, ALU.max).then_inc(s_read, 1)
                        dve.wait_ge(s_read, it * MU + MU)
                        dve.tensor_reduce(qtok[:, :, :].rearrange("p q (j s) -> p q j s", j=hg)[:, :, :, d],
                                          mx[:, :, :, :], AX.X, ALU.max, negate=True).then_inc(maxed, 1)
                        n += 1
                        dve.wait_ge(proj_made, it * U + (n + 1))
                        dve.tensor_copy(QTt[:, :], pj[:, n % 2, 0:S]).then_inc(vq_kept, 1)
                        dve.wait_ge(pv_done, it * EU + EU + 1)
                        pvv = pv[:, :, 0:VW].rearrange("p q (j w) -> p q j w", j=hg)
                        dve.wait_ge(normed, it + 1)
                        dve.reciprocal(rsum[:, :, :], pvv[:, :, :, d]).then_inc(step, 1)
                        dve.wait_ge(step, it * STEPS + STEPS + 1)
                        for q in range(QT):
                            o = out_tok[:, bass.ds(b * QT + q, 1), bass.ds(g * (hg * d), hg * d)]
                            ins = dve.tensor_tensor(o.rearrange("p o (j w) -> p (o j) w", j=hg),
                                                    pvv[:, q, :, 0:d],
                                                    rsum[:, q, :].unsqueeze(2).broadcast_to([P, hg, d]), ALU.mult)
                        ins.then_inc(normed, 1)


def head_mix_stage(nc, R, dram, scratch):
    H, d = 16, 16
    with Stage(nc) as st:
        w = st.sb("w_qkv", [P, DC, 3 * D])
        bias = st.sb("b_qkv", [P, 3 * D])
        qkv = [st.sb("qkv", [P, 3 * D]) for _ in range(2)]
        prod = st.sb("products", [P, H, H, d])
        sc = st.sb("scores", [P, H, H])
        ex = st.sb("exps", [P, H, H])
        mx, sm = st.sb("max", [P, H]), st.sb("sum", [P, H])
        o = [st.sb("mixed", [P, H, d]) for _ in range(2)]
        ps = [st.ps("qkv_ps", [P, 2, 512]) for _ in range(2)]
        loaded, made, kept, step = st.sem("w_loaded"), st.sem("qkv_made"), st.sem("qkv_kept"), st.sem("dve_step")
        shifted, exped, mixed = st.sem("shifted"), st.sem("exp_done"), st.sem("mixed")
        stored = [st.sem("stored") for _ in range(2)]
        with nc.Block() as block:

            @block.sync
            def _(sp):
                sp.dma_start(w[:, :, :], dram["w4"]).then_inc(loaded, 16)
                sp.dma_start(bias[:, :], dram["b4"]).then_inc(loaded, 16)
                for t in range(NT):
                    b, q = t // QT, t % QT
                    sp.wait_ge(mixed, t + 1)
                    sp.dma_start(scratch[b, :, q * P:(q + 1) * P, :].rearrange("h s d -> s h d"),
                                 o[t % 2][:, :, :]).then_inc(stored[t % 2], 16)
                for s in stored:
                    sp.wait_ge(s, 16 * NT // 2)

            @block.tensor
            def _(pe):
                pe.wait_ge(loaded, 32)
                for t in range(NT):
                    if t >= 2:
                        pe.wait_ge(kept, t - 1)
                    for h, (c0, c1) in enumerate(((0, 512), (512, 768))):
                        for c in range(DC):
                            last = pe.matmul(ps[t % 2][:, h, 0:c1 - c0], R.xnT[:, c, t * P:(t + 1) * P],
                                             w[:, c, c0:c1], start=(c == 0), stop=(c == DC - 1))
                    last.then_inc(made, 1)

            @block.scalar
            def _(act):
                for t in range(NT):
                    act.wait_ge(shifted, t + 1)
                    act.activation(ex[:, :, :], sc[:, :, :], ACT.Exp, scale=0.25).then_inc(exped, 1)

            @block.vector
            def _(dve):
                dve.wait_ge(loaded, 32)
                n = 0
                for t in range(NT):
                    a = qkv[t % 2]
                    dve.wait_ge(made, t + 1)
                    flat = ps[t % 2][:, :, :].rearrange("p a b -> p (a b)")[:, 0:3 * D]
                    dve.tensor_tensor(a[:, :], flat, bias[:, :], ALU.add).then_inc(kept, 1)
                    q, k, v = (a[:, i * D:(i + 1) * D].rearrange("p (h d) -> p h d", h=H) for i in range(3))
                    dve.wait_ge(kept, t + 1)
                    dve.tensor_tensor(prod[:, :, :, :], q.unsqueeze(2).broadcast_to([P, H, H, d]),
                                      k.unsqueeze(1).broadcast_to([P, H, H, d]), ALU.mult).then_inc(step, 1)
                    dve.wait_ge(step, n + 1)
                    dve.tensor_reduce(sc[:, :, :], prod[:, :, :, :], AX.X, ALU.add).then_inc(step, 1)
                    dve.wait_ge(step, n + 2)
                    dve.tensor_reduce(mx[:, :], sc[:, :, :], AX.X, ALU.max).then_inc(step, 1)
                    dve.wait_ge(step, n + 3)
                    dve.tensor_tensor(sc[:, :, :], sc[:, :, :], mx[:, :].unsqueeze(2).broadcast_to([P, H, H]),
                                      ALU.subtract).then_inc(shifted, 1)
                    dve.wait_ge(exped, t + 1)
                    dve.tensor_reduce(sm[:, :], ex[:, :, :], AX.X, ALU.add).then_inc(step, 1)
                    dve.tensor_tensor(prod[:, :, :, :], ex[:, :, :].unsqueeze(2).broadcast_to([P, H, d, H]),
                                      v.rearrange("p h d -> p d h").unsqueeze(1).broadcast_to([P, H, d, H]),
                                      ALU.mult).then_inc(step, 1)
                    dve.wait_ge(step, n + 5)
                    dve.reciprocal(sm[:, :], sm[:, :]).then_inc(step, 1)
                    if t >= 2:
                        dve.wait_ge(stored[t % 2], 16 * (t // 2))
                    dve.tensor_reduce(o[t % 2][:, :, :], prod[:, :, :, :], AX.X, ALU.add).then_inc(step, 1)
                    n += 7
                    dve.wait_ge(step, n)
                    dve.tensor_tensor(o[t % 2][:, :, :], o[t % 2][:, :, :],
                                      sm[:, :].unsqueeze(2).broadcast_to([P, H, d]), ALU.mult).then_inc(mixed, 1)


def reload_stage(nc, att, scratch):
    with Stage(nc) as st:
        loaded = st.sem("reloaded")
        with nc.Block() as block:

            @block.sync
            def _(sp):
                flat = scratch.rearrange("b h s d -> (b h s d)").rearrange("(t p m) -> p t m", p=P, m=D)
                sp.dma_start(att[:, :, :], flat).then_inc(loaded, 16)
                sp.wait_ge(loaded, 16)


def experts_stage(nc, R, dram, layer, E, func, shared_weight):
    NE, HT = 8, 4
    gated = layer == 5
    rw_d, rb_d = dram[f"rw{layer}"], dram[f"rb{layer}"]
    w1_d, w2_d = dram[f"e1_{layer}"], dram[f"e2_{layer}"]
    with Stage(nc) as st:
        rw, rb, desc = st.sb("router_w", [P, DC, NE]), st.sb("router_b", [P, NE]), st.sb("descending", [P, NE])
        lg, l2, tmp = st.sb("logits", [P, NT, NE]), st.sb("logits2", [P, NT, NE]), st.sb("tie", [P, NT, NE])
        one = [st.sb("one_hot", [P, NT, NE]) for _ in range(2)]
        top = [st.sb("top", [P, NT]) for _ in range(2)]
        tie = st.sb("tie_max", [P, NT])
        pr = [st.sb("prob", [P, NT]) for _ in range(2)]
        comb = st.sb("weights", [P, NT, E])
        cur = [st.sb("weight_now", [P, NT]) for _ in range(2)]
        w1, w2 = st.sb("w1", [P, DC, HT * P]), st.sb("w2", [P, HT, D])
        w3 = st.sb("w3", [P, DC, HT * P]) if gated else None
        b1 = None if gated else st.sb("b1", [P, HT])
        hs = [st.sb("h_silu", [P, NT * P]) for _ in range(2)] if gated else None
        hT = st.sb("hT", [P, HT, NT * P])
        h_ps = [st.ps("h_ps", [P, NT * P]) for _ in range(2)]
        u_ps = [st.ps("u_ps", [P, NT * P]) for _ in range(2)] if gated else None
        y_ps = [st.ps("y_ps", [P, 512]) for _ in range(2)]
        r_ps = st.ps("router_ps", [P, NT, NE])
        if not gated:
            b2, combT = st.sb("b2", [E, D]), st.sb("weightsT", [E, NT * P])
            c_ps = st.ps("weightsT_ps", [E, NT * P])
        r_loaded, routed, step, e2s = st.sem("router_loaded"), st.sem("routed"), st.sem("dve_step"), st.sem("exp_done")
        turned, bias_made = st.sem("turned"), st.sem("bias_made")
        w1_loaded, w2_loaded = st.sem("w1_loaded"), st.sem("w2_loaded")
        h_made, silu_done, h_kept = st.sem("h_made"), st.sem("silu_done"), st.sem("h_kept")
        y_made, y_added, cur_ready = st.sem("y_made"), st.sem("y_added"), st.sem("weight_ready")
        own = st.sem("routing_step")
        NL1 = 2
        NR = 3 if gated else 4
        YB = 0 if gated else NT

        with nc.Block() as block:

            @block.sync
            def _(sp):
                sp.dma_start(rw[:, :, :], rw_d).then_inc(r_loaded, 16)
                sp.dma_start(rb[:, :], rb_d).then_inc(r_loaded, 16)
                sp.dma_start(desc[:, :], dram["descending"]).then_inc(r_loaded, 16)
                if not gated:
                    sp.dma_start(b2[:, :], dram["b2_2"]).then_inc(r_loaded, 16)

            @block.gpsimd
            def _(pool):
                with pool.Fori(0, E) as e:
                    pool.wait_ge(h_kept, e * HT + 1)
                    pool.dma_start(w1[:, :, :], w1_d[bass.ds(e, 1)].rearrange("o p c h -> (o p) c h"))\
                        .then_inc(w1_loaded, 16)
                    if gated:
                        pool.dma_start(w3[:, :, :], dram["e3_5"][bass.ds(e, 1)].rearrange("o p c h -> (o p) c h"))\
                            .then_inc(w1_loaded, 16)
                    else:
                        pool.dma_start(b1[:, :], dram["b1_2"][bass.ds(e, 1)].rearrange("o p h -> (o p) h"))\
                            .then_inc(w1_loaded, 16)

            @block.tensor
            def _(pe):
                pe.sem_inc(y_made, 1)
                pe.wait_ge(r_loaded, 16 * NR)
                for t in range(NT):
                    for c in range(DC):
                        last = pe.matmul(r_ps[:, t, :], R.xnT[:, c, t * P:(t + 1) * P], rw[:, c, :],
                                         start=(c == 0), stop=(c == DC - 1))
                last.then_inc(turned, 1)
                if not gated:
                    pe.wait_ge(routed, 1)
                    for t in range(NT):
                        last = pe.transpose(c_ps[:, t * P:(t + 1) * P], comb[:, t, :], R.identf[:, :])
                    last.then_inc(turned, 1)
                    pe.wait_ge(bias_made, 1)
                    for t in range(NT):
                        if t >= 2:
                            pe.wait_ge(y_added, t)
                        pe.matmul(y_ps[t % 2][:, 0:D], combT[:, t * P:(t + 1) * P], b2[:, :],
                                  start=True, stop=True).then_inc(turned, 1)
                with pe.Fori(0, E) as e:
                    pe.wait_ge(w1_loaded, e * (16 * NL1) + 16 * NL1)
                    for f in range(HT):
                        if f >= 2:
                            pe.wait_ge(h_kept, e * HT + f)
                        else:
                            pe.wait_ge(h_kept, e * HT + 1)
                        for w, ps in ((w1, h_ps), (w3, u_ps)):
                            if w is not None:
                                for c in range(DC):
                                    last = pe.matmul(ps[f % 2][:, :], w[:, c, f * P:(f + 1) * P], R.xnT[:, c, :],
                                                     start=(c == 0), stop=(c == DC - 1))
                        last.then_inc(h_made, 1)
                    pe.wait_ge(h_kept, e * HT + HT + 1)
                    pe.wait_ge(w2_loaded, e * 16 + 16)
                    for t in range(NT):
                        pe.wait_ge(y_added, e * NT + (YB + 1 + max(t - 1, 0)))
                        for f in range(HT):
                            last = pe.matmul(y_ps[t % 2][:, 0:D], hT[:, f, t * P:(t + 1) * P], w2[:, f, :],
                                             start=(f == 0), stop=(f == HT - 1))
                        last.then_inc(y_made, 1)

            @block.scalar
            def _(act):
                act.wait_ge(step, 1)
                act.activation(pr[1][:, :], pr[1][:, :], ACT.Exp).then_inc(e2s, 1)
                if not gated:
                    act.sem_inc(h_kept, 1)
                    act.wait_ge(turned, 2)
                    act.activation(combT[:, :], c_ps[:, :], ACT.Copy).then_inc(bias_made, 1)
                with act.Fori(0, E) as e:
                    act.wait_ge(y_made, e * NT + 1)
                    act.dma_start(w2[:, :, :], w2_d[bass.ds(e, 1)].rearrange("o p h m -> (o p) h m"))\
                       .then_inc(w2_loaded, 16)
                    for f in range(HT):
                        act.wait_ge(h_made, e * HT + (f + 1))
                        if gated:
                            act.wait_ge(h_kept, e * HT + max(f - 1, 0) + 1)
                            act.activation(hs[f % 2][:, :], h_ps[f % 2][:, :], func).then_inc(silu_done, 1)
                        else:
                            act.wait_ge(y_made, e * NT + 1)
                            act.activation(hT[:, f, :], h_ps[f % 2][:, :], func, bias=b1[:, f:f + 1])\
                               .then_inc(h_kept, 1)

            @block.vector
            def _(dve):
                dve.sem_inc(y_added, 1)
                dve.sem_inc(cur_ready, 1)
                if gated:
                    dve.sem_inc(h_kept, 1)

                def over(v):
                    return v[:, :].unsqueeze(2).broadcast_to([P, NT, NE])

                def row(v):
                    return v[:, :].unsqueeze(1).broadcast_to([P, NT, NE])

                n = 0
                dve.wait_ge(r_loaded, 16 * NR)
                dve.wait_ge(turned, 1)
                dve.tensor_tensor(lg[:, :, :], r_ps[:, :, :], row(rb), ALU.add).then_inc(own, 1)
                for k, src in enumerate((lg, l2)):
                    n += 1
                    dve.wait_ge(own, n)
                    dve.tensor_reduce(top[k][:, :], src[:, :, :], AX.X, ALU.max).then_inc(own, 1)
                    n += 1
                    dve.wait_ge(own, n)
                    dve.tensor_tensor(tmp[:, :, :], src[:, :, :], over(top[k]), ALU.is_equal).then_inc(own, 1)
                    n += 1
                    dve.wait_ge(own, n)
                    dve.tensor_tensor(tmp[:, :, :], tmp[:, :, :], row(desc), ALU.mult).then_inc(own, 1)
                    n += 1
                    dve.wait_ge(own, n)
                    dve.tensor_reduce(tie[:, :], tmp[:, :, :], AX.X, ALU.max).then_inc(own, 1)
                    n += 1
                    dve.wait_ge(own, n)
                    dve.tensor_tensor(one[k][:, :, :], tmp[:, :, :], over(tie), ALU.is_equal).then_inc(own, 1)
                    if k == 0:
                        n += 1
                        dve.wait_ge(own, n)
                        dve.scalar_tensor_tensor(out=l2[:, :, :].rearrange("p t e -> p (t e)"),
                                                 in0=one[0][:, :, :].rearrange("p t e -> p (t e)"), scalar=MASKED,
                                                 in1=lg[:, :, :].rearrange("p t e -> p (t e)"),
                                                 op0=ALU.mult, op1=ALU.add).then_inc(own, 1)
                dve.tensor_tensor(pr[1][:, :], top[1][:, :], top[0][:, :], ALU.subtract).then_inc(step, 1)
                dve.wait_ge(e2s, 1)
                dve.tensor_scalar(pr[0][:, :], pr[1][:, :], 1.0, None, ALU.add).then_inc(own, 1)
                n += 2
                dve.wait_ge(own, n)
                dve.reciprocal(pr[0][:, :], pr[0][:, :]).then_inc(own, 1)
                n += 1
                dve.wait_ge(own, n)
                dve.tensor_tensor(pr[1][:, :], pr[1][:, :], pr[0][:, :], ALU.mult).then_inc(own, 1)
                dve.tensor_tensor(one[0][:, :, :], one[0][:, :, :], over(pr[0]), ALU.mult).then_inc(own, 1)
                n += 2
                dve.wait_ge(own, n)
                dve.tensor_tensor(one[1][:, :, :], one[1][:, :, :], over(pr[1]), ALU.mult).then_inc(own, 1)
                dve.memset(comb[:, :, NE:E], shared_weight).then_inc(own, 1)
                n += 2
                dve.wait_ge(own, n)
                dve.tensor_tensor(comb[:, :, 0:NE], one[0][:, :, :], one[1][:, :, :], ALU.add).then_inc(routed, 1)
                if not gated:
                    for t in range(NT):
                        dve.wait_ge(turned, 3 + t)
                        dve.tensor_tensor(R.x[:, t, :], R.x[:, t, :], y_ps[t % 2][:, 0:D], ALU.add)\
                           .then_inc(y_added, 1)
                dve.wait_ge(routed, 1)
                with dve.Fori(0, E) as e:
                    if gated:
                        for f in range(HT):
                            dve.wait_ge(silu_done, e * HT + (f + 1))
                            dve.tensor_tensor(hT[:, f, :], hs[f % 2][:, :], u_ps[f % 2][:, :], ALU.mult)\
                               .then_inc(h_kept, 1)
                    dve.wait_ge(y_added, e * NT + (YB + 1))
                    dve.tensor_copy(cur[0][:, :], comb[:, :, bass.ds(e, 1)].rearrange("p t o -> p (t o)"))\
                       .then_inc(cur_ready, 1)
                    dve.wait_ge(cur_ready, e + 2)
                    for t in range(NT):
                        dve.wait_ge(y_made, e * NT + (t + 2))
                        dve.scalar_tensor_tensor(out=R.x[:, t, :], in0=y_ps[t % 2][:, 0:D], scalar=cur[0][:, t:t + 1],
                                                 in1=R.x[:, t, :], op0=ALU.mult, op1=ALU.add).then_inc(y_added, 1)


def signs_stage(nc, R, dram):
    HT = 8
    with Stage(nc) as st:
        k0 = st.sb("k0_words", [P, 2 * DC, HT * P // 4], I32)
        k1 = st.sb("k1_words", [P, HT, HT * P // 4], I32)
        k2 = st.sb("k2_words", [P, HT, D // 4], I32)
        w0 = st.sb("w0", [P, DC, HT * P])
        w1 = st.sb("w1", [P, HT, HT * P])
        w2 = st.sb("w2", [P, HT, D])
        sc = st.sb("scales", [P, 3])
        h1, h2 = st.sb("h1T", [P, HT, NT * P]), st.sb("h2T", [P, HT, NT * P])
        ps = [st.ps("h_ps", [P, NT * P]) for _ in range(4)]
        y_ps = [st.ps("y_ps", [P, 512]) for _ in range(2)]
        loaded, widened, made, kept = st.sem("loaded"), st.sem("widened"), st.sem("h_made"), st.sem("h_kept")
        y_made, y_added, differed = st.sem("y_made"), st.sem("y_added"), st.sem("differed")
        with nc.Block() as block:

            @block.sync
            def _(sp):
                sp.dma_start(k0[:, :, :], dram["k0"]).then_inc(loaded, 16)
                sp.dma_start(sc[:, :], dram["signs_scales"]).then_inc(loaded, 16)
                sp.dma_start(k1[:, :, :], dram["k1"]).then_inc(loaded, 16)
                sp.dma_start(k2[:, :, :], dram["k2"]).then_inc(loaded, 16)

            @block.vector
            def _(dve):
                dve.wait_ge(loaded, 64)
                a = k0[:, :, :].bitcast(U8)
                dve.tensor_tensor(w0[:, :, :], a[:, 0:DC, :], a[:, DC:2 * DC, :], ALU.subtract).then_inc(differed, 1)
                dve.wait_ge(differed, 1)
                dve.tensor_scalar(w0[:, :, :], w0[:, :, :], 4.0, None, ALU.mult).then_inc(widened, 1)
                dve.tensor_scalar(w1[:, :, :], k1[:, :, :].bitcast(U8), 4.0, -2.0, ALU.mult, ALU.add)\
                   .then_inc(widened, 1)
                dve.tensor_scalar(w2[:, :, :], k2[:, :, :].bitcast(U8), 2.0, -1.0, ALU.mult, ALU.add)\
                   .then_inc(widened, 1)
                for t in range(NT):
                    dve.wait_ge(y_made, t + 1)
                    dve.scalar_tensor_tensor(out=R.x[:, t, :], in0=y_ps[t % 2][:, 0:D], scalar=sc[:, 2:3],
                                             in1=R.x[:, t, :], op0=ALU.mult, op1=ALU.add).then_inc(y_added, 1)

            @block.tensor
            def _(pe):
                n = 0
                for w, src, C, ready in ((w0, R.xnT, DC, 1), (w1, h1, HT, 2)):
                    pe.wait_ge(widened, ready)
                    for f in range(HT):
                        if n >= 4:
                            pe.wait_ge(kept, n - 3)
                        if C == HT and f == 0:
                            pe.wait_ge(kept, HT)
                        for c in range(C):
                            last = pe.matmul(ps[n % 4][:, :], w[:, c, f * P:(f + 1) * P], src[:, c, :],
                                             start=(c == 0), stop=(c == C - 1))
                        last.then_inc(made, 1)
                        n += 1
                pe.wait_ge(widened, 3)
                pe.wait_ge(kept, 2 * HT)
                for t in range(NT):
                    if t >= 2:
                        pe.wait_ge(y_added, t - 1)
                    for c in range(HT):
                        last = pe.matmul(y_ps[t % 2][:, 0:D], h2[:, c, t * P:(t + 1) * P], w2[:, c, :],
                                         start=(c == 0), stop=(c == HT - 1))
                    last.then_inc(y_made, 1)

            @block.scalar
            def _(act):
                act.wait_ge(loaded, 64)
                for n in range(2 * HT):
                    act.wait_ge(made, n + 1)
                    h = h1 if n < HT else h2
                    act.activation(h[:, n % HT, :], ps[n % 4][:, :], ACT.Relu,
                                   scale=sc[:, n // HT:n // HT + 1]).then_inc(kept, 1)


def split_context_stage(nc, R, att, w, scale, ctxT, parts_d, masks=None, key_mask=None):
    H, d = 16, 16
    VW = d + 1
    XR, M0, MASKROW = 100, 96, 99
    NKT, KC = SK // P, SK // 512
    HG = D // P
    EU, EK = 8, 4
    MU = QT * KC
    NX = 4
    TURNS = H // NX
    PAIRS = ((0, 0), (0, 1), (0, 2), (1, 0), (1, 1), (2, 0))
    WHEN = (3, 3, 2, 2, 2, 2, 2, 0)
    PRO = HG * KC + NKT + QT
    CLEARED = 2 + NX + 1 + (key_mask is not None)
    with Stage(nc) as st:
        cx = st.sb("ctxT", [P, DC, SK])
        ws = st.sb("w_kqv", [P, DC, D + D + H * VW])
        bs = st.sb("biases", [P, HG + D + H * VW])
        qsrc = st.sb("qsrc", [P, DC, S])
        kst = st.sb("key_parts", [P, 3, SK], BF16)
        kr = [st.sb("key_rest", [P, 512]) for _ in range(2)]
        V = st.sb("V", [P, NKT, H, VW])
        qf, qr = (cx[:, 1, i * QT * D:(i + 1) * QT * D].rearrange("p (q f) -> p q f", q=QT) for i in range(2))
        Q = st.sb("Q_all", [P, QT, H, P], BF16)
        X = [st.sb("X", [XR, SK], BF16) for _ in range(NX)]
        Vh = [st.sb("V_head", [P, NKT, 32]) for _ in range(2)]
        Qh = [st.sb("Q_head", [P, QT, P], BF16) for _ in range(2)]
        Qm = [st.sb("QT_max", [P, S], BF16) for _ in range(2)]
        Qe = [st.sb("QT_exp", [P, S], BF16) for _ in range(2)]
        PT = [cx[:, 0, i * EK * S:(i + 1) * EK * S] for i in range(4)]
        mx, nm, nr = st.sb("max_parts", [P, QT, KC]), st.sb("neg_max", [P, QT]), st.sb("neg_rest", [P, QT])
        osb = st.sb("groups", [P, S])
        rs = st.sb("sum_recip", [P, QT])
        sel = st.sb("group_sum", [P, 32])
        mb = st.ps("max_scores", [P, 2, 512])
        sT = st.ps("scoresT", [P, 2, EK * S])
        pb = [st.ps("weighted", [P, 512]) for _ in range(2)]
        if masks is not None:
            words = [kst[:, n, :].bitcast(I32) for n in range(2)]
            mq, mk = [st.sb("mask_add", [P, QT * SK], BF16) for _ in range(2)]
            junk = [cx[:, 1, a:a + 256].bitcast(BF16) for a in range(2 * QT * D, 2 * QT * D + 8 * 256, 256)]
        if key_mask is not None:
            km, kadd = st.sb("key_mask", [1, SK], I32), st.sb("key_add", [1, SK], BF16)

        w_loaded, ctx_loaded = st.sem("w_loaded"), st.sem("ctx_loaded")
        mask_loaded, mask_ready = st.sem("mask_loaded"), st.sem("mask_ready")
        km_done = st.sem("k_middle_done")
        passed = st.sem("wait_passed")
        cleared, src_ready = st.sem("cleared"), st.sem("src_ready")
        pro_made, pro_kept, kh_done, kl_done = (st.sem(n) for n in ("pro_made", "pro_kept", "k_high_done", "k_low_done"))
        k_stored = [st.sem("k_stored") for _ in range(KC)]
        q_step = st.sem("q_step")
        x_loaded = [st.sem("x_loaded") for _ in range(NX)]
        row_set = st.sem("mask_row_set")
        q_staged, v_staged = st.sem("q_staged"), st.sem("v_staged")
        t_made, qm_kept, qe_kept = st.sem("turned"), st.sem("QT_max_kept"), st.sem("QT_exp_kept")
        m_made, m_read, n_step, negm = (st.sem(n) for n in ("max_scores_made", "max_scores_read", "neg_step", "neg_max_ready"))
        st_made, exp_done, pv_done = st.sem("scoresT_made"), st.sem("exp_done"), st.sem("weighted_done")
        o_kept, fin, summed, normed = st.sem("groups_kept"), st.sem("groups_summed"), st.sem("recip_done"), st.sem("normalised")

        def heads(eng, b, step):
            with eng.Fori(0, TURNS - 1) as turn:
                for u in range(NX):
                    step(turn * NX + u, u, turn, True)
            for u in range(NX):
                step((TURNS - 1) * NX + u, u, TURNS - 1, u < NX - 1)

        with nc.Block() as block:

            @block.sync
            def _(sp):
                sp.dma_start(ws[:, :, :], w[0]).then_inc(w_loaded, 16)
                sp.dma_start(bs[:, :], w[1]).then_inc(w_loaded, 16)
                sp.dma_start(sel[:, :], w[2]).then_inc(w_loaded, 16)
                with sp.Fori(0, B) as b:
                    for n in range(HG * KC):
                        g, c = n // KC, n % KC
                        sp.wait_ge(kl_done, b * (HG * KC) + (n + 1))
                        sp.dma_start(parts_d[:, g * P:(g + 1) * P, c * 512:(c + 1) * 512].rearrange("a p k -> p a k"),
                                     kst[:, :, c * 512:(c + 1) * 512]).then_inc(k_stored[c], 16)
                    if key_mask is not None:
                        sp.wait_ge(mask_ready, b + 2)
                        for x in X:
                            sp.dma_start(x[MASKROW:XR, :], kadd[:, :]).then_inc(row_set, 16)

            @block.gpsimd
            def _(pool):
                pool.wait_ge(cleared, CLEARED)
                with pool.Fori(0, B) as b:
                    pool.wait_ge(pv_done, b * (H * EU) + 4)
                    pool.sem_inc(passed, 1)
                    pool.dma_start(cx[:, :, :], ctxT[bass.ds(b, 1)].rearrange("o p c k -> (o p) c k"))\
                        .then_inc(ctx_loaded, 16)
                    if key_mask is not None:
                        pool.dma_start(km[:, :], key_mask[bass.ds(b, 1), :]).then_inc(mask_loaded, 16)
                    for n in range(HG * KC):
                        c = n % KC
                        part = kst[:, :, c * 512:(c + 1) * 512]
                        pool.wait_ge(pro_kept, b * PRO + (n + 1))
                        pool.tensor_tensor(part[:, 1, :], kr[n % 2][:, :],
                                           R.onesf[:, 0:1].broadcast_to([P, 512]), ALU.mult)\
                            .then_inc(km_done, 1)
                        pool.wait_ge(km_done, b * (HG * KC) + (n + 1))
                        pool.tensor_tensor(part[:, 2, :], kr[n % 2][:, :], part[:, 1, :], ALU.subtract)\
                            .then_inc(kl_done, 1)
                    for s in k_stored:
                        pool.wait_ge(s, b * (HG * 16) + (HG * 16 + 1))
                    pool.sem_inc(passed, 1)
                    if masks is not None:
                        for n in range(2):
                            pool.dma_start(words[n], masks[n][bass.ds(b, 1)].rearrange("o p k -> (o p) k"))\
                                .then_inc(mask_loaded, 16)
                    pool.wait_ge(q_step, b * 7 + 7)
                    pool.wait_ge(pro_kept, b * PRO + PRO)

                    def load(h, u):
                        for r0, n, part in ((0, 3, 0), (48, 2, 1), (80, 1, 2)):
                            src = parts_d[part, bass.ds(h * d, d), :]
                            for i in range(n):
                                pool.dma_start(X[u][r0 + i * d:r0 + (i + 1) * d, :], src).then_inc(x_loaded[u], 16)

                    def stage_q(h, p):
                        pool.tensor_copy(Qh[p][:, :, :], Q[:, :, bass.ds(h, 1), :].rearrange("p q o c -> p q (o c)"))\
                            .then_inc(q_staged, 1)

                    def stage_v(h, p):
                        pool.tensor_copy(Vh[p][:, :, 0:VW],
                                         V[:, :, bass.ds(h, 1), :].rearrange("p k o v -> p k (o v)"))\
                            .then_inc(v_staged, 1)

                    pool.sem_inc(passed, 1)
                    for h in range(NX - 1):
                        load(h, h)
                    for h in range(2):
                        stage_q(h, h)
                        stage_v(h, h)

                    def step(h, u, turn, more):
                        hi = b * H + h
                        last_turn = isinstance(turn, int)
                        if not (last_turn and u > 0):
                            pool.wait_ge(pv_done, hi * EU + 4)
                            pool.sem_inc(passed, 1)
                            load(h + (NX - 1), (u + NX - 1) % NX)
                        if not (last_turn and u > 1):
                            pool.wait_ge(st_made, hi * EU + 1)
                            pool.sem_inc(passed, 1)
                            stage_q(h + 2, u % 2)
                            pool.wait_ge(pv_done, hi * EU + (EU + 4))
                            pool.sem_inc(passed, 1)
                            stage_v(h + 2, u % 2)

                    heads(pool, b, step)

            @block.tensor
            def _(pe):
                pe.sem_inc(pv_done, 4)
                pe.wait_ge(w_loaded, 48)
                pe.wait_ge(cleared, CLEARED)
                with pe.Fori(0, B) as b:
                    for n in range(PRO):
                        if n == 0:
                            pe.wait_ge(ctx_loaded, b * 16 + 16)
                        if n >= 2:
                            pe.wait_ge(pro_kept, b * PRO + (n - 1))
                        if n == HG * KC + NKT:
                            pe.wait_ge(src_ready, b + 1)
                        bank = mb[:, n % 2, :]
                        for c in range(DC):
                            if n < HG * KC:
                                g, k = n // KC, n % KC
                                ops = bank, ws[:, c, g * P:(g + 1) * P], cx[:, c, k * 512:(k + 1) * 512]
                            elif n < HG * KC + NKT:
                                k = n - HG * KC
                                ops = bank[:, 0:H * VW], cx[:, c, k * P:(k + 1) * P], ws[:, c, 2 * D:2 * D + H * VW]
                            else:
                                q = n - HG * KC - NKT
                                ops = bank[:, 0:D], qsrc[:, c, q * P:(q + 1) * P], ws[:, c, D:2 * D]
                            last = pe.matmul(*ops, start=(c == 0), stop=(c == DC - 1))
                        last.then_inc(pro_made, 1)

                    def turn_queries(p, bank, at):
                        o = bank[:, at:at + P].bitcast(BF16)
                        for q in range(QT):
                            last = pe.transpose(o[:, q * P:(q + 1) * P], Qh[p][:, q, :], R.identb[:, :])
                        last.then_inc(t_made, 1)

                    def max_unit(hi, u, turn, n):
                        if n == 0:
                            pe.wait_ge(qm_kept, hi + 1)
                            pe.wait_ge(x_loaded[u], (b * TURNS + turn) * 96 + 96)
                            if key_mask is not None:
                                pe.wait_ge(row_set, b * (16 * NX) + 16 * NX)
                        q, k = n // KC, n % KC
                        pe.matmul(mb[:, n % 2, :], Qm[u % 2][0:XR, q * P:(q + 1) * P], X[u][:, k * 512:(k + 1) * 512],
                                  start=True, stop=True).then_inc(m_made, 1)

                    pe.wait_ge(q_staged, b * H + 1)
                    pe.wait_ge(normed, b * H + 1)
                    pe.wait_ge(pro_kept, b * PRO + PRO)
                    turn_queries(0, pb[0], 384)
                    for n in range(MU):
                        if n >= 2:
                            pe.wait_ge(m_read, b * (H * MU) + (n - 1))
                        max_unit(b * H, 0, 0, n)
                    pe.wait_ge(negm, b * H + 1)
                    turn_queries(0, pb[0], 256)
                    pe.wait_ge(q_staged, b * H + 2)
                    pe.wait_ge(qe_kept, b * H + 1)
                    turn_queries(1, pb[0], 384)
                    if masks is not None:
                        pe.wait_ge(mask_ready, b * 2 + 3)
                        pe.sem_inc(passed, 1)

                    def step(h, u, turn, more):
                        hi, p = b * H + h, u % 2
                        last_turn = isinstance(turn, int)
                        n = 0
                        acc = pb[p]

                        def weigh(e):
                            pe.wait_ge(exp_done, hi * EU + (e + 3))
                            if e == 0:
                                pe.wait_ge(v_staged, hi + 1)
                            for i in range(EK):
                                kt = e * EK + i
                                last = pe.matmul(acc[32 * i:32 * (i + 1), 0:S], Vh[p][:, kt, :],
                                                 PT[e % 4][:, i * S:(i + 1) * S], start=(e == 0), stop=(e == EU - 1))
                            last.then_inc(pv_done, 1)

                        for e in range(EU):
                            if e == 0:
                                pe.wait_ge(qe_kept, hi + 1)
                                pe.wait_ge(qm_kept, hi + 2 if not (last_turn and u == NX - 1) else hi + 1)
                            pe.wait_ge(exp_done, hi * EU + (e + 1))
                            for half in range(2):
                                bank = sT[:, e % 2, half * 512:(half + 1) * 512]
                                k0 = (e * EK + 2 * half) * S
                                if masks is not None:
                                    pe.matmul(bank, R.identb[:, :], mk[:, k0:k0 + 512], start=True, stop=False)
                                for i in range(2):
                                    kt = e * EK + 2 * half + i
                                    last = pe.matmul(bank[:, i * S:(i + 1) * S], X[u][:, kt * P:(kt + 1) * P],
                                                     Qe[p][0:XR, :], start=(masks is None),
                                                     stop=(masks is None or i == 1))
                            last.then_inc(st_made, 1)
                            if more:
                                for _ in range(WHEN[e]):
                                    pe.wait_ge(m_read, hi * MU + (MU + n - 1))
                                    max_unit(hi + 1, (u + 1) % NX, turn + (1 if u == NX - 1 else 0), n)
                                    n += 1
                            if e == EU - 1 and more:
                                pe.wait_ge(negm, hi + 2)
                                turn_queries(1 - p, pb[1 - p], 256)
                            if e >= 1:
                                weigh(e - 1)
                        if not (last_turn and u > NX - 3):
                            pe.wait_ge(q_staged, hi + 3)
                            pe.wait_ge(qe_kept, hi + 2)
                            turn_queries(p, pb[1 - p], 384)
                        weigh(EU - 1)
                        pe.wait_ge(o_kept, hi + 1)
                        for q in range(QT):
                            last = pe.matmul(acc[:, 256 + q * 32:256 + q * 32 + VW], osb[:, q * P:(q + 1) * P],
                                             sel[:, 0:VW], start=True, stop=True)
                        last.then_inc(fin, 1)

                    heads(pe, b, step)

            @block.scalar
            def _(act):
                act.sem_inc(exp_done, 2)
                for s in k_stored:
                    act.sem_inc(s, 1)
                act.wait_ge(w_loaded, 48)
                with act.Fori(0, B) as b:
                    for n in range(HG * KC):
                        g, c = n // KC, n % KC
                        act.wait_ge(pro_made, b * PRO + (n + 1))
                        act.wait_ge(k_stored[c], b * (HG * 16) + (g * 16 + 1))
                        if n == 0 and masks is not None:
                            act.wait_ge(mask_ready, b * 2 + 1)
                        act.activation(kst[:, 0, c * 512:(c + 1) * 512], mb[:, n % 2, :], ACT.Identity,
                                       bias=bs[:, g:g + 1]).then_inc(kh_done, 1)

                    def keep_qm(head, p, bank):
                        act.wait_ge(t_made, head * 2 + 1)
                        act.activation(Qm[p][:, :], bank[:, 384:512].bitcast(BF16), ACT.Copy).then_inc(qm_kept, 1)

                    keep_qm(b * H, 0, pb[0])
                    keep_qm(b * H + 1, 1, pb[0])

                    def step(h, u, turn, more):
                        hi, p = b * H + h, u % 2
                        last_turn = isinstance(turn, int)
                        for e in range(EU):
                            act.wait_ge(st_made, hi * EU + (e + 1))
                            act.wait_ge(pv_done, hi * EU + (e + 1))
                            act.activation(PT[e % 4], sT[:, e % 2, :], ACT.Exp, scale=scale).then_inc(exp_done, 1)
                        if not (last_turn and u > NX - 3):
                            keep_qm(hi + 2, p, pb[1 - p])
                        act.wait_ge(pv_done, hi * EU + (EU + 4))
                        act.activation(osb[:, :], pb[p][:, 0:S], ACT.Copy).then_inc(o_kept, 1)

                    heads(act, b, step)

            @block.vector
            def _(dve):
                dve.sem_inc(normed, 1)
                dve.sem_inc(mask_ready, 1)
                for v in Vh:
                    dve.memset(v[:, :, :], 0.0).then_inc(cleared, 1)
                for x in X:
                    dve.memset(x[M0:XR, :], 1.0).then_inc(cleared, 1)
                dve.memset(Q[:, :, :, :], 0.0).then_inc(cleared, 1)
                dve.wait_ge(cleared, 2 + NX + 1)
                if key_mask is not None:
                    dve.memset(Q[:, :, :, MASKROW:MASKROW + 1], 1.0).then_inc(cleared, 1)
                dve.wait_ge(w_loaded, 48)
                dve.wait_ge(cleared, CLEARED)
                with dve.Fori(0, B) as b:
                    dve.wait_ge(pv_done, b * (H * EU) + 4)
                    dve.tensor_copy(qsrc[:, :, :], R.xnT[:, :, bass.ds(b * S, S)]).then_inc(src_ready, 1)
                    for n in range(HG * KC):
                        g, c = n // KC, n % KC
                        dve.wait_ge(kh_done, b * (HG * KC) + (n + 1))
                        if n >= 2:
                            dve.wait_ge(kl_done, b * (HG * KC) + (n - 1))
                        dve.scalar_tensor_tensor(out=kr[n % 2][:, :], in0=mb[:, n % 2, :], scalar=bs[:, g:g + 1],
                                                 in1=kst[:, 0, c * 512:(c + 1) * 512], op0=ALU.add,
                                                 op1=ALU.subtract).then_inc(pro_kept, 1)
                    if key_mask is not None:
                        dve.wait_ge(mask_loaded, b * 16 + 16)
                        dve.tensor_scalar(kadd[:, :], km[:, :], 0.0, MASKED, ALU.is_equal, ALU.mult)\
                           .then_inc(mask_ready, 1)
                    for k in range(NKT):
                        n = HG * KC + k
                        dve.wait_ge(pro_made, b * PRO + (n + 1))
                        dve.tensor_tensor(V[:, k, :, :].rearrange("p h v -> p (h v)"), mb[:, n % 2, 0:H * VW],
                                          bs[:, HG + D:HG + D + H * VW], ALU.add).then_inc(pro_kept, 1)
                    for q in range(QT):
                        n = HG * KC + NKT + q
                        dve.wait_ge(pro_made, b * PRO + (n + 1))
                        dve.tensor_tensor(qf[:, q, :], mb[:, n % 2, 0:D], bs[:, HG:HG + D], ALU.add)\
                           .then_inc(pro_kept, 1)
                    blk = [Q[:, :, :, i * d:(i + 1) * d] for i in range(6)]
                    q4, r4 = (t[:, :, :].rearrange("p q (h f) -> p q h f", h=H) for t in (qf, qr))
                    dve.wait_ge(pro_kept, b * PRO + PRO)
                    dve.tensor_copy(blk[0], q4).then_inc(q_step, 1)
                    dve.wait_ge(q_step, b * 7 + 1)
                    dve.tensor_tensor(r4, q4, blk[0], ALU.subtract).then_inc(q_step, 1)
                    dve.tensor_copy(blk[3], blk[0]).then_inc(q_step, 1)
                    dve.tensor_copy(blk[5], blk[0]).then_inc(q_step, 1)
                    dve.wait_ge(q_step, b * 7 + 4)
                    dve.tensor_copy(blk[1], r4).then_inc(q_step, 1)
                    dve.wait_ge(q_step, b * 7 + 5)
                    dve.tensor_copy(blk[4], blk[1]).then_inc(q_step, 1)
                    dve.tensor_tensor(blk[2], r4, blk[1], ALU.subtract).then_inc(q_step, 1)
                    if masks is not None:
                        dve.wait_ge(mask_loaded, b * 32 + 32)
                        dve.tensor_scalar(mq[:, :], words[0].bitcast(U8), MASKED, None, ALU.mult)\
                           .then_inc(mask_ready, 1)
                        dve.tensor_scalar(mk[:, :], words[1].bitcast(U8), MASKED, None, ALU.mult)\
                           .then_inc(mask_ready, 1)
                        dve.wait_ge(mask_ready, b * 2 + 3)

                    def maxima(head, p):
                        for n in range(MU):
                            q, k = n // KC, n % KC
                            dve.wait_ge(m_made, head * MU + (n + 1))
                            if masks is not None:
                                if n >= 8:
                                    dve.wait_ge(m_read, head * MU + (n - 7))
                                dve.sem_inc(passed, 1)
                                dve.tensor_tensor_reduce(junk[n % 8], mb[:, n % 2, :],
                                                         mq[:, q * SK + k * 512:q * SK + (k + 1) * 512], 1.0, -3e38,
                                                         ALU.add, ALU.max, mx[:, q, k:k + 1]).then_inc(m_read, 1)
                            else:
                                dve.tensor_reduce(mx[:, q, k:k + 1], mb[:, n % 2, :], AX.X, ALU.max)\
                                   .then_inc(m_read, 1)
                        part = [Qh[p][:, :, M0 + i] for i in range(3)]
                        dve.wait_ge(m_read, head * MU + MU)
                        dve.tensor_reduce(nm[:, :], mx[:, :, :], AX.X, ALU.max, negate=True).then_inc(n_step, 1)
                        dve.wait_ge(n_step, head * 4 + 1)
                        dve.tensor_copy(part[0], nm[:, :]).then_inc(n_step, 1)
                        dve.wait_ge(n_step, head * 4 + 2)
                        dve.tensor_tensor(nr[:, :], nm[:, :], part[0], ALU.subtract).then_inc(n_step, 1)
                        dve.wait_ge(n_step, head * 4 + 3)
                        dve.tensor_copy(part[1], nr[:, :]).then_inc(n_step, 1)
                        dve.wait_ge(n_step, head * 4 + 4)
                        dve.tensor_tensor(part[2], nr[:, :], part[1], ALU.subtract).then_inc(negm, 1)

                    def keep_qe(head, p, bank):
                        dve.wait_ge(t_made, head * 2 + 2)
                        dve.tensor_copy(Qe[p][:, :], bank[:, 256:384].bitcast(BF16)).then_inc(qe_kept, 1)

                    maxima(b * H, 0)
                    keep_qe(b * H, 0, pb[0])

                    def step(h, u, turn, more):
                        hi, p = b * H + h, u % 2
                        if more:
                            maxima(hi + 1, 1 - p)
                            keep_qe(hi + 1, 1 - p, pb[1 - p])
                        both = pb[p][:, 256:320].rearrange("p (q w) -> p q w", q=QT)
                        dve.wait_ge(fin, hi + 1)
                        dve.wait_ge(normed, hi + 1)
                        dve.reciprocal(rs[:, :], both[:, :, d]).then_inc(summed, 1)
                        dve.wait_ge(summed, hi + 1)
                        for q in range(QT):
                            ins = dve.tensor_scalar(
                                att[:, bass.ds(b * QT + q, 1), bass.ds(h * d, d)].rearrange("p o w -> p (o w)"),
                                both[:, q, 0:d], rs[:, q:q + 1], None, ALU.mult)
                        ins.then_inc(normed, 1)

                    heads(dve, b, step)


def context_stage(nc, R, att, ctxT_d, ctx_d):
    NKT, EK = SK // P, 4
    EU = NKT // EK
    parts = SK // 1024
    VW = D + 1
    with Stage(nc) as st:
        KT = st.sb("ctxT", [P, DC, SK])
        V = st.sb("ctx_ones", [P, NKT, VW])
        mx = st.sb("max_parts", [P, QT, parts])
        neg = st.sb("neg_max", [P, QT])
        nrow = st.sb("neg_max_row", [1, S])
        rsum = st.sb("sum_recip", [P, QT])
        PT = [st.sb("probsT", [P, EK * S]) for _ in range(3)]
        big = st.ps("scores", [P, 2, 1024])
        pv = st.ps("weighted", [P, QT, 512])
        rp = st.ps("row_ps", [1, S])
        loaded, ones_set = st.sem("loaded"), st.sem("ones_set")
        s_made, s_read, maxed, turned, row_kept = (st.sem(n) for n in (
            "scores_made", "scores_read", "maxed", "turned", "row_kept"))
        st_made, exp_done, pv_done, summed, normed = (st.sem(n) for n in (
            "scoresT_made", "exp_done", "weighted_done", "summed", "normalised"))
        MU = QT * parts
        with nc.Block() as block:

            @block.sync
            def _(sp):
                for b in range(B):
                    if b:
                        sp.wait_ge(pv_done, b * EU)
                    sp.dma_start(KT[:, :, :], ctxT_d[b]).then_inc(loaded, 16)
                    sp.dma_start(V[:, :, 0:D], ctx_d[b]).then_inc(loaded, 16)

            @block.gpsimd
            def _(pool):
                pool.memset(V[:, :, D:VW], 1.0).then_inc(ones_set, 1)

            @block.tensor
            def _(pe):
                pe.wait_ge(ones_set, 1)
                for b in range(B):
                    pe.wait_ge(loaded, (b + 1) * 32)
                    u = b * MU
                    if b:
                        pe.wait_ge(exp_done, b * EU)
                    for q in range(QT):
                        for k in range(parts):
                            if u % MU >= 2:
                                pe.wait_ge(s_read, u - 1)
                            for h in range(2):
                                k0 = k * 1024 + h * 512
                                for c in range(DC):
                                    last = pe.matmul(big[:, u % 2, h * 512:(h + 1) * 512],
                                                     R.xnT[:, c, b * S + q * P:b * S + (q + 1) * P],
                                                     KT[:, c, k0:k0 + 512], start=(c == 0), stop=(c == DC - 1))
                            last.then_inc(s_made, 1)
                            u += 1
                    pe.wait_ge(maxed, b + 1)
                    for q in range(QT):
                        last = pe.transpose(rp[:, q * P:(q + 1) * P], neg[:, q:q + 1], R.identf[:, :])
                    last.then_inc(turned, 1)
                    pe.wait_ge(row_kept, b + 1)

                    def weigh(e):
                        pe.wait_ge(exp_done, b * EU + e + 1)
                        if e == 0 and b:
                            pe.wait_ge(normed, b)
                        for i in range(EK):
                            kt = e * EK + i
                            for q in range(QT):
                                last = pe.matmul(pv[:, q, 0:VW], PT[e % 3][:, i * S + q * P:i * S + (q + 1) * P],
                                                 V[:, kt, :], start=(kt == 0), stop=(kt == NKT - 1))
                        last.then_inc(pv_done, 1)

                    for e in range(EU):
                        if e >= 2:
                            pe.wait_ge(exp_done, b * EU + e - 1)
                        for i in range(EK):
                            kt = e * EK + i
                            o = big[:, e % 2, i * S:(i + 1) * S]
                            for c in range(DC):
                                pe.matmul(o, KT[:, c, kt * P:(kt + 1) * P], R.xnT[:, c, b * S:(b + 1) * S],
                                          start=(c == 0), stop=False)
                            last = pe.matmul(o, R.onesf[0:1, :], nrow[:, :], start=False, stop=True)
                        last.then_inc(st_made, 1)
                        if e >= 1:
                            weigh(e - 1)
                    weigh(EU - 1)

            @block.scalar
            def _(act):
                for e in range(B * EU):
                    act.wait_ge(st_made, e + 1)
                    if e >= 3:
                        act.wait_ge(pv_done, e - 2)
                    act.activation(PT[e % EU % 3][:, :], big[:, e % 2, :], ACT.Exp).then_inc(exp_done, 1)

            @block.vector
            def _(dve):
                for b in range(B):
                    for u in range(MU):
                        dve.wait_ge(s_made, b * MU + u + 1)
                        dve.tensor_reduce(mx[:, u // parts, u % parts:u % parts + 1], big[:, u % 2, :],
                                          AX.X, ALU.max).then_inc(s_read, 1)
                    dve.wait_ge(s_read, (b + 1) * MU)
                    dve.tensor_reduce(neg[:, :], mx[:, :, :], AX.X, ALU.max, negate=True).then_inc(maxed, 1)
                    dve.wait_ge(turned, b + 1)
                    dve.tensor_copy(nrow[:, :], rp[:, :]).then_inc(row_kept, 1)
                    dve.wait_ge(pv_done, (b + 1) * EU)
                    dve.reciprocal(rsum[:, :], pv[:, :, D]).then_inc(summed, 1)
                    dve.wait_ge(summed, b + 1)
                    for q in range(QT):
                        ins = dve.tensor_scalar(att[:, b * QT + q, :], pv[:, q, 0:D], rsum[:, q:q + 1], None, ALU.mult)
                    ins.then_inc(normed, 1)


def combine_stage(nc, R, att, dram):
    with Stage(nc) as st:
        w, rowp = st.sb("w_comb", [P, 2 * DC, D]), st.sb("b_gamma_beta", [P, 3, D])
        aT = st.sb("attT", [P, DC, NT * P])
        y = st.sb("y", [P, NT, D])
        stats, mv, rstd = st.sb("stats", [P, NT, 6]), st.sb("mean_var", [P, NT, 2]), st.sb("rstd", [P, NT])
        tp = [st.ps("tp", [P, NT * P]) for _ in range(DC)]
        acc = [st.ps("acc", [P, 512]) for _ in range(NT)]
        loaded, turned, kept, made, step, rooted = (st.sem(n) for n in (
            "loaded", "turned", "kept", "made", "dve_step", "rooted"))
        with nc.Block() as block:

            @block.sync
            def _(sp):
                sp.dma_start(w[:, :, :], dram["w9"]).then_inc(loaded, 16)
                sp.dma_start(rowp[:, :, :], dram["r9"]).then_inc(loaded, 16)

            @block.tensor
            def _(pe):
                for c in range(DC):
                    for t in range(NT):
                        last = pe.transpose(tp[c][:, t * P:(t + 1) * P], att[:, t, c * P:(c + 1) * P], R.identf[:, :])
                    last.then_inc(turned, 1)
                pe.wait_ge(kept, DC)
                pe.wait_ge(loaded, 32)
                for t in range(NT):
                    for c in range(2 * DC):
                        src = aT if c < DC else R.xnT
                        last = pe.matmul(acc[t][:, 0:D], src[:, c % DC, t * P:(t + 1) * P], w[:, c, :],
                                         start=(c == 0), stop=(c == 2 * DC - 1))
                    last.then_inc(made, 1)

            @block.scalar
            def _(act):
                for c in range(DC):
                    act.wait_ge(turned, c + 1)
                    act.activation(aT[:, c, :], tp[c][:, :], ACT.Copy).then_inc(kept, 1)
                act.wait_ge(step, 3 * NT + 1)
                act.activation(rstd[:, :], rstd[:, :], ACT.Sqrt).then_inc(rooted, 1)

            @block.vector
            def _(dve):
                dve.wait_ge(loaded, 32)
                for t in range(NT):
                    dve.wait_ge(made, t + 1)
                    dve.tensor_tensor(y[:, t, :], acc[t][:, 0:D], rowp[:, 0, :], ALU.add).then_inc(step, 1)
                for t in range(NT):
                    dve.wait_ge(step, t + 1)
                    dve.bn_stats(stats[:, t, :], y[:, t, :]).then_inc(step, 1)
                for t in range(NT):
                    dve.wait_ge(step, NT + t + 1)
                    dve.bn_aggr(mv[:, t, :], stats[:, t, :]).then_inc(step, 1)
                dve.wait_ge(step, 3 * NT)
                dve.tensor_scalar(rstd[:, :], mv[:, :, 1], EPS, None, ALU.add).then_inc(step, 1)
                dve.wait_ge(rooted, 1)
                dve.reciprocal(rstd[:, :], rstd[:, :]).then_inc(step, 1)
                n = 3 * NT + 2
                dve.wait_ge(step, n)
                for t in range(NT):
                    dve.tensor_scalar(y[:, t, :], y[:, t, :], mv[:, t, 0:1], rstd[:, t:t + 1],
                                      ALU.subtract, ALU.mult).then_inc(step, 1)
                for k, op in ((1, ALU.mult), (2, ALU.add)):
                    for t in range(NT):
                        n += 1
                        dve.wait_ge(step, n)
                        dve.tensor_tensor(y[:, t, :], y[:, t, :], rowp[:, k, :], op).then_inc(step, 1)
                for t in range(NT):
                    n += 1
                    dve.wait_ge(step, n)
                    dve.tensor_tensor(R.x[:, t, :], R.x[:, t, :], y[:, t, :], ALU.add)


def quantised_stage(nc, R, dram):
    HT = 8
    MAGIC = 1.5 * 2.0 ** 23
    SMALL = 1e-8
    with Stage(nc) as st:
        w1, w2 = st.sb("w1", [P, HT, D]), st.sb("w2", [P, DC, HT * P])
        b1, b2 = st.sb("b1", [P, HT]), st.sb("b2", [P, DC])
        w1q, w2q = st.sb("w1q", [P, HT, D], BF16), st.sb("w2q", [P, DC, HT * P], BF16)
        w1T, w2T = st.sb("w1qT", [P, DC, HT * P], BF16), st.sb("w2qT", [P, HT, D], BF16)
        s1, s2, i1, i2 = (st.sb(n, [P, w]) for n, w in (("s1", HT), ("s2", DC), ("i1", HT), ("i2", DC)))
        c1, c2 = st.sb("bq1", [P, HT]), st.sb("bq2", [P, DC])
        pm, gm, gs, gi = (st.sb(n, [P, 2]) for n in ("part_max", "all_max", "in_scale", "in_inverse"))
        grow = st.sb("max_row", [1, 2])
        xq = st.sb("xq", [P, DC, NT * P], BF16)
        h, hq = st.sb("h", [P, HT, NT * P]), st.sb("hq", [P, HT, NT * P], BF16)
        yT = st.sb("yT", [P, DC, NT * P])
        wp = [st.ps("w_turned", [P, 1024], BF16) for _ in range(2)]
        tp = st.ps("max_turned", [P, 512])
        ps = [st.ps("h_ps", [P, NT * P]) for _ in range(3)]
        yp = [st.ps("y_turned", [P, 512]) for _ in range(2)]
        loaded, step, wq_ready, w_turned, w_kept = (st.sem(n) for n in (
            "loaded", "dve_step", "w_quantised", "w_turned", "w_kept"))
        maxed, m_turned, row_ready, x_ready, made, kept, bias_ready = (st.sem(n) for n in (
            "maxed", "max_turned", "max_row_ready", "x_quantised", "made", "kept", "bias_ready"))
        out_turned, part = st.sem("out_turned"), st.sem("h_part_max")
        with nc.Block() as block:

            @block.sync
            def _(sp):
                sp.dma_start(w1[:, :, :], dram["w11_1"]).then_inc(loaded, 16)
                sp.dma_start(b1[:, :], dram["b11_1"]).then_inc(loaded, 16)
                sp.dma_start(w2[:, :, :], dram["w11_2"]).then_inc(loaded, 16)
                sp.dma_start(b2[:, :], dram["b11_2"]).then_inc(loaded, 16)

            @block.vector
            def _(dve):
                n = 0

                def did(ins):
                    nonlocal n
                    ins.then_inc(step, 1)
                    n += 1

                def round_to(out, src, inverse, low, high):
                    did(dve.tensor_scalar(src, src, inverse, MAGIC, ALU.mult, ALU.add))
                    dve.wait_ge(step, n)
                    did(dve.tensor_scalar(src, src, -MAGIC, low, ALU.add, ALU.max))
                    dve.wait_ge(step, n)
                    return dve.tensor_scalar(out, src, high, None, ALU.min)

                def weights(w, wq, s, inv, count):
                    did(dve.tensor_reduce(s[:, :], w[:, :, :], AX.X, ALU.max, apply_absolute_value=True))
                    dve.wait_ge(step, n)
                    did(dve.tensor_scalar(s[:, :], s[:, :], SMALL, 1.0 / 127.0, ALU.max, ALU.mult))
                    dve.wait_ge(step, n)
                    did(dve.reciprocal(inv[:, :], s[:, :]))
                    dve.wait_ge(step, n)
                    for f in range(count):
                        round_to(wq[:, f, :], w[:, f, :], inv[:, f:f + 1], -128.0, 127.0).then_inc(wq_ready, 1)

                def input_scale(k):
                    dve.wait_ge(m_turned, 2 * k + 1)
                    dve.tensor_reduce(grow[:, k:k + 1], tp[0:1, 0:P], AX.X, ALU.max).then_inc(row_ready, 1)
                    dve.wait_ge(m_turned, 2 * k + 2)
                    did(dve.tensor_scalar(gs[:, k:k + 1], tp[:, P:P + 1], SMALL, 1.0 / 255.0, ALU.max, ALU.mult))
                    dve.wait_ge(step, n)
                    did(dve.reciprocal(gi[:, k:k + 1], gs[:, k:k + 1]))
                    dve.wait_ge(step, n)

                def bias(s, inv, b, c, k):
                    did(dve.tensor_scalar(s[:, :], s[:, :], gs[:, k:k + 1], None, ALU.mult))
                    dve.wait_ge(step, n)
                    did(dve.reciprocal(inv[:, :], s[:, :]))
                    dve.wait_ge(step, n)
                    did(dve.tensor_tensor(c[:, :], b[:, :], inv[:, :], ALU.mult))
                    dve.wait_ge(step, n)
                    did(dve.tensor_scalar(c[:, :], c[:, :], MAGIC, -MAGIC, ALU.add, ALU.add))
                    dve.wait_ge(step, n)
                    dve.tensor_tensor(c[:, :], c[:, :], s[:, :], ALU.mult).then_inc(bias_ready, 1)

                dve.tensor_reduce(pm[:, 0:1], R.xnT[:, :, :], AX.XY, ALU.max).then_inc(maxed, 1)
                dve.wait_ge(loaded, 64)
                weights(w1, w1q, s1, i1, HT)
                input_scale(0)
                for c in range(DC):
                    round_to(xq[:, c, :], R.xnT[:, c, :], gi[:, 0:1], 0.0, 255.0).then_inc(x_ready, 1)
                bias(s1, i1, b1, c1, 0)
                weights(w2, w2q, s2, i2, DC)
                dve.wait_ge(kept, HT)
                dve.tensor_reduce(pm[:, 1:2], h[:, :, :], AX.XY, ALU.max).then_inc(maxed, 1)
                input_scale(1)
                for c in range(HT):
                    round_to(hq[:, c, :], h[:, c, :], gi[:, 1:2], 0.0, 255.0).then_inc(x_ready, 1)
                bias(s2, i2, b2, c2, 1)
                for t in range(NT):
                    dve.wait_ge(out_turned, t // 2 * 2 + 2)
                    dve.tensor_tensor(R.x[:, t, :], R.x[:, t, :], yp[t // 2][:, (t % 2) * D:(t % 2 + 1) * D], ALU.add)

            @block.tensor
            def _(pe):
                def all_max(k):
                    pe.wait_ge(maxed, k + 1)
                    pe.transpose(tp[0:1, 0:P], pm[:, k:k + 1], R.identf[:, :]).then_inc(m_turned, 1)
                    pe.wait_ge(row_ready, k + 1)
                    pe.matmul(tp[:, P:P + 1], R.onesf[0:1, :], grow[:, k:k + 1], start=True, stop=True)\
                      .then_inc(m_turned, 1)

                all_max(0)
                for c in range(DC):
                    pe.wait_ge(wq_ready, HT)
                    for f in range(HT):
                        last = pe.transpose(wp[c][:, f * P:(f + 1) * P], w1q[:, f, c * P:(c + 1) * P], R.identb[:, :])
                    last.then_inc(w_turned, 1)
                pe.wait_ge(w_kept, 2)
                pe.wait_ge(x_ready, DC)
                for f in range(HT):
                    if f >= 3:
                        pe.wait_ge(kept, f - 2)
                    for c in range(DC):
                        last = pe.matmul(ps[f % 3][:, :], w1T[:, c, f * P:(f + 1) * P], xq[:, c, :],
                                         start=(c == 0), stop=(c == DC - 1))
                    last.then_inc(made, 1)
                pe.wait_ge(wq_ready, HT + DC)
                for o in range(2):
                    for f in range(4):
                        for c in range(DC):
                            last = pe.transpose(wp[o][:, f * D + c * P:f * D + (c + 1) * P],
                                                w2q[:, c, (4 * o + f) * P:(4 * o + f + 1) * P], R.identb[:, :])
                    last.then_inc(w_turned, 1)
                pe.wait_ge(kept, HT)
                all_max(1)
                pe.wait_ge(w_kept, 4)
                pe.wait_ge(x_ready, DC + HT)
                for o in range(DC):
                    for f in range(HT):
                        last = pe.matmul(ps[o][:, :], w2T[:, f, o * P:(o + 1) * P], hq[:, f, :],
                                         start=(f == 0), stop=(f == HT - 1))
                    last.then_inc(made, 1)
                pe.wait_ge(kept, HT + DC)
                for t in range(NT):
                    for o in range(DC):
                        last = pe.transpose(yp[t // 2][:, (t % 2) * D + o * P:(t % 2) * D + (o + 1) * P],
                                            yT[:, o, t * P:(t + 1) * P], R.identf[:, :])
                    last.then_inc(out_turned, 1)

            @block.scalar
            def _(act):
                for c in range(DC):
                    act.wait_ge(w_turned, c + 1)
                    act.activation(w1T[:, c, :], wp[c][:, :], ACT.Copy).then_inc(w_kept, 1)
                act.wait_ge(bias_ready, 1)
                for f in range(HT):
                    act.wait_ge(made, f + 1)
                    act.activation(h[:, f, :], ps[f % 3][:, :], ACT.Relu, bias=c1[:, f:f + 1],
                                   scale=s1[:, f:f + 1]).then_inc(kept, 1)
                for o in range(2):
                    act.wait_ge(w_turned, 3 + o)
                    act.activation(w2T[:, 4 * o:4 * (o + 1), :], wp[o][:, :].rearrange("p (f m) -> p f m", f=4),
                                   ACT.Copy).then_inc(w_kept, 1)
                act.wait_ge(bias_ready, 2)
                for o in range(DC):
                    act.wait_ge(made, HT + o + 1)
                    act.activation(yT[:, o, :], ps[o][:, :], ACT.Identity, bias=c2[:, o:o + 1],
                                   scale=s2[:, o:o + 1]).then_inc(kept, 1)


def mamba_stages(nc, R, dram):
    CT, NS, K = 4, 16, 4
    T = NT * P
    bc_d = nc.dram_tensor("bc_rows", [2 * NS, T], F32, kind="Internal").ap()
    with ExitStack() as keep:
        def sb(name, shape, dt=F32):
            return keep.enter_context(nc.sbuf_tensor("ssm_" + name, shape, dt))

        actT, gate, delta, dx = (sb(n, [P, CT, T]) for n in ("act", "gate", "delta", "dx"))
        yT, A = sb("y", [P, CT, T]), sb("A", [P, CT, NS])
        cols = sb("cols", [P, CT, 9])
        BI, BG, CB, BD, DS, TAP = 0, 1, 2, 3, 4, 5
        wd = sb("w_delta", [P, CT, CT * P])
        wbc = sb("w_bc", [P, CT, 2 * NS])

        with Stage(nc) as st:
            win, wg = st.sb("w_in", [P, DC, CT * P]), st.sb("w_gate", [P, DC, CT * P])
            xz = st.sb("xz", [P, CT, B, K - 1 + S])
            cv = st.sb("conv", [P, CT, T])
            ps = [st.ps("ps", [P, T]) for _ in range(4)]
            loaded, made, xz_kept, conv, gate_kept, acted, zeroed = (st.sem(n) for n in (
                "loaded", "made", "xz_kept", "conv_step", "gate_kept", "acted", "zeroed"))
            with nc.Block() as block:

                @block.sync
                def _(sp):
                    sp.dma_start(cols[:, :, :], dram["s_cols"]).then_inc(loaded, 16)
                    sp.dma_start(win[:, :, :], dram["s_win"]).then_inc(loaded, 16)
                    sp.dma_start(wg[:, :, :], dram["s_wgate"]).then_inc(loaded, 16)
                    sp.dma_start(A[:, :, :], dram["s_alog"]).then_inc(loaded, 16)
                    sp.dma_start(wd[:, :, :], dram["s_wdelta"]).then_inc(loaded, 16)
                    sp.dma_start(wbc[:, :, :], dram["s_wbc"]).then_inc(loaded, 16)

                @block.gpsimd
                def _(pool):
                    pool.memset(xz[:, :, :, 0:K - 1], 0.0).then_inc(zeroed, 1)

                @block.tensor
                def _(pe):
                    pe.wait_ge(loaded, 96)
                    for n in range(2 * CT):
                        w, f = (win, n) if n < CT else (wg, n - CT)
                        if n >= 4:
                            pe.wait_ge(xz_kept, n - 3)
                        for c in range(DC):
                            last = pe.matmul(ps[n % 4][:, :], w[:, c, f * P:(f + 1) * P], R.xnT[:, c, :],
                                             start=(c == 0), stop=(c == DC - 1))
                        last.then_inc(made, 1)

                @block.vector
                def _(dve):
                    dve.wait_ge(zeroed, 1)
                    for f in range(CT):
                        dve.wait_ge(xz_kept, f + 1)
                        dst = cv[:, f, :].rearrange("p (b s) -> p b s", b=B)
                        for k in range(K):
                            src = xz[:, f, :, k:k + S]
                            tap = cols[:, f, TAP + k:TAP + k + 1]
                            if k == 0:
                                dve.tensor_scalar(dst, src, tap, None, ALU.mult).then_inc(conv, 1)
                            else:
                                dve.wait_ge(conv, f * K + k)
                                dve.scalar_tensor_tensor(out=dst, in0=src, scalar=tap, in1=dst,
                                                         op0=ALU.mult, op1=ALU.add).then_inc(conv, 1)

                @block.scalar
                def _(act):
                    for f in range(CT):
                        act.wait_ge(made, f + 1)
                        act.activation(xz[:, f, :, K - 1:K - 1 + S], ps[f][:, :].rearrange("p (b s) -> p b s", b=B),
                                       ACT.Identity, bias=cols[:, f, BI:BI + 1]).then_inc(xz_kept, 1)
                    for f in range(CT):
                        act.wait_ge(made, CT + f + 1)
                        act.activation(gate[:, f, :], ps[f][:, :], ACT.Silu, bias=cols[:, f, BG:BG + 1])
                    for f in range(CT):
                        act.wait_ge(conv, (f + 1) * K)
                        act.activation(actT[:, f, :], cv[:, f, :], ACT.Silu, bias=cols[:, f, CB:CB + 1])
                    act.activation(A[:, :, :], A[:, :, :], ACT.Exp).then_inc(acted, 1)

        with Stage(nc) as st:
            z, ez = st.sb("z", [P, CT, T]), st.sb("ez", [P, CT, T])
            bc = st.sb("bc", [2 * NS, T])
            ps = [st.ps("ps", [P, T]) for _ in range(CT)]
            bp = st.ps("bc_ps", [2 * NS, T])
            made, kept, lned, step, bc_made, stored = (st.sem(n) for n in (
                "made", "z_kept", "ln_done", "dve_step", "bc_kept", "bc_stored"))
            with nc.Block() as block:

                @block.tensor
                def _(pe):
                    for c in range(CT):
                        last = pe.matmul(bp[:, :], wbc[:, c, :], actT[:, c, :], start=(c == 0), stop=(c == CT - 1))
                    last.then_inc(made, 1)
                    for f in range(CT):
                        for c in range(CT):
                            last = pe.matmul(ps[f][:, :], wd[:, c, f * P:(f + 1) * P], actT[:, c, :],
                                             start=(c == 0), stop=(c == CT - 1))
                        last.then_inc(made, 1)

                @block.sync
                def _(sp):
                    sp.wait_ge(bc_made, 1)
                    sp.dma_start(bc_d, bc[:, :]).then_inc(stored, 16)
                    sp.wait_ge(stored, 16)

                @block.scalar
                def _(act):
                    act.wait_ge(made, 1)
                    act.activation(bc[:, :], bp[:, :], ACT.Copy).then_inc(bc_made, 1)
                    for f in range(CT):
                        act.wait_ge(made, f + 2)
                        act.activation(z[:, f, :], ps[f][:, :], ACT.Identity, bias=cols[:, f, BD:BD + 1])\
                           .then_inc(kept, 1)
                    act.wait_ge(kept, CT)
                    act.activation(ez[:, :, :], z[:, :, :], ACT.Abs).then_inc(kept, 1)
                    act.wait_ge(kept, CT + 1)
                    act.activation(ez[:, :, :], ez[:, :, :], ACT.Exp, scale=-1.0).then_inc(kept, 1)
                    act.wait_ge(kept, CT + 2)
                    act.activation(ez[:, :, :], ez[:, :, :], ACT.Ln, bias=1.0).then_inc(lned, 1)

                @block.vector
                def _(dve):
                    dve.tensor_scalar(A[:, :, :], A[:, :, :], -1.0, None, ALU.mult)
                    dve.wait_ge(lned, 1)
                    dve.tensor_scalar(delta[:, :, :], z[:, :, :], 0.0, None, ALU.max).then_inc(step, 1)
                    dve.wait_ge(step, 1)
                    dve.tensor_tensor(delta[:, :, :], delta[:, :, :], ez[:, :, :], ALU.add).then_inc(step, 1)
                    dve.wait_ge(step, 2)
                    dve.tensor_tensor(dx[:, :, :], delta[:, :, :], actT[:, :, :], ALU.mult)

        with Stage(nc) as st:
            bcb = st.sb("bc_all", [P, 2 * NS, T])
            dA, dB = ([st.sb(n, [P, T]) for _ in range(2)] for n in ("dA", "dBx"))
            hh, hc = ([st.sb(n, [P, T]) for _ in range(2)] for n in ("h", "hC"))
            zero = st.sb("zero", [P, T])
            An = st.sb("A_now", [P, CT])
            yp = [st.ps("y_ps", [P, T]) for _ in range(CT)]
            loaded, a_ready, da, db, scanned, hc_ready, summed = (st.sem(n) for n in (
                "bc_loaded", "A_ready", "dA_ready", "dBx_ready", "scanned", "hC_ready", "summed"))
            cleared = st.sem("cleared")
            with nc.Block() as block:

                @block.sync
                def _(sp):
                    sp.dma_start(bcb[:, :, :], bc_d.partition_broadcast(P)).then_inc(loaded, 16)
                    sp.wait_ge(loaded, 16)

                @block.scalar
                def _(act):
                    act.sem_inc(a_ready, 1)
                    act.sem_inc(da, 1)
                    with act.Fori(0, NS) as n:
                        act.wait_ge(da, n * CT + 1)
                        act.activation(An[:, :], A[:, :, bass.ds(n, 1)].rearrange("p c o -> p (c o)"), ACT.Copy)\
                           .then_inc(a_ready, 1)
                        act.wait_ge(a_ready, n + 2)
                        for i in range(CT):
                            act.wait_ge(scanned, n * CT + (1 + max(i - 1, 0)))
                            act.activation(dA[i % 2][:, :], delta[:, i, :], ACT.Exp, scale=An[:, i:i + 1])\
                               .then_inc(da, 1)

                @block.vector
                def _(dve):
                    dve.memset(zero[:, :], 0.0).then_inc(cleared, 1)
                    dve.sem_inc(scanned, 1)
                    dve.sem_inc(hc_ready, 1)
                    dve.wait_ge(loaded, 16)
                    with dve.Fori(0, NS) as n:
                        for i in range(CT):
                            dve.tensor_tensor(dB[i % 2][:, :], dx[:, i, :],
                                              bcb[:, bass.ds(n, 1), :].rearrange("p o t -> p (o t)"), ALU.mult)\
                               .then_inc(db, 1)
                            dve.wait_ge(da, n * CT + (i + 2))
                            dve.wait_ge(db, n * CT + (i + 1))
                            dve.wait_ge(hc_ready, n * CT + (1 + max(i - 1, 0)))
                            for b in range(B):
                                s = slice(b * S, (b + 1) * S)
                                ins = dve.tensor_tensor_scan(hh[i % 2][:, s], dA[i % 2][:, s], dB[i % 2][:, s],
                                                             0.0, ALU.mult, ALU.add)
                            ins.then_inc(scanned, 1)
                            dve.wait_ge(scanned, n * CT + (i + 2))
                            dve.wait_ge(summed, n * CT + (1 + max(i - 1, 0)))
                            dve.tensor_tensor(hc[i % 2][:, :], hh[i % 2][:, :],
                                              bcb[:, bass.ds(n + NS, 1), :].rearrange("p o t -> p (o t)"),
                                              ALU.mult).then_inc(hc_ready, 1)

                @block.tensor
                def _(pe):
                    pe.wait_ge(cleared, 1)
                    for i in range(CT):
                        last = pe.matmul(yp[i][:, :], R.identf[:, :], zero[:, :], start=True, stop=False,
                                         skip_group_check=True)
                    last.then_inc(summed, 1)
                    with pe.Fori(0, NS) as n:
                        for i in range(CT):
                            pe.wait_ge(hc_ready, n * CT + (i + 2))
                            pe.matmul(yp[i][:, :], R.identf[:, :], hc[i % 2][:, :], start=False, stop=False,
                                      skip_group_check=True).then_inc(summed, 1)
                    for i in range(CT):
                        pe.matmul(yp[i][:, :], R.identf[:, :], zero[:, :], start=False, stop=True,
                                  skip_group_check=True).then_inc(summed, 1)

            with nc.Block() as block:

                @block.vector
                def _(dve):
                    for i in range(CT):
                        dve.scalar_tensor_tensor(out=yT[:, i, :], in0=actT[:, i, :], scalar=cols[:, i, DS:DS + 1],
                                                 in1=yp[i][:, :], op0=ALU.mult, op1=ALU.add).then_inc(cleared, 1)
                    for i in range(CT):
                        dve.wait_ge(cleared, i + 2)
                        dve.tensor_tensor(yT[:, i, :], yT[:, i, :], gate[:, i, :], ALU.mult)

        with Stage(nc) as st:
            wo, bo = st.sb("w_out", [P, CT, D]), st.sb("b_out", [P, D])
            ps = [st.ps("ps", [P, 512]) for _ in range(NT)]
            loaded, made, biased = st.sem("loaded"), st.sem("made"), st.sem("biased")
            with nc.Block() as block:

                @block.sync
                def _(sp):
                    sp.dma_start(wo[:, :, :], dram["s_wout"]).then_inc(loaded, 16)
                    sp.dma_start(bo[:, :], dram["s_bout"]).then_inc(loaded, 16)

                @block.tensor
                def _(pe):
                    pe.wait_ge(loaded, 32)
                    for t in range(NT):
                        for c in range(CT):
                            last = pe.matmul(ps[t][:, 0:D], yT[:, c, t * P:(t + 1) * P], wo[:, c, :],
                                             start=(c == 0), stop=(c == CT - 1))
                        last.then_inc(made, 1)

                @block.vector
                def _(dve):
                    dve.wait_ge(loaded, 32)
                    for t in range(NT):
                        dve.tensor_tensor(R.x[:, t, :], R.x[:, t, :], bo[:, :], ALU.add).then_inc(biased, 1)
                    for t in range(NT):
                        dve.wait_ge(biased, t + 1)
                        dve.wait_ge(made, t + 1)
                        dve.tensor_tensor(R.x[:, t, :], R.x[:, t, :], ps[t][:, 0:D], ALU.add)


class Resident:
    pass


def build(nc, dram, out):
    R = Resident()
    Stage.number = 0
    with ExitStack() as keep:
        def sb(name, shape, dt=F32):
            return keep.enter_context(nc.sbuf_tensor(name, shape, dt))

        R.x, R.xn = sb("x_res", [P, NT, D]), sb("xn", [P, NT, D])
        R.xnT = sb("xnT", [P, DC, NT * P])
        R.identf, R.identb, R.onesf = sb("identf", [P, P]), sb("identb", [P, P], BF16), sb("onesf", [P, P])
        R.stored = nc.alloc_semaphore("out_stored")
        setup_stage(nc, R, dram["x"])

        def attend(layer, width, nk, hg, d, scale, out_bias, **how):
            norm_stage(nc, R)
            with nc.sbuf_tensor(f"att{layer}", [P, NT, width], F32) as att:
                attention_stage(nc, R, att, dram[f"w{layer}"], nk, hg, d, scale, **how)
                add_projected_stage(nc, R, att, width, dram[f"o{layer}"], dram[f"ob{layer}"] if out_bias else None)

        parts_d = nc.dram_tensor("key_parts_rows", [3, D, SK], BF16, kind="Internal").ap()

        def attend_context(layer, out_bias, **how):
            norm_stage(nc, R)
            with nc.sbuf_tensor(f"att{layer}", [P, NT, D], F32) as att:
                split_context_stage(nc, R, att, (dram[f"w{layer}"], dram[f"b{layer}"], dram["group_sum"]), 0.25,
                                    dram["ctxT"], parts_d, **how)
                add_projected_stage(nc, R, att, D, dram[f"o{layer}"], dram[f"ob{layer}"] if out_bias else None)

        causal = (dram["causal_q"], dram["causal_k"])
        if 0 in LAYERS:
            attend_context(0, True, masks=(dram["m0q"], dram["m0k"]))
        if 1 in LAYERS:
            attend(1, D, S, 4, 16, 1.0 / 16, False, masks=causal, rope=(dram["rope_k"], dram["rope_q"]))
        if 2 in LAYERS:
            norm_stage(nc, R)
            experts_stage(nc, R, dram, 2, 10, ACT.Gelu, 0.5)
        if 3 in LAYERS:
            attend(3, 1024, SK, 1, 64, 0.125, True, ctxT=dram["ctxT"], masks=(dram["m3q"], dram["m3k"]))
        if 4 in LAYERS:
            scratch = nc.dram_tensor("mixed_heads", [B, 16, S, 16], F32, kind="Internal").ap()
            norm_stage(nc, R)
            head_mix_stage(nc, R, dram, scratch)
            with nc.sbuf_tensor("att4", [P, NT, D], F32) as att:
                reload_stage(nc, att, scratch)
                add_projected_stage(nc, R, att, D, dram["o4"], dram["ob4"])
        if 5 in LAYERS:
            norm_stage(nc, R)
            experts_stage(nc, R, dram, 5, 9, ACT.Silu, 1.0)
        if 6 in LAYERS:
            attend_context(6, False, key_mask=dram["m6"])
        if 7 in LAYERS:
            norm_stage(nc, R)
            mamba_stages(nc, R, dram)
        if 8 in LAYERS:
            norm_stage(nc, R)
            signs_stage(nc, R, dram)
        if 9 in LAYERS:
            norm_stage(nc, R)
            with nc.sbuf_tensor("att9", [P, NT, D], F32) as att:
                context_stage(nc, R, att, dram["ctxT"], dram["ctx"])
                combine_stage(nc, R, att, dram)
        if 10 in LAYERS:
            attend(10, D, S, 4, 16, 0.25, False, masks=causal)
        if 11 in LAYERS:
            norm_stage(nc, R)
            quantised_stage(nc, R, dram)
        store_stage(nc, R, out)


def store_stage(nc, R, out):
    with nc.Block() as block:

        @block.sync
        def _(sp):
            sp.dma_start(out, R.x[:, :, :]).then_inc(R.stored, 16)
            sp.wait_ge(R.stored, 16)



def kernel(**inputs):
    import concourse.bacc as bacc
    from concourse.bass_utils import run_bass_kernel_spmd as run

    a = {k: np.asarray(v) for k, v in inputs.items()}
    nc = bacc.Bacc("TRN2", target_bir_lowering=False, num_devices=1)
    arrays, dram = {}, {}

    def give(name, v):
        v = np.ascontiguousarray(v)
        arrays["in_" + name] = v
        dram[name] = nc.dram_tensor("in_" + name, v.shape, mybir.dt.from_np(v.dtype), kind="ExternalInput").ap()

    def rows(w):
        return w.reshape(-1, P, w.shape[-1]).transpose(1, 0, 2)

    def spread(v):
        return np.broadcast_to(v.reshape(1, -1), (P, v.size))

    def pack(wk, wq, wv, bk, bq, bv, hg, d, rope=False):
        off, wf = pack_offsets(hg, d, rope)
        hs, vw, dt = P // hg, hg * (d + 1), wk.dtype
        out = np.zeros((16 // hg, P, wf), np.float32 if dt == np.float32 else dt)
        swap = np.arange(d) ^ 1
        for g in range(16 // hg):
            for j in range(hg):
                c = slice((g * hg + j) * d, (g * hg + j + 1) * d)
                for name, w, perm in (("wk", wk, None), ("wq", wq, None), ("wks", wk, swap), ("wqs", wq, swap)):
                    if name in off:
                        a0, a1 = off[name]
                        part = w[:, c] if perm is None else w[:, c][:, perm]
                        out[g, :, a0:a1].reshape(P, DC, P)[:, :, j * hs:j * hs + d] = rows(part)
                a0, a1 = off["wv"]
                out[g, :, a0:a1].reshape(P, DC, vw)[:, :, j * (d + 1):j * (d + 1) + d] = rows(wv[:, c])
                kb, qb, vb = off["kb"][0], off["qb"][0], off["vb"][0]
                if bk is not None:
                    out[g, j * hs:j * hs + d, kb] = bk[c]
                    out[g, :, qb + j * hs:qb + j * hs + d] = bq[c]
                    out[g, :, vb + j * (d + 1):vb + j * (d + 1) + d] = bv[c]
                out[g, j * hs + d, kb] = 1.0
                out[g, :, vb + j * (d + 1) + d] = 1.0
                if hs > d + 1:
                    out[g, :, qb + j * hs + d + 1] = 1.0
        return out

    def words(m):
        return np.ascontiguousarray(m).view(np.int32)

    def both_masks(m):
        m = m.view(np.uint8)
        nk = m.shape[2]
        return (m.reshape(B, QT, P, nk).transpose(0, 2, 1, 3).reshape(B, P, QT * nk),
                m.reshape(B, S, nk // P, P).transpose(0, 3, 2, 1).reshape(B, P, nk // P * S))

    def rope_tables():
        inv = (np.float32(1.0) / np.float32(10000.0) ** (np.arange(0, 16, 2, dtype=np.float32) / np.float32(16))).astype(np.float32)
        freq = (np.arange(S, dtype=np.float32)[:, None] * inv[None, :]).astype(np.float32)
        cos, sin = np.zeros((S, P), np.float32), np.zeros((S, P), np.float32)
        for j in range(4):
            for odd in range(2):
                c = slice(32 * j + odd, 32 * j + 16, 2)
                cos[:, c] = np.cos(freq)
                sin[:, c] = np.sin(freq) if odd else -np.sin(freq)
        return cos, sin

    give("x", rows(a["x"].reshape(B * S, D)))
    ctx = a["ctx_1024"]
    give("ctxT", ctx.reshape(B, SK, DC, P).transpose(0, 3, 2, 1))
    for n, m in zip(("m0q", "m0k"), both_masks(a["mask_BxSxS2_bf0"])):
        give(n, words(m))
    for n, m in zip(("m3q", "m3k"), both_masks(a["mask_BxSxS2_bk1"])):
        give(n, words(m))
    later = np.arange(S)[None, :] > np.arange(S)[:, None]
    for n, m in zip(("causal_q", "causal_k"), both_masks(np.broadcast_to(later, (B, S, S)).copy())):
        give(n, words(m))
    give("m6", a["mask_BxS2_ik1"])
    sel = np.zeros((1, P), np.float32)
    sel[0, 17::32] = 1.0
    give("key_sel", sel)
    cos, sin = rope_tables()
    give("rope_k", np.stack([cos.T, sin.T], 1))
    give("rope_q", np.stack([rows(cos), rows(sin)], 1))

    xw = ("Wk", "Wq", "Wv", "bk", "bq", "bv")
    def ones_after(v):
        out = np.zeros((v.shape[0], 16, 17), np.float32)
        out[:, :, :16] = v.reshape(-1, 16, 16)
        return out

    def kqv(name):
        return rows(np.concatenate([a[name + "Wk"], a[name + "Wq"], ones_after(a[name + "Wv"]).reshape(D, -1)], 1))

    def kqv_bias(bk, bq, bv):
        vb = ones_after(bv[None])
        vb[:, :, 16] = 1.0
        return np.concatenate([bk.reshape(2, P).T, spread(bq), spread(vb)], 1)

    give("w0", kqv("L0_xattn_"))
    give("b0", kqv_bias(a["L0_xattn_bk"], a["L0_xattn_bq"], a["L0_xattn_bv"]))
    group_sum = np.zeros((P, 32), np.float32)
    group_sum[np.arange(P), np.arange(P) % 32] = 1.0
    give("group_sum", group_sum)
    give("o0", rows(a["L0_xattn_Wo"]))
    give("ob0", spread(a["L0_xattn_bo"]))
    give("w1", pack(a["L0_attn_kw"], a["L0_attn_qw"], a["L0_attn_vw"], None, None, None, 4, 16, rope=True))
    give("o1", rows(a["L0_attn_ow"]))
    give("w3", pack(*[a["L1_xattn_" + n] for n in xw[:3]], None, None, None, 1, 64))
    give("o3", rows(a["L1_xattn_Wo"]))
    give("ob3", spread(a["L1_xattn_bo"]))
    give("w4", rows(np.concatenate([a["L1_attn_" + n].T for n in ("Wq", "Wk", "Wv")], 1)))
    give("b4", spread(np.concatenate([a["L1_attn_" + n] for n in ("bq", "bk", "bv")])))
    give("o4", rows(a["L1_attn_Wo"].T))
    give("ob4", spread(a["L1_attn_bo"]))
    give("w6", kqv("L2_xattn_"))
    give("b6", kqv_bias(*[np.zeros(D, np.float32)] * 3))
    give("o6", rows(a["L2_xattn_Wo"]))
    w = a["L3_attn_in_proj_weight"]
    give("w10", pack(w[D:2 * D].T, w[:D].T, w[2 * D:].T, None, None, None, 4, 16))
    give("o10", rows(a["L3_attn_out_proj_weight"].T))

    def all_experts(routed, shared):
        w = np.concatenate([routed, shared], 0)
        return w.reshape(len(w), -1, P, w.shape[2]).transpose(0, 2, 1, 3)

    give("descending", spread(np.arange(8, 0, -1).astype(np.float32)))
    give("rw2", rows(a["L0_ffn_router_w"]))
    give("rb2", spread(a["L0_ffn_router_b"]))
    give("e1_2", all_experts(a["L0_ffn_w1"], a["L0_ffn_sw1"]))
    give("e2_2", all_experts(a["L0_ffn_w2"], a["L0_ffn_sw2"]))
    give("b1_2", np.concatenate([a["L0_ffn_b1"], a["L0_ffn_sb1"]]).reshape(10, 4, P).transpose(0, 2, 1))
    give("b2_2", np.concatenate([a["L0_ffn_b2"], a["L0_ffn_sb2"]]))
    give("rw5", rows(a["L1_ffn_router_w"].T))
    give("rb5", spread(a["L1_ffn_experts_bias"]))
    give("e1_5", all_experts(a["L1_ffn_w1"], a["L1_ffn_sw1"]))
    give("e3_5", all_experts(a["L1_ffn_w3"], a["L1_ffn_sw3"]))
    give("e2_5", all_experts(a["L1_ffn_w2"], a["L1_ffn_sw2"]))

    for k in ("k0", "k1", "k2"):
        give(k, words(rows(a["L2_ffn_" + k].view(np.uint8))))
    give("signs_scales", spread(np.stack([a["L2_ffn_s0"], a["L2_ffn_s1"], a["L2_ffn_s2"]])))

    give("ctx", ctx.reshape(B, SK // P, P, D).transpose(0, 2, 1, 3))
    give("w9", rows(a["L3_xattn_W"].T))
    r9 = np.stack([a["L3_xattn_b"], a["L3_xattn_gamma"], a["L3_xattn_beta"]])
    give("r9", np.broadcast_to(r9[None], (P, 3, D)))

    give("w11_1", rows(a["L3_ffn_w1"]))
    give("w11_2", rows(a["L3_ffn_w2"]))
    give("b11_1", a["L3_ffn_b1"].reshape(8, P).T)
    give("b11_2", a["L3_ffn_b2"].reshape(DC, P).T)

    m = {k[8:]: v for k, v in a.items() if k.startswith("L2_attn_")}
    tiles = [m[k].reshape(4, P).T for k in ("b_in", "b_gate", "conv_b", "b_delta", "D_skip")]
    taps = m["conv_w"].reshape(4, P, 4).transpose(1, 0, 2)
    give("s_cols", np.concatenate([np.stack(tiles, 2), taps], 2))
    give("s_win", rows(m["W_in"]))
    give("s_wgate", rows(m["W_gate"]))
    give("s_alog", rows(m["A_log"]))
    give("s_wdelta", rows(m["W_delta"]))
    give("s_wbc", rows(np.concatenate([m["W_B"], m["W_C"]], 1)))
    give("s_wout", rows(m["W_out"]))
    give("s_bout", spread(m["b_out"]))

    out = nc.dram_tensor("out_x", (P, NT, D), F32, kind="ExternalOutput").ap()
    build(nc, dram, out)
    r = run(nc, [arrays], core_ids=[0])
    got = r.results[0]["out_x"]
    return got.transpose(1, 0, 2).reshape(B, S, D)
```

```python
import concourse.bass as bass
import numpy as np
from concourse import mybir
from contextlib import ExitStack, contextmanager

LAYERS = (0, 1, 2, 3, 4, 5, 6, 7, 8, 9, 10, 11)

F32 = mybir.dt.float32
BF16 = mybir.dt.bfloat16
F16 = mybir.dt.float16
U8 = mybir.dt.uint8
I32 = mybir.dt.int32
ALU = mybir.AluOpType
ACT = mybir.ActivationFunctionType
AX = mybir.AxisListType

B, S, D = 2, 256, 256
SK = 4096
P = 128
NT = B * S // P
QT = S // P
DC = D // P
MASKED = -1e30
EPS = 1e-5


class Stage:

    number = 0

    def __init__(self, nc):
        self.nc, self.stack, self.sems = nc, ExitStack(), []

    def own(self, name):
        Stage.number += 1
        return f"{name}_{Stage.number}"

    def __enter__(self):
        self.stack.__enter__()
        return self

    def sb(self, name, shape, dt=F32):
        return self.stack.enter_context(self.nc.sbuf_tensor(self.own(name), shape, dt))

    def ps(self, name, shape, dt=F32):
        return self.stack.enter_context(self.nc.psum_tensor(self.own(name), shape, dt))

    def sem(self, name):
        s = self.nc.alloc_semaphore(self.own(name))
        self.sems.append(s)
        return s

    def __exit__(self, *a):
        r = self.stack.__exit__(*a)
        if a[0] is None:
            self.nc.clear_and_free_semaphores(self.sems)
            self.nc.all_engine_barrier()
        return r


def setup_stage(nc, R, x):
    with Stage(nc) as st:
        loaded, zeroed, made = st.sem("x_loaded"), st.sem("ident_zeroed"), st.sem("ident_made")
        with nc.Block() as block:

            @block.sync
            def _(sp):
                sp.dma_start(R.x[:, :, :], x).then_inc(loaded, 16)
                sp.wait_ge(loaded, 16)

            @block.gpsimd
            def _(pool):
                pool.memset(R.identf[:, :], 0.0).then_inc(zeroed, 1)
                pool.memset(R.onesf[:, :], 1.0).then_inc(zeroed, 1)
                pool.wait_ge(zeroed, 2)
                pool.affine_select(out=R.identf[:, :], in_=R.identf[:, :], compare_op=ALU.not_equal, fill=1.0,
                                   base=0, pattern=[[-1, P]], channel_multiplier=1).then_inc(made, 1)

            @block.vector
            def _(dve):
                dve.wait_ge(made, 1)
                dve.tensor_copy(R.identb[:, :], R.identf[:, :]).then_inc(made, 1)


def norm_stage(nc, R):
    with Stage(nc) as st:
        stats = st.sb("stats", [P, NT, 6])
        mv = st.sb("mean_var", [P, NT, 2])
        rstd = st.sb("rstd", [P, NT])
        tp = st.ps("tp", [P, DC, NT * P])
        done = st.sem("dve_step")
        rooted, normed, turned = st.sem("rooted"), st.sem("normed"), st.sem("turned")
        with nc.Block() as block:

            @block.vector
            def _(dve):
                for t in range(NT):
                    dve.bn_stats(stats[:, t, :], R.x[:, t, :]).then_inc(done, 1)
                for t in range(NT):
                    dve.wait_ge(done, t + 1)
                    dve.bn_aggr(mv[:, t, :], stats[:, t, :]).then_inc(done, 1)
                dve.wait_ge(done, 2 * NT)
                dve.tensor_scalar(rstd[:, :], mv[:, :, 1], EPS, None, ALU.add).then_inc(done, 1)
                dve.wait_ge(rooted, 1)
                dve.reciprocal(rstd[:, :], rstd[:, :]).then_inc(done, 1)
                dve.wait_ge(done, 2 * NT + 2)
                for t in range(NT):
                    dve.tensor_scalar(R.xn[:, t, :], R.x[:, t, :], mv[:, t, 0:1], rstd[:, t:t + 1],
                                      ALU.subtract, ALU.mult).then_inc(normed, 1)
                dve.wait_ge(turned, DC * NT)
                dve.tensor_copy(R.xnT[:, 0, :], tp[:, 0, :])

            @block.scalar
            def _(act):
                act.wait_ge(done, 2 * NT + 1)
                act.activation(rstd[:, :], rstd[:, :], ACT.Sqrt).then_inc(rooted, 1)
                act.wait_ge(turned, DC * NT)
                act.activation(R.xnT[:, 1, :], tp[:, 1, :], ACT.Copy)

            @block.tensor
            def _(pe):
                for t in range(NT):
                    pe.wait_ge(normed, t + 1)
                    for c in range(DC):
                        pe.transpose(tp[:, c, t * P:(t + 1) * P], R.xn[:, t, c * P:(c + 1) * P],
                                     R.identf[:, :]).then_inc(turned, 1)


def add_projected_stage(nc, R, src, width, w, brow):
    C = width // P
    with Stage(nc) as st:
        srcT = st.sb("srcT", [P, C, NT * P])
        wt = st.sb("w_out", [P, C, D], w.dtype)
        wf = st.sb("w_out_f", [P, C, D]) if w.dtype != F32 else wt
        bt = st.sb("b_out", [P, D])
        tp = [st.ps("tp", [P, NT * P]) for _ in range(2)]
        acc = [st.ps("acc", [P, D]) for _ in range(2)]
        loaded, widened, turned, kept = st.sem("w_loaded"), st.sem("w_widened"), st.sem("turned"), st.sem("srcT_kept")
        made, added, added_bias = st.sem("product_made"), st.sem("product_added"), st.sem("bias_added")
        n_loads = 2 if brow is not None else 1
        with nc.Block() as block:

            @block.sync
            def _(sp):
                sp.dma_start(wt[:, :, :], w).then_inc(loaded, 16)
                if brow is not None:
                    sp.dma_start(bt[:, :], brow).then_inc(loaded, 16)

            @block.tensor
            def _(pe):
                for c in range(C):
                    if c >= 2:
                        pe.wait_ge(kept, c - 1)
                    for t in range(NT):
                        last = pe.transpose(tp[c % 2][:, t * P:(t + 1) * P], src[:, t, c * P:(c + 1) * P],
                                            R.identf[:, :])
                    last.then_inc(turned, 1)
                pe.wait_ge(kept, C)
                pe.wait_ge(widened, 1)
                for t in range(NT):
                    if t >= 2:
                        pe.wait_ge(added, t - 1)
                    for c in range(C):
                        last = pe.matmul(acc[t % 2][:, :], srcT[:, c, t * P:(t + 1) * P], wf[:, c, :],
                                         start=(c == 0), stop=(c == C - 1))
                    last.then_inc(made, 1)

            @block.scalar
            def _(act):
                for c in range(C):
                    act.wait_ge(turned, c + 1)
                    act.activation(srcT[:, c, :], tp[c % 2][:, :], ACT.Copy).then_inc(kept, 1)

            @block.vector
            def _(dve):
                dve.wait_ge(loaded, 16 * n_loads)
                if w.dtype != F32:
                    dve.tensor_copy(wf[:, :, :], wt[:, :, :]).then_inc(widened, 1)
                else:
                    dve.engine_nop().then_inc(widened, 1)
                if brow is not None:
                    for t in range(NT):
                        dve.tensor_tensor(R.x[:, t, :], R.x[:, t, :], bt[:, :], ALU.add).then_inc(added_bias, 1)
                for t in range(NT):
                    if brow is not None:
                        dve.wait_ge(added_bias, t + 1)
                    dve.wait_ge(made, t + 1)
                    dve.tensor_tensor(R.x[:, t, :], R.x[:, t, :], acc[t % 2][:, :], ALU.add).then_inc(added, 1)


def self_attention_stage(nc, R, att, w_d, scale, masks, rope=None):
    H, d = 16, 16
    M0, VP, PAIRS, GROUPS = 96, 32, H // 2, H // 4
    narrow = w_d.dtype != F32
    NW = (5 if rope is not None else 3) * D
    with Stage(nc) as st:
        w = st.sb("w_qkv", [P, DC, NW])
        wl = st.sb("w_half", [P, DC, NW], w_d.dtype) if narrow else w
        if rope is not None:
            table = st.sb("rope", [P, QT, 2, D])
            ra, rb = [st.sb("rotated", [P, 2 * D]) for _ in range(2)]
        tok = st.sb("tokT", [P, DC, S])
        qk, rest = st.sb("q_k", [P, 2, QT, D]), st.sb("q_k_rest", [P, 2, QT, D])
        parts = st.sb("parts", [P, 2, QT, H, P], BF16)
        V = st.sb("V", [P, QT, H, VP])
        TT = st.sb("turned", [P, H, 2, S], BF16)
        QE = st.sb("QT_exp", [P, H, S], BF16)
        words = [st.sb("mask_words", [P, QT * S // 4], I32) for _ in range(2)]
        mq, mk = [st.sb("mask_add", [P, QT * S], BF16) for _ in range(2)]
        nm, nr = st.sb("neg_max", [P, H, QT]), st.sb("neg_rest", [P, QT, H])
        PT = [st.sb("probsT", [P, 2 * QT * S]) for _ in range(3)]
        osb, rs = st.sb("groups", [P, 2, S]), st.sb("sum_recip", [P, QT, 4])
        sc = st.ps("scores", [P, 2, 1024])
        tb = st.ps("turning", [P, 2, 512])
        pv = [st.ps("weighted", [P, 512]) for _ in range(2)]

        loaded, mask_loaded, widened, cleared = (st.sem(n) for n in ("loaded", "mask_loaded", "widened", "cleared"))
        v_cleared, mask_ready, src_ready, zeroed = st.sem("v_cleared"), st.sem("mask_ready"), st.sem("src_ready"), st.sem("max_zeroed")
        pj_made, v_kept, pj_kept, rotated = (st.sem(n) for n in ("proj_made", "v_kept", "qk_kept", "rotated"))
        split, spread = st.sem("split_step"), st.sem("parts_spread")
        ta_made, ta_kept, sa_made, max_read, n_step = (st.sem(n) for n in (
            "turned", "turned_kept", "max_scores_made", "max_scores_read", "neg_step"))
        tb_made, qe_kept, sb_made, exp_done, pv_done = (st.sem(n) for n in (
            "max_turned", "QT_exp_kept", "scoresT_made", "exp_done", "weighted_done"))
        o_kept, fin, summed, normed = (st.sem(n) for n in ("groups_kept", "fin", "recip_done", "normalised"))
        n_loads = 2 if rope is not None else 1

        with nc.Block() as block:

            @block.sync
            def _(sp):
                sp.dma_start(wl[:, :, :], w_d).then_inc(loaded, 16)
                if rope is not None:
                    sp.dma_start(table[:, :, :, :], rope).then_inc(loaded, 16)
                for n in range(2):
                    sp.dma_start(words[n][:, :], masks[n][0]).then_inc(mask_loaded, 16)

            @block.gpsimd
            def _(pool):
                pool.memset(V[:, :, :, :], 0.0).then_inc(v_cleared, 1)
                pool.wait_ge(v_cleared, 1)
                pool.memset(V[:, :, :, d:d + 1], 1.0).then_inc(v_cleared, 1)

            @block.tensor
            def _(pe):
                pe.sem_inc(pj_made, 1)
                pe.sem_inc(pv_done, 1)
                pe.sem_inc(fin, 2)
                if narrow:
                    pe.wait_ge(widened, 1)
                pe.wait_ge(loaded, 16 * n_loads)
                pe.wait_ge(mask_ready, 2)
                with pe.Fori(0, B) as b:
                    pe.wait_ge(exp_done, b * PAIRS + 1)
                    pe.wait_ge(qe_kept, b * PAIRS + 1)
                    pe.wait_ge(src_ready, b + 1)
                    for t in range(QT):
                        for c in range(DC):
                            x = tok[:, c, t * P:(t + 1) * P]
                            pe.matmul(sc[:, t, 0:512], x, w[:, c, 0:512], start=(c == 0), stop=(c == DC - 1))
                            if rope is not None:
                                pe.matmul(sc[:, t, 512:1024], x, w[:, c, 512:1024],
                                          start=(c == 0), stop=(c == DC - 1))
                            last = pe.matmul(tb[:, t, 0:D], x, w[:, c, NW - D:NW], start=(c == 0), stop=(c == DC - 1))
                        last.then_inc(pj_made, 1)

                    def turn(u):
                        if u >= 2:
                            pe.wait_ge(ta_kept, b * PAIRS + (u - 1))
                        o = tb[:, u % 2, :].bitcast(BF16)
                        for i in range(2):
                            for a in range(2):
                                for t in range(QT):
                                    n = (i * 2 + a) * QT + t
                                    last = pe.transpose(o[:, n * P:(n + 1) * P], parts[:, a, t, 2 * u + i, :],
                                                        R.identb[:, :])
                        last.then_inc(ta_made, 1)

                    def max_scores(u):
                        pe.wait_ge(ta_kept, b * PAIRS + (u + 1))
                        if u >= 2:
                            pe.wait_ge(max_read, b * PAIRS + (u - 1))
                        for i in range(2):
                            h, bank = 2 * u + i, sc[:, u % 2, i * 512:(i + 1) * 512]
                            pe.matmul(bank, R.identb[:, :], mq[:, :], start=True, stop=False)
                            for q in range(QT):
                                last = pe.matmul(bank[:, q * S:(q + 1) * S], TT[:, h, 0, q * P:(q + 1) * P],
                                                 TT[:, h, 1, :], start=False, stop=(q == QT - 1))
                        last.then_inc(sa_made, 1)

                    pe.wait_ge(split, b * 4 + 4)
                    pe.wait_ge(spread, b + 1)
                    pe.wait_ge(v_kept, b * QT + QT)
                    turn(0)
                    for u in range(PAIRS):
                        if u + 1 < PAIRS:
                            turn(u + 1)
                        max_scores(u)

                    def turn_again(u):
                        if u >= 2:
                            pe.wait_ge(qe_kept, b * PAIRS + (u - 1 + 1))
                        o = tb[:, u % 2, :].bitcast(BF16)
                        for i in range(2):
                            for t in range(QT):
                                n = i * QT + t
                                last = pe.transpose(o[:, n * P:(n + 1) * P], parts[:, 0, t, 2 * u + i, :],
                                                    R.identb[:, :])
                        last.then_inc(tb_made, 1)

                    def weigh(u):
                        pe.wait_ge(exp_done, b * PAIRS + (u + 1 + 1))
                        if u % 2 == 0:
                            pe.wait_ge(normed, b * GROUPS + (u // 2 - 1 + 2))
                        for i in range(2):
                            j = u % 2 * 2 + i
                            for kt in range(QT):
                                n = i * QT + kt
                                last = pe.matmul(pv[u // 2 % 2][j * VP:(j + 1) * VP, 0:S], V[:, kt, 2 * u + i, :],
                                                 PT[u % 3][:, n * S:(n + 1) * S], start=(kt == 0), stop=(kt == QT - 1))
                        last.then_inc(pv_done, 1)

                    def turn_weighted(g):
                        pe.wait_ge(o_kept, b * GROUPS + (g + 1))
                        for q in range(QT):
                            last = pe.transpose(pv[g % 2][:, S + q * P:S + (q + 1) * P],
                                                osb[:, g % 2, q * P:(q + 1) * P], R.identf[:, :])
                        last.then_inc(fin, 1)

                    pe.wait_ge(n_step, b * 4 + (4 + 1))
                    pe.wait_ge(ta_kept, b * PAIRS + PAIRS)
                    pe.wait_ge(max_read, b * PAIRS + PAIRS)
                    turn_again(0)
                    turn_again(1)
                    for u in range(PAIRS):
                        pe.wait_ge(qe_kept, b * PAIRS + (u + 1 + 1))
                        if u >= 2:
                            pe.wait_ge(exp_done, b * PAIRS + (u - 1 + 1))
                        for i in range(2):
                            h, bank = 2 * u + i, sc[:, u % 2, i * 512:(i + 1) * 512]
                            pe.matmul(bank, R.identb[:, :], mk[:, :], start=True, stop=False)
                            for kt in range(QT):
                                last = pe.matmul(bank[:, kt * S:(kt + 1) * S], TT[:, h, 1, kt * P:(kt + 1) * P],
                                                 QE[:, h, :], start=False, stop=(kt == QT - 1))
                        last.then_inc(sb_made, 1)
                        if u % 2 and u >= 3:
                            turn_weighted((u - 3) // 2)
                        if u + 2 < PAIRS:
                            turn_again(u + 2)
                        if u >= 1:
                            weigh(u - 1)
                    weigh(PAIRS - 1)
                    turn_weighted(GROUPS - 1)

            @block.scalar
            def _(act):
                act.sem_inc(exp_done, 1)
                act.wait_ge(v_cleared, 2)
                with act.Fori(0, B) as b:
                    for t in range(QT):
                        act.wait_ge(pj_made, b * QT + (t + 1 + 1))
                        act.activation(V[:, t, :, 0:d], tb[:, t, 0:D].rearrange("p (h w) -> p h w", h=H), ACT.Copy)\
                           .then_inc(v_kept, 1)

                    def block_of(a, i):
                        return parts[:, a, :, :, i * d:(i + 1) * d]

                    act.wait_ge(split, b * 4 + 1)
                    for a, to, frm in ((1, 3, 0), (1, 4, 0), (0, 1, 0), (0, 2, 0), (1, 1, 5), (0, 3, 5)):
                        if (a, to) == (1, 1):
                            act.wait_ge(split, b * 4 + 3)
                        last = act.activation(block_of(a, to), block_of(a, frm), ACT.Copy)
                    last.then_inc(spread, 1)
                    for u in range(PAIRS):
                        act.wait_ge(ta_made, b * PAIRS + (u + 1))
                        act.activation(TT[:, 2 * u:2 * u + 2, :, :].rearrange("p h a s -> p (h a s)"),
                                       tb[:, u % 2, :].bitcast(BF16), ACT.Copy).then_inc(ta_kept, 1)

                    def keep_groups(g):
                        act.wait_ge(pv_done, b * PAIRS + (2 * g + 2 + 1))
                        act.wait_ge(fin, b * GROUPS + (g - 1 + 2))
                        act.activation(osb[:, g % 2, :], pv[g % 2][:, 0:S], ACT.Copy).then_inc(o_kept, 1)

                    for u in range(PAIRS):
                        act.wait_ge(sb_made, b * PAIRS + (u + 1))
                        act.wait_ge(pv_done, b * PAIRS + (max(u - 2, 0) + 1))
                        act.activation(PT[u % 3][:, :], sc[:, u % 2, :], ACT.Exp, scale=scale).then_inc(exp_done, 1)
                        if u % 2 == 0 and u >= 2:
                            keep_groups(u // 2 - 1)
                    keep_groups(GROUPS - 1)

            @block.vector
            def _(dve):
                dve.sem_inc(qe_kept, 1)
                dve.sem_inc(n_step, 1)
                dve.sem_inc(normed, 2)
                dve.memset(parts[:, :, :, :, :], 0.0).then_inc(cleared, 1)
                dve.wait_ge(cleared, 1)
                dve.memset(parts[:, 1, :, :, M0:M0 + 3], 1.0).then_inc(cleared, 1)
                dve.wait_ge(mask_loaded, 32)
                for src, add in zip(words, (mq, mk)):
                    dve.tensor_scalar(add[:, :], src[:, :].bitcast(U8), MASKED, None, ALU.mult).then_inc(mask_ready, 1)
                dve.wait_ge(loaded, 16 * n_loads)
                if narrow:
                    dve.tensor_copy(w[:, :, :], wl[:, :, :]).then_inc(widened, 1)
                dve.wait_ge(cleared, 2)
                with dve.Fori(0, B) as b:
                    dve.wait_ge(pj_made, b * QT + 1)
                    dve.tensor_copy(tok[:, :, :], R.xnT[:, :, bass.ds(b * S, S)]).then_inc(src_ready, 1)
                    dve.wait_ge(n_step, b * 4 + 1)
                    dve.memset(parts[:, 0, :, :, M0:M0 + 3], 0.0).then_inc(zeroed, 1)
                    for t in range(QT):
                        dve.wait_ge(pj_made, b * QT + (t + 1 + 1))
                        both = sc[:, t, 0:512].rearrange("p (a f) -> p a f", a=2)
                        if rope is None:
                            dve.tensor_copy(qk[:, :, t, :], both).then_inc(pj_kept, 1)
                        else:
                            swapped = sc[:, t, 512:1024].rearrange("p (a f) -> p a f", a=2)
                            a3, b3 = (r[:, :].rearrange("p (a f) -> p a f", a=2) for r in (ra, rb))
                            cos, sin = (table[:, t, n, :].unsqueeze(1).broadcast_to([P, 2, D]) for n in range(2))
                            if t:
                                dve.wait_ge(pj_kept, b * QT + t)
                            dve.tensor_tensor(a3, both, cos, ALU.mult).then_inc(rotated, 1)
                            dve.tensor_tensor(b3, swapped, sin, ALU.mult).then_inc(rotated, 1)
                            dve.wait_ge(rotated, b * (2 * QT) + (2 * t + 2))
                            dve.tensor_tensor(qk[:, :, t, :], a3, b3, ALU.add).then_inc(pj_kept, 1)

                    def four(x):
                        return x.rearrange("p a t (h f) -> p (a t) h f", h=H)

                    def blocks(i):
                        return parts[:, :, :, :, i * d:(i + 1) * d].rearrange("p a t h f -> p (a t) h f")

                    def rows_of(a, x):
                        return x[:, a, :, :].rearrange("p t (h f) -> p t h f", h=H)

                    dve.wait_ge(pj_kept, b * QT + QT)
                    dve.tensor_copy(blocks(0), four(qk[:, :, :, :])).then_inc(split, 1)
                    dve.wait_ge(split, b * 4 + 1)
                    dve.tensor_tensor(four(rest[:, :, :, :]), four(qk[:, :, :, :]), blocks(0), ALU.subtract)\
                       .then_inc(split, 1)
                    dve.wait_ge(split, b * 4 + 2)
                    dve.tensor_copy(blocks(5), four(rest[:, :, :, :])).then_inc(split, 1)
                    dve.wait_ge(split, b * 4 + 3)
                    for a, i in ((0, 4), (1, 2)):
                        last = dve.tensor_tensor(parts[:, a, :, :, i * d:(i + 1) * d], rows_of(a, rest),
                                                 parts[:, a, :, :, 5 * d:6 * d], ALU.subtract)
                    last.then_inc(split, 1)
                    for u in range(PAIRS):
                        dve.wait_ge(sa_made, b * PAIRS + (u + 1))
                        dve.tensor_reduce(nm[:, 2 * u:2 * u + 2, :], sc[:, u % 2, :].rearrange(
                            "p (h q k) -> p h q k", h=2, q=QT), AX.X, ALU.max, negate=True).then_inc(max_read, 1)
                    part = [parts[:, 0, :, :, M0 + i] for i in range(3)]
                    nmt = nm[:, :, :].rearrange("p h q -> p q h")
                    dve.wait_ge(max_read, b * PAIRS + PAIRS)
                    dve.wait_ge(zeroed, b + 1)
                    dve.tensor_copy(part[0], nmt).then_inc(n_step, 1)
                    dve.wait_ge(n_step, b * 4 + (1 + 1))
                    dve.tensor_tensor(nr[:, :, :], nmt, part[0], ALU.subtract).then_inc(n_step, 1)
                    dve.wait_ge(n_step, b * 4 + (2 + 1))
                    dve.tensor_copy(part[1], nr[:, :, :]).then_inc(n_step, 1)
                    dve.wait_ge(n_step, b * 4 + (3 + 1))
                    dve.tensor_tensor(part[2], nr[:, :, :], part[1], ALU.subtract).then_inc(n_step, 1)

                    def keep_turned(u):
                        dve.wait_ge(tb_made, b * PAIRS + (u + 1))
                        dve.tensor_copy(QE[:, 2 * u:2 * u + 2, :].rearrange("p h s -> p (h s)"),
                                        tb[:, u % 2, 0:S].bitcast(BF16)).then_inc(qe_kept, 1)

                    def normalise(g):
                        both = pv[g % 2][:, S:2 * S].rearrange("p (q j w) -> p q j w", q=QT, j=4)
                        dve.wait_ge(fin, b * GROUPS + (g + 1 + 2))
                        dve.wait_ge(normed, b * GROUPS + (g + 2))
                        dve.reciprocal(rs[:, :, :], both[:, :, :, d]).then_inc(summed, 1)
                        dve.wait_ge(summed, b * GROUPS + (g + 1))
                        for q in range(QT):
                            o = att[:, bass.ds(b * QT + q, 1), 4 * g * d:4 * (g + 1) * d]
                            ins = dve.tensor_tensor(o.rearrange("p o (j w) -> p (o j) w", j=4), both[:, q, :, 0:d],
                                                    rs[:, q, :].unsqueeze(2).broadcast_to([P, 4, d]), ALU.mult)
                        ins.then_inc(normed, 1)

                    keep_turned(0)
                    keep_turned(1)
                    for u in range(PAIRS):
                        if u % 2 and u >= 3:
                            normalise((u - 3) // 2)
                        if u + 2 < PAIRS:
                            keep_turned(u + 2)
                    normalise(GROUPS - 1)


def head_mix_stage(nc, R, dram, scratch):
    H, d = 16, 16
    with Stage(nc) as st:
        w = st.sb("w_qkv", [P, DC, 3 * D])
        bias = st.sb("b_qkv", [P, 3 * D])
        qkv = [st.sb("qkv", [P, 3 * D]) for _ in range(2)]
        prod = st.sb("products", [P, H, H, d])
        sc = st.sb("scores", [P, H, H])
        ex = st.sb("exps", [P, H, H])
        mx, sm = st.sb("max", [P, H]), st.sb("sum", [P, H])
        o = [st.sb("mixed", [P, H, d]) for _ in range(2)]
        ps = [st.ps("qkv_ps", [P, 2, 512]) for _ in range(2)]
        loaded, made, kept, step = st.sem("w_loaded"), st.sem("qkv_made"), st.sem("qkv_kept"), st.sem("dve_step")
        shifted, exped, mixed = st.sem("shifted"), st.sem("exp_done"), st.sem("mixed")
        stored = [st.sem("stored") for _ in range(2)]
        with nc.Block() as block:

            @block.sync
            def _(sp):
                sp.dma_start(w[:, :, :], dram["w4"]).then_inc(loaded, 16)
                sp.dma_start(bias[:, :], dram["b4"]).then_inc(loaded, 16)
                for t in range(NT):
                    b, q = t // QT, t % QT
                    sp.wait_ge(mixed, t + 1)
                    sp.dma_start(scratch[b, :, q * P:(q + 1) * P, :].rearrange("h s d -> s h d"),
                                 o[t % 2][:, :, :]).then_inc(stored[t % 2], 16)
                for s in stored:
                    sp.wait_ge(s, 16 * NT // 2)

            @block.tensor
            def _(pe):
                pe.wait_ge(loaded, 32)
                for t in range(NT):
                    if t >= 2:
                        pe.wait_ge(kept, t - 1)
                    for h, (c0, c1) in enumerate(((0, 512), (512, 768))):
                        for c in range(DC):
                            last = pe.matmul(ps[t % 2][:, h, 0:c1 - c0], R.xnT[:, c, t * P:(t + 1) * P],
                                             w[:, c, c0:c1], start=(c == 0), stop=(c == DC - 1))
                    last.then_inc(made, 1)

            @block.scalar
            def _(act):
                for t in range(NT):
                    act.wait_ge(shifted, t + 1)
                    act.activation(ex[:, :, :], sc[:, :, :], ACT.Exp, scale=0.25).then_inc(exped, 1)

            @block.vector
            def _(dve):
                dve.wait_ge(loaded, 32)
                n = 0
                for t in range(NT):
                    a = qkv[t % 2]
                    dve.wait_ge(made, t + 1)
                    flat = ps[t % 2][:, :, :].rearrange("p a b -> p (a b)")[:, 0:3 * D]
                    dve.tensor_tensor(a[:, :], flat, bias[:, :], ALU.add).then_inc(kept, 1)
                    q, k, v = (a[:, i * D:(i + 1) * D].rearrange("p (h d) -> p h d", h=H) for i in range(3))
                    dve.wait_ge(kept, t + 1)
                    dve.tensor_tensor(prod[:, :, :, :], q.unsqueeze(2).broadcast_to([P, H, H, d]),
                                      k.unsqueeze(1).broadcast_to([P, H, H, d]), ALU.mult).then_inc(step, 1)
                    dve.wait_ge(step, n + 1)
                    dve.tensor_reduce(sc[:, :, :], prod[:, :, :, :], AX.X, ALU.add).then_inc(step, 1)
                    dve.wait_ge(step, n + 2)
                    dve.tensor_reduce(mx[:, :], sc[:, :, :], AX.X, ALU.max).then_inc(step, 1)
                    dve.wait_ge(step, n + 3)
                    dve.tensor_tensor(sc[:, :, :], sc[:, :, :], mx[:, :].unsqueeze(2).broadcast_to([P, H, H]),
                                      ALU.subtract).then_inc(shifted, 1)
                    dve.wait_ge(exped, t + 1)
                    dve.tensor_reduce(sm[:, :], ex[:, :, :], AX.X, ALU.add).then_inc(step, 1)
                    dve.tensor_tensor(prod[:, :, :, :], ex[:, :, :].unsqueeze(2).broadcast_to([P, H, d, H]),
                                      v.rearrange("p h d -> p d h").unsqueeze(1).broadcast_to([P, H, d, H]),
                                      ALU.mult).then_inc(step, 1)
                    dve.wait_ge(step, n + 5)
                    dve.reciprocal(sm[:, :], sm[:, :]).then_inc(step, 1)
                    if t >= 2:
                        dve.wait_ge(stored[t % 2], 16 * (t // 2))
                    dve.tensor_reduce(o[t % 2][:, :, :], prod[:, :, :, :], AX.X, ALU.add).then_inc(step, 1)
                    n += 7
                    dve.wait_ge(step, n)
                    dve.tensor_tensor(o[t % 2][:, :, :], o[t % 2][:, :, :],
                                      sm[:, :].unsqueeze(2).broadcast_to([P, H, d]), ALU.mult).then_inc(mixed, 1)


def reload_stage(nc, att, scratch):
    with Stage(nc) as st:
        loaded = st.sem("reloaded")
        with nc.Block() as block:

            @block.sync
            def _(sp):
                flat = scratch.rearrange("b h s d -> (b h s d)").rearrange("(t p m) -> p t m", p=P, m=D)
                sp.dma_start(att[:, :, :], flat).then_inc(loaded, 16)
                sp.wait_ge(loaded, 16)


def experts_stage(nc, R, dram, layer, E, func, shared_weight):
    NE, HT = 8, 4
    gated = layer == 5
    rw_d, rb_d = dram[f"rw{layer}"], dram[f"rb{layer}"]
    w1_d, w2_d = dram[f"e1_{layer}"], dram[f"e2_{layer}"]
    with Stage(nc) as st:
        rw, rb, desc = st.sb("router_w", [P, DC, NE]), st.sb("router_b", [P, NE]), st.sb("descending", [P, NE])
        lg, l2, tmp = st.sb("logits", [P, NT, NE]), st.sb("logits2", [P, NT, NE]), st.sb("tie", [P, NT, NE])
        one = [st.sb("one_hot", [P, NT, NE]) for _ in range(2)]
        top = [st.sb("top", [P, NT]) for _ in range(2)]
        tie = st.sb("tie_max", [P, NT])
        pr = [st.sb("prob", [P, NT]) for _ in range(2)]
        comb = st.sb("weights", [P, NT, E])
        cur = [st.sb("weight_now", [P, NT]) for _ in range(2)]
        w1, w2 = st.sb("w1", [P, DC, HT * P]), st.sb("w2", [P, HT, D])
        w3 = st.sb("w3", [P, DC, HT * P]) if gated else None
        b1 = None if gated else st.sb("b1", [P, HT])
        hs = [st.sb("h_silu", [P, NT * P]) for _ in range(2)] if gated else None
        hT = st.sb("hT", [P, HT, NT * P])
        h_ps = [st.ps("h_ps", [P, NT * P]) for _ in range(2)]
        u_ps = [st.ps("u_ps", [P, NT * P]) for _ in range(2)] if gated else None
        y_ps = [st.ps("y_ps", [P, 512]) for _ in range(2)]
        r_ps = st.ps("router_ps", [P, NT, NE])
        if not gated:
            b2, combT = st.sb("b2", [E, D]), st.sb("weightsT", [E, NT * P])
            c_ps = st.ps("weightsT_ps", [E, NT * P])
        r_loaded, routed, step, e2s = st.sem("router_loaded"), st.sem("routed"), st.sem("dve_step"), st.sem("exp_done")
        turned, bias_made = st.sem("turned"), st.sem("bias_made")
        w1_loaded, w2_loaded = st.sem("w1_loaded"), st.sem("w2_loaded")
        h_made, silu_done, h_kept = st.sem("h_made"), st.sem("silu_done"), st.sem("h_kept")
        y_made, y_added, cur_ready = st.sem("y_made"), st.sem("y_added"), st.sem("weight_ready")
        own = st.sem("routing_step")
        NL1 = 2
        NR = 3 if gated else 4
        YB = 0 if gated else NT

        with nc.Block() as block:

            @block.sync
            def _(sp):
                sp.dma_start(rw[:, :, :], rw_d).then_inc(r_loaded, 16)
                sp.dma_start(rb[:, :], rb_d).then_inc(r_loaded, 16)
                sp.dma_start(desc[:, :], dram["descending"]).then_inc(r_loaded, 16)
                if not gated:
                    sp.dma_start(b2[:, :], dram["b2_2"]).then_inc(r_loaded, 16)

            @block.gpsimd
            def _(pool):
                with pool.Fori(0, E) as e:
                    pool.wait_ge(h_kept, e * HT + 1)
                    pool.dma_start(w1[:, :, :], w1_d[bass.ds(e, 1)].rearrange("o p c h -> (o p) c h"))\
                        .then_inc(w1_loaded, 16)
                    if gated:
                        pool.dma_start(w3[:, :, :], dram["e3_5"][bass.ds(e, 1)].rearrange("o p c h -> (o p) c h"))\
                            .then_inc(w1_loaded, 16)
                    else:
                        pool.dma_start(b1[:, :], dram["b1_2"][bass.ds(e, 1)].rearrange("o p h -> (o p) h"))\
                            .then_inc(w1_loaded, 16)

            @block.tensor
            def _(pe):
                pe.sem_inc(y_made, 1)
                pe.wait_ge(r_loaded, 16 * NR)
                for t in range(NT):
                    for c in range(DC):
                        last = pe.matmul(r_ps[:, t, :], R.xnT[:, c, t * P:(t + 1) * P], rw[:, c, :],
                                         start=(c == 0), stop=(c == DC - 1))
                last.then_inc(turned, 1)
                if not gated:
                    pe.wait_ge(routed, 1)
                    for t in range(NT):
                        last = pe.transpose(c_ps[:, t * P:(t + 1) * P], comb[:, t, :], R.identf[:, :])
                    last.then_inc(turned, 1)
                    pe.wait_ge(bias_made, 1)
                    for t in range(NT):
                        if t >= 2:
                            pe.wait_ge(y_added, t)
                        pe.matmul(y_ps[t % 2][:, 0:D], combT[:, t * P:(t + 1) * P], b2[:, :],
                                  start=True, stop=True).then_inc(turned, 1)
                with pe.Fori(0, E) as e:
                    pe.wait_ge(w1_loaded, e * (16 * NL1) + 16 * NL1)
                    for f in range(HT):
                        if f >= 2:
                            pe.wait_ge(h_kept, e * HT + f)
                        else:
                            pe.wait_ge(h_kept, e * HT + 1)
                        for w, ps in ((w1, h_ps), (w3, u_ps)):
                            if w is not None:
                                for c in range(DC):
                                    last = pe.matmul(ps[f % 2][:, :], w[:, c, f * P:(f + 1) * P], R.xnT[:, c, :],
                                                     start=(c == 0), stop=(c == DC - 1))
                        last.then_inc(h_made, 1)
                    pe.wait_ge(h_kept, e * HT + HT + 1)
                    pe.wait_ge(w2_loaded, e * 16 + 16)
                    for t in range(NT):
                        pe.wait_ge(y_added, e * NT + (YB + 1 + max(t - 1, 0)))
                        for f in range(HT):
                            last = pe.matmul(y_ps[t % 2][:, 0:D], hT[:, f, t * P:(t + 1) * P], w2[:, f, :],
                                             start=(f == 0), stop=(f == HT - 1))
                        last.then_inc(y_made, 1)

            @block.scalar
            def _(act):
                act.wait_ge(step, 1)
                act.activation(pr[1][:, :], pr[1][:, :], ACT.Exp).then_inc(e2s, 1)
                if not gated:
                    act.sem_inc(h_kept, 1)
                    act.wait_ge(turned, 2)
                    act.activation(combT[:, :], c_ps[:, :], ACT.Copy).then_inc(bias_made, 1)
                with act.Fori(0, E) as e:
                    act.wait_ge(y_made, e * NT + 1)
                    act.dma_start(w2[:, :, :], w2_d[bass.ds(e, 1)].rearrange("o p h m -> (o p) h m"))\
                       .then_inc(w2_loaded, 16)
                    for f in range(HT):
                        act.wait_ge(h_made, e * HT + (f + 1))
                        if gated:
                            act.wait_ge(h_kept, e * HT + max(f - 1, 0) + 1)
                            act.activation(hs[f % 2][:, :], h_ps[f % 2][:, :], func).then_inc(silu_done, 1)
                        else:
                            act.wait_ge(y_made, e * NT + 1)
                            act.activation(hT[:, f, :], h_ps[f % 2][:, :], func, bias=b1[:, f:f + 1])\
                               .then_inc(h_kept, 1)

            @block.vector
            def _(dve):
                dve.sem_inc(y_added, 1)
                dve.sem_inc(cur_ready, 1)
                if gated:
                    dve.sem_inc(h_kept, 1)

                def over(v):
                    return v[:, :].unsqueeze(2).broadcast_to([P, NT, NE])

                def row(v):
                    return v[:, :].unsqueeze(1).broadcast_to([P, NT, NE])

                n = 0
                dve.wait_ge(r_loaded, 16 * NR)
                dve.wait_ge(turned, 1)
                dve.tensor_tensor(lg[:, :, :], r_ps[:, :, :], row(rb), ALU.add).then_inc(own, 1)
                for k, src in enumerate((lg, l2)):
                    n += 1
                    dve.wait_ge(own, n)
                    dve.tensor_reduce(top[k][:, :], src[:, :, :], AX.X, ALU.max).then_inc(own, 1)
                    n += 1
                    dve.wait_ge(own, n)
                    dve.tensor_tensor(tmp[:, :, :], src[:, :, :], over(top[k]), ALU.is_equal).then_inc(own, 1)
                    n += 1
                    dve.wait_ge(own, n)
                    dve.tensor_tensor(tmp[:, :, :], tmp[:, :, :], row(desc), ALU.mult).then_inc(own, 1)
                    n += 1
                    dve.wait_ge(own, n)
                    dve.tensor_reduce(tie[:, :], tmp[:, :, :], AX.X, ALU.max).then_inc(own, 1)
                    n += 1
                    dve.wait_ge(own, n)
                    dve.tensor_tensor(one[k][:, :, :], tmp[:, :, :], over(tie), ALU.is_equal).then_inc(own, 1)
                    if k == 0:
                        n += 1
                        dve.wait_ge(own, n)
                        dve.scalar_tensor_tensor(out=l2[:, :, :].rearrange("p t e -> p (t e)"),
                                                 in0=one[0][:, :, :].rearrange("p t e -> p (t e)"), scalar=MASKED,
                                                 in1=lg[:, :, :].rearrange("p t e -> p (t e)"),
                                                 op0=ALU.mult, op1=ALU.add).then_inc(own, 1)
                dve.tensor_tensor(pr[1][:, :], top[1][:, :], top[0][:, :], ALU.subtract).then_inc(step, 1)
                dve.wait_ge(e2s, 1)
                dve.tensor_scalar(pr[0][:, :], pr[1][:, :], 1.0, None, ALU.add).then_inc(own, 1)
                n += 2
                dve.wait_ge(own, n)
                dve.reciprocal(pr[0][:, :], pr[0][:, :]).then_inc(own, 1)
                n += 1
                dve.wait_ge(own, n)
                dve.tensor_tensor(pr[1][:, :], pr[1][:, :], pr[0][:, :], ALU.mult).then_inc(own, 1)
                dve.tensor_tensor(one[0][:, :, :], one[0][:, :, :], over(pr[0]), ALU.mult).then_inc(own, 1)
                n += 2
                dve.wait_ge(own, n)
                dve.tensor_tensor(one[1][:, :, :], one[1][:, :, :], over(pr[1]), ALU.mult).then_inc(own, 1)
                dve.memset(comb[:, :, NE:E], shared_weight).then_inc(own, 1)
                n += 2
                dve.wait_ge(own, n)
                dve.tensor_tensor(comb[:, :, 0:NE], one[0][:, :, :], one[1][:, :, :], ALU.add).then_inc(routed, 1)
                if not gated:
                    for t in range(NT):
                        dve.wait_ge(turned, 3 + t)
                        dve.tensor_tensor(R.x[:, t, :], R.x[:, t, :], y_ps[t % 2][:, 0:D], ALU.add)\
                           .then_inc(y_added, 1)
                dve.wait_ge(routed, 1)
                with dve.Fori(0, E) as e:
                    if gated:
                        for f in range(HT):
                            dve.wait_ge(silu_done, e * HT + (f + 1))
                            dve.tensor_tensor(hT[:, f, :], hs[f % 2][:, :], u_ps[f % 2][:, :], ALU.mult)\
                               .then_inc(h_kept, 1)
                    dve.wait_ge(y_added, e * NT + (YB + 1))
                    dve.tensor_copy(cur[0][:, :], comb[:, :, bass.ds(e, 1)].rearrange("p t o -> p (t o)"))\
                       .then_inc(cur_ready, 1)
                    dve.wait_ge(cur_ready, e + 2)
                    for t in range(NT):
                        dve.wait_ge(y_made, e * NT + (t + 2))
                        dve.scalar_tensor_tensor(out=R.x[:, t, :], in0=y_ps[t % 2][:, 0:D], scalar=cur[0][:, t:t + 1],
                                                 in1=R.x[:, t, :], op0=ALU.mult, op1=ALU.add).then_inc(y_added, 1)


def signs_stage(nc, R, dram):
    HT = 8
    with Stage(nc) as st:
        k0 = st.sb("k0_words", [P, 2 * DC, HT * P // 4], I32)
        k1 = st.sb("k1_words", [P, HT, HT * P // 4], I32)
        k2 = st.sb("k2_words", [P, HT, D // 4], I32)
        w0 = st.sb("w0", [P, DC, HT * P])
        w1 = st.sb("w1", [P, HT, HT * P])
        w2 = st.sb("w2", [P, HT, D])
        sc = st.sb("scales", [P, 3])
        h1, h2 = st.sb("h1T", [P, HT, NT * P]), st.sb("h2T", [P, HT, NT * P])
        ps = [st.ps("h_ps", [P, NT * P]) for _ in range(4)]
        y_ps = [st.ps("y_ps", [P, 512]) for _ in range(2)]
        loaded, widened, made, kept = st.sem("loaded"), st.sem("widened"), st.sem("h_made"), st.sem("h_kept")
        y_made, y_added, differed = st.sem("y_made"), st.sem("y_added"), st.sem("differed")
        with nc.Block() as block:

            @block.sync
            def _(sp):
                sp.dma_start(k0[:, :, :], dram["k0"]).then_inc(loaded, 16)
                sp.dma_start(sc[:, :], dram["signs_scales"]).then_inc(loaded, 16)
                sp.dma_start(k1[:, :, :], dram["k1"]).then_inc(loaded, 16)
                sp.dma_start(k2[:, :, :], dram["k2"]).then_inc(loaded, 16)

            @block.vector
            def _(dve):
                dve.wait_ge(loaded, 64)
                a = k0[:, :, :].bitcast(U8)
                dve.tensor_tensor(w0[:, :, :], a[:, 0:DC, :], a[:, DC:2 * DC, :], ALU.subtract).then_inc(differed, 1)
                dve.wait_ge(differed, 1)
                dve.tensor_scalar(w0[:, :, :], w0[:, :, :], 4.0, None, ALU.mult).then_inc(widened, 1)
                dve.tensor_scalar(w1[:, :, :], k1[:, :, :].bitcast(U8), 4.0, -2.0, ALU.mult, ALU.add)\
                   .then_inc(widened, 1)
                dve.tensor_scalar(w2[:, :, :], k2[:, :, :].bitcast(U8), 2.0, -1.0, ALU.mult, ALU.add)\
                   .then_inc(widened, 1)
                for t in range(NT):
                    dve.wait_ge(y_made, t + 1)
                    dve.scalar_tensor_tensor(out=R.x[:, t, :], in0=y_ps[t % 2][:, 0:D], scalar=sc[:, 2:3],
                                             in1=R.x[:, t, :], op0=ALU.mult, op1=ALU.add).then_inc(y_added, 1)

            @block.tensor
            def _(pe):
                n = 0
                for w, src, C, ready in ((w0, R.xnT, DC, 1), (w1, h1, HT, 2)):
                    pe.wait_ge(widened, ready)
                    for f in range(HT):
                        if n >= 4:
                            pe.wait_ge(kept, n - 3)
                        if C == HT and f == 0:
                            pe.wait_ge(kept, HT)
                        for c in range(C):
                            last = pe.matmul(ps[n % 4][:, :], w[:, c, f * P:(f + 1) * P], src[:, c, :],
                                             start=(c == 0), stop=(c == C - 1))
                        last.then_inc(made, 1)
                        n += 1
                pe.wait_ge(widened, 3)
                pe.wait_ge(kept, 2 * HT)
                for t in range(NT):
                    if t >= 2:
                        pe.wait_ge(y_added, t - 1)
                    for c in range(HT):
                        last = pe.matmul(y_ps[t % 2][:, 0:D], h2[:, c, t * P:(t + 1) * P], w2[:, c, :],
                                         start=(c == 0), stop=(c == HT - 1))
                    last.then_inc(y_made, 1)

            @block.scalar
            def _(act):
                act.wait_ge(loaded, 64)
                for n in range(2 * HT):
                    act.wait_ge(made, n + 1)
                    h = h1 if n < HT else h2
                    act.activation(h[:, n % HT, :], ps[n % 4][:, :], ACT.Relu,
                                   scale=sc[:, n // HT:n // HT + 1]).then_inc(kept, 1)


def split_context_stage(nc, R, att, w, scale, ctxT, parts_d, masks=None, key_mask=None):
    H, d = 16, 16
    VW = d + 1
    XR, M0, MASKROW = 100, 96, 99
    NKT, KC = SK // P, SK // 512
    HG = D // P
    EU, EK = 8, 4
    MU = QT * KC
    NX = 4
    TURNS = H // NX
    WHEN = (2, 3, 3, 2, 2, 2, 2, 0)
    PRO = HG * KC + NKT + QT
    TURN = 4
    CLEARED = 2 + NX + 1 + (key_mask is not None)
    with Stage(nc) as st:
        cx = st.sb("ctxT", [P, DC, SK])
        ws = st.sb("w_kqv", [P, DC, D + D + H * VW])
        bs = st.sb("biases", [P, HG + D + H * VW])
        qsrc = st.sb("qsrc", [P, DC, S])
        kst = st.sb("key_parts", [P, 3, SK], BF16)
        kr = [st.sb("key_rest", [P, 512]) for _ in range(2)]
        V = st.sb("V", [P, NKT, H, VW])
        qf, qr = (cx[:, 1, i * QT * D:(i + 1) * QT * D].rearrange("p (q f) -> p q f", q=QT) for i in range(2))
        Q = st.sb("Q_all", [P, QT, H, P], BF16)
        X = [st.sb("X", [XR, SK], BF16) for _ in range(NX)]
        Vh = [st.sb("V_head", [P, NKT, 32]) for _ in range(2)]
        Qh = [st.sb("Q_head", [P, QT, P], BF16) for _ in range(2)]
        Qm = [st.sb("QT_max", [P, S], BF16) for _ in range(2)]
        Qe = [st.sb("QT_exp", [P, S], BF16) for _ in range(2)]
        PT = [cx[:, 0, i * EK * S:(i + 1) * EK * S] for i in range(4)]
        mx, nm, nr = st.sb("max_parts", [P, QT, KC]), st.sb("neg_max", [P, QT]), st.sb("neg_rest", [P, QT])
        osb = st.sb("groups", [P, S])
        rs = st.sb("sum_recip", [P, QT])
        sel = st.sb("group_sum", [P, 32])
        mb = st.ps("max_scores", [P, 2, 512])
        sT = st.ps("scoresT", [P, 2, EK * S])
        pb = [st.ps("weighted", [P, 512]) for _ in range(2)]
        if masks is not None:
            xn = R.xn[:, :, :].rearrange("p t f -> p (t f)")
            words = [xn[:, i * 512:(i + 1) * 512].bitcast(I32) for i in range(2)]
            junk = [xn[:, i * 256:(i + 1) * 256].bitcast(BF16) for i in range(4)]
            mq, mk = [st.sb("mask_add", [P, QT * SK], BF16) for _ in range(2)]
        if key_mask is not None:
            km, kadd = st.sb("key_mask", [1, SK], I32), st.sb("key_add", [1, SK], BF16)

        w_loaded = st.sem("w_loaded")
        ctx_loaded = [st.sem("ctx_loaded") for _ in range(4)]
        mask_loaded, mask_ready = [st.sem("mask_loaded") for _ in range(2)], st.sem("mask_ready")
        km_done = st.sem("k_middle_done")
        passed = st.sem("wait_passed")
        cleared, src_ready = st.sem("cleared"), st.sem("src_ready")
        pro_made, pro_kept, kh_done, kl_done = (st.sem(n) for n in ("pro_made", "pro_kept", "k_high_done", "k_low_done"))
        k_stored = [st.sem("k_stored") for _ in range(KC)]
        q_step = st.sem("q_step")
        x_loaded = [st.sem("x_loaded") for _ in range(NX)]
        row_set = st.sem("mask_row_set")
        q_staged, v_staged = st.sem("q_staged"), st.sem("v_staged")
        tm_made, te_made, qm_kept, qe_kept = (st.sem(n) for n in (
            "queries_turned", "max_turned", "QT_max_kept", "QT_exp_kept"))
        m_made, m_read, n_step, negm = (st.sem(n) for n in ("max_scores_made", "max_scores_read", "neg_step", "neg_max_ready"))
        st_made, exp_done, pv_done = st.sem("scoresT_made"), st.sem("exp_done"), st.sem("weighted_done")
        o_kept, fin, summed, normed = st.sem("groups_kept"), st.sem("groups_summed"), st.sem("recip_done"), st.sem("normalised")

        def heads(eng, b, step):
            with eng.Fori(0, TURNS - 1) as turn:
                for u in range(NX):
                    step(turn * NX + u, u, turn, True)
            for u in range(NX):
                step((TURNS - 1) * NX + u, u, TURNS - 1, u < NX - 1)

        with nc.Block() as block:

            @block.sync
            def _(sp):
                sp.dma_start(ws[:, :, :], w[0]).then_inc(w_loaded, 16)
                sp.dma_start(bs[:, :], w[1]).then_inc(w_loaded, 16)
                sp.dma_start(sel[:, :], w[2]).then_inc(w_loaded, 16)
                with sp.Fori(0, B) as b:
                    for n in range(HG * KC):
                        g, c = n // KC, n % KC
                        sp.wait_ge(kl_done, b * (HG * KC) + (n + 1))
                        sp.dma_start(parts_d[:, g * P:(g + 1) * P, c * 512:(c + 1) * 512].rearrange("a p k -> p a k"),
                                     kst[:, :, c * 512:(c + 1) * 512]).then_inc(k_stored[c], 16)
                    if key_mask is not None:
                        sp.wait_ge(mask_ready, b + 2)
                        for x in X:
                            sp.dma_start(x[MASKROW:XR, :], kadd[:, :]).then_inc(row_set, 16)
                    for s in k_stored:
                        sp.wait_ge(s, b * (HG * 16) + (HG * 16 + 1))

                    def load(h, u):
                        for r0, n, part in ((0, 3, 0), (48, 2, 1), (80, 1, 2)):
                            sp.dma_start(X[u][r0:r0 + n * d, :],
                                         parts_d[part, bass.ds(h * d, d), :].unsqueeze(0).broadcast_to([n, d, SK]))\
                              .then_inc(x_loaded[u], 16)

                    def step(h, u, turn, more):
                        if not (isinstance(turn, int) and u > 0):
                            sp.wait_ge(pv_done, (b * H + h) * EU + 4)
                            load(h + (NX - 1), (u + NX - 1) % NX)

                    for h in range(NX - 1):
                        load(h, h)
                    heads(sp, b, step)

            @block.gpsimd
            def _(pool):
                with pool.Fori(0, B) as b:
                    ctx_b = ctxT[bass.ds(b, 1)].rearrange("o p c k -> (o p) c k")

                    def load_context(c):
                        for i in range(4):
                            keys = slice(i * SK // 4, (i + 1) * SK // 4)
                            pool.dma_start(cx[:, c, keys], ctx_b[:, c, keys]).then_inc(ctx_loaded[i], 16)

                    load_context(1)
                    pool.wait_ge(pv_done, b * (H * EU) + 4)
                    pool.sem_inc(passed, 1)
                    load_context(0)
                    if key_mask is not None:
                        pool.dma_start(km[:, :], key_mask[bass.ds(b, 1), :]).then_inc(mask_loaded[0], 16)
                    for n in range(HG * KC):
                        c = n % KC
                        part = kst[:, :, c * 512:(c + 1) * 512]
                        pool.wait_ge(km_done, b * (HG * KC) + (n + 1))
                        pool.tensor_tensor(part[:, 2, :], kr[n % 2][:, :], part[:, 1, :], ALU.subtract)\
                            .then_inc(kl_done, 1)
                    if masks is not None:
                        pool.wait_ge(m_read, b * (H * MU) + 1)
                        for i in range(8):
                            pool.wait_ge(mask_ready, b * 8 + (max(i - 1, 0) + 1))
                            pool.sem_inc(passed, 1)
                            pool.dma_start(words[i % 2], masks[i // 4][bass.ds(b, 1)].rearrange(
                                "o p k -> (o p) k")[:, i % 4 * 512:(i % 4 + 1) * 512]).then_inc(mask_loaded[i % 2], 16)
                    pool.wait_ge(q_step, b * 7 + 7)
                    pool.wait_ge(pro_kept, b * PRO + PRO)

                    def stage_q(h, p):
                        pool.tensor_copy(Qh[p][:, :, :], Q[:, :, bass.ds(h, 1), :].rearrange("p q o c -> p q (o c)"))\
                            .then_inc(q_staged, 1)

                    def stage_v(h, p):
                        pool.tensor_copy(Vh[p][:, :, 0:VW],
                                         V[:, :, bass.ds(h, 1), :].rearrange("p k o v -> p k (o v)"))\
                            .then_inc(v_staged, 1)

                    pool.sem_inc(passed, 1)
                    for h in range(2):
                        stage_q(h, h)
                        stage_v(h, h)

                    def step(h, u, turn, more):
                        hi = b * H + h
                        last_turn = isinstance(turn, int)
                        if not (last_turn and u > 1):
                            pool.wait_ge(st_made, hi * EU + 1)
                            pool.sem_inc(passed, 1)
                            stage_q(h + 2, u % 2)
                            pool.wait_ge(pv_done, hi * EU + (EU + 4))
                            pool.sem_inc(passed, 1)
                            stage_v(h + 2, u % 2)

                    heads(pool, b, step)

            @block.tensor
            def _(pe):
                pe.sem_inc(pv_done, 4)
                pe.wait_ge(w_loaded, 48)
                pe.wait_ge(cleared, CLEARED)
                with pe.Fori(0, B) as b:
                    for n in range(PRO):
                        if n < KC and n % (KC // 4) == 0:
                            pe.wait_ge(ctx_loaded[n // (KC // 4)], b * 32 + 32)
                        if n >= 2:
                            pe.wait_ge(pro_kept, b * PRO + (n - 1))
                        if n == HG * KC + NKT:
                            pe.wait_ge(src_ready, b + 1)
                        bank = mb[:, n % 2, :]
                        for c in range(DC):
                            if n < HG * KC:
                                g, k = n // KC, n % KC
                                ops = bank, ws[:, c, g * P:(g + 1) * P], cx[:, c, k * 512:(k + 1) * 512]
                            elif n < HG * KC + NKT:
                                k = n - HG * KC
                                ops = bank[:, 0:H * VW], cx[:, c, k * P:(k + 1) * P], ws[:, c, 2 * D:2 * D + H * VW]
                            else:
                                q = n - HG * KC - NKT
                                ops = bank[:, 0:D], qsrc[:, c, q * P:(q + 1) * P], ws[:, c, D:2 * D]
                            last = pe.matmul(*ops, start=(c == 0), stop=(c == DC - 1))
                        last.then_inc(pro_made, 1)

                    def turn_queries(p, bank, at, made):
                        o = bank[:, at:at + P].bitcast(BF16)
                        for q in range(QT):
                            last = pe.transpose(o[:, q * P:(q + 1) * P], Qh[p][:, q, :], R.identb[:, :])
                        last.then_inc(made, 1)

                    def max_unit(hi, u, turn, n):
                        if n == 0:
                            pe.wait_ge(qm_kept, hi + 1)
                            pe.wait_ge(x_loaded[u], (b * TURNS + turn) * 48 + 48)
                            if key_mask is not None:
                                pe.wait_ge(row_set, b * (16 * NX) + 16 * NX)
                        q, k = n // KC, n % KC
                        pe.matmul(mb[:, n % 2, :], Qm[u % 2][0:XR, q * P:(q + 1) * P], X[u][:, k * 512:(k + 1) * 512],
                                  start=True, stop=True).then_inc(m_made, 1)

                    pe.wait_ge(q_staged, b * H + 1)
                    pe.wait_ge(normed, b * H + 2)
                    pe.wait_ge(pro_kept, b * PRO + PRO)
                    turn_queries(0, pb[0], 384, tm_made)
                    for n in range(MU):
                        if n >= 2:
                            pe.wait_ge(m_read, b * (H * MU) + (n - 1 + 1))
                        max_unit(b * H, 0, 0, n)
                    pe.wait_ge(negm, b * H + 1)
                    turn_queries(0, pb[0], 256, te_made)
                    pe.wait_ge(q_staged, b * H + 2)
                    pe.wait_ge(qe_kept, b * H + 1)
                    turn_queries(1, pb[0], 384, tm_made)
                    if masks is not None:
                        pe.wait_ge(mask_ready, b * 8 + 9)
                        pe.sem_inc(passed, 1)

                    def add_groups(hi, p):
                        pe.wait_ge(o_kept, hi + 1)
                        for q in range(QT):
                            last = pe.matmul(pb[p][:, 256 + q * 32:256 + q * 32 + VW], osb[:, q * P:(q + 1) * P],
                                             sel[:, 0:VW], start=True, stop=True)
                        last.then_inc(fin, 1)

                    def step(h, u, turn, more):
                        hi, p = b * H + h, u % 2
                        two_more = not (isinstance(turn, int) and u > NX - 3)
                        n = 0
                        acc = pb[p]

                        def weigh(e):
                            pe.wait_ge(exp_done, hi * EU + (e + 3))
                            if e == 0:
                                pe.wait_ge(v_staged, hi + 1)
                                pe.wait_ge(normed, hi + 1)
                            for i in range(EK):
                                kt = e * EK + i
                                last = pe.matmul(acc[32 * i:32 * (i + 1), 0:S], Vh[p][:, kt, :],
                                                 PT[e % 4][:, i * S:(i + 1) * S], start=(e == 0), stop=(e == EU - 1))
                            last.then_inc(pv_done, 1)

                        def some_max(i):
                            nonlocal n
                            if more and i < WHEN[e]:
                                pe.wait_ge(m_read, hi * MU + (MU + n - 1 + 1))
                                max_unit(hi + 1, (u + 1) % NX, turn + (1 if u == NX - 1 else 0), n)
                                n += 1

                        for e in range(EU):
                            if e == 0:
                                pe.wait_ge(qe_kept, hi + 1)
                            pe.wait_ge(exp_done, hi * EU + (e + 1))
                            for half in range(2):
                                bank = sT[:, e % 2, half * 512:(half + 1) * 512]
                                k0 = (e * EK + 2 * half) * S
                                if masks is not None:
                                    pe.matmul(bank, R.identb[:, :], mk[:, k0:k0 + 512], start=True, stop=False)
                                for i in range(2):
                                    kt = e * EK + 2 * half + i
                                    last = pe.matmul(bank[:, i * S:(i + 1) * S], X[u][:, kt * P:(kt + 1) * P],
                                                     Qe[p][0:XR, :], start=(masks is None),
                                                     stop=(masks is None or i == 1))
                                if half == 1:
                                    last.then_inc(st_made, 1)
                                elif WHEN[e]:
                                    some_max(0)
                            some_max(1)
                            if e == 0 and u > 0:
                                add_groups(hi - 1, 1 - p)
                            if e == TURN and two_more:
                                pe.wait_ge(q_staged, hi + 3)
                                pe.wait_ge(normed, hi + 2)
                                turn_queries(p, pb[1 - p], 384, tm_made)
                            if e >= 1:
                                weigh(e - 1)
                            if WHEN[e] > 2:
                                some_max(2)
                        if more:
                            if two_more:
                                pe.wait_ge(qm_kept, hi + 3)
                            pe.wait_ge(normed, hi + 2)
                            pe.wait_ge(negm, hi + 2)
                            turn_queries(1 - p, pb[1 - p], 256, te_made)
                        weigh(EU - 1)
                        if u == NX - 1:
                            add_groups(hi, p)

                    heads(pe, b, step)

            @block.scalar
            def _(act):
                act.sem_inc(exp_done, 2)
                for s in k_stored:
                    act.sem_inc(s, 1)
                act.wait_ge(w_loaded, 48)
                with act.Fori(0, B) as b:
                    def middle(n):
                        c = n % KC
                        act.wait_ge(pro_kept, b * PRO + (n + 1))
                        act.activation(kst[:, 1, c * 512:(c + 1) * 512], kr[n % 2][:, :], ACT.Copy).then_inc(km_done, 1)

                    for n in range(HG * KC):
                        g, c = n // KC, n % KC
                        act.wait_ge(pro_made, b * PRO + (n + 1))
                        act.wait_ge(k_stored[c], b * (HG * 16) + (g * 16 + 1))
                        act.activation(kst[:, 0, c * 512:(c + 1) * 512], mb[:, n % 2, :], ACT.Identity,
                                       bias=bs[:, g:g + 1]).then_inc(kh_done, 1)
                        if n >= 1:
                            middle(n - 1)
                    middle(HG * KC - 1)
                    if masks is not None:
                        for i in range(8):
                            act.wait_ge(mask_loaded[i % 2], b * 64 + (i // 2 * 16 + 16))
                            act.activation((mq, mk)[i // 4][:, i % 4 * 2048:(i % 4 + 1) * 2048],
                                           words[i % 2].bitcast(U8), ACT.Copy, scale=MASKED).then_inc(mask_ready, 1)

                    def keep_qm(head, p, bank):
                        act.wait_ge(tm_made, head + 1)
                        act.activation(Qm[p][:, :], bank[:, 384:512].bitcast(BF16), ACT.Copy).then_inc(qm_kept, 1)

                    keep_qm(b * H, 0, pb[0])
                    keep_qm(b * H + 1, 1, pb[0])

                    def step(h, u, turn, more):
                        hi, p = b * H + h, u % 2
                        last_turn = isinstance(turn, int)
                        for e in range(EU):
                            act.wait_ge(st_made, hi * EU + (e + 1))
                            act.wait_ge(pv_done, hi * EU + (e + 1))
                            act.activation(PT[e % 4], sT[:, e % 2, :], ACT.Exp, scale=scale).then_inc(exp_done, 1)
                            if e == TURN and not (last_turn and u > NX - 3):
                                keep_qm(hi + 2, p, pb[1 - p])
                        act.wait_ge(pv_done, hi * EU + (EU + 4))
                        act.activation(osb[:, :], pb[p][:, 0:S], ACT.Copy).then_inc(o_kept, 1)

                    heads(act, b, step)

            @block.vector
            def _(dve):
                dve.sem_inc(normed, 2)
                dve.sem_inc(m_read, 1)
                dve.sem_inc(mask_ready, 1)
                for v in Vh:
                    dve.memset(v[:, :, :], 0.0).then_inc(cleared, 1)
                for x in X:
                    dve.memset(x[M0:XR, :], 1.0).then_inc(cleared, 1)
                dve.memset(Q[:, :, :, M0:P], 0.0).then_inc(cleared, 1)
                dve.wait_ge(cleared, 2 + NX + 1)
                if key_mask is not None:
                    dve.memset(Q[:, :, :, MASKROW:MASKROW + 1], 1.0).then_inc(cleared, 1)
                dve.wait_ge(w_loaded, 48)
                dve.wait_ge(cleared, CLEARED)
                with dve.Fori(0, B) as b:
                    dve.wait_ge(pv_done, b * (H * EU) + 4)
                    dve.tensor_copy(qsrc[:, :, :], R.xnT[:, :, bass.ds(b * S, S)]).then_inc(src_ready, 1)
                    for n in range(HG * KC):
                        g, c = n // KC, n % KC
                        dve.wait_ge(kh_done, b * (HG * KC) + (n + 1))
                        if n >= 2:
                            dve.wait_ge(kl_done, b * (HG * KC) + (n - 1))
                        dve.scalar_tensor_tensor(out=kr[n % 2][:, :], in0=mb[:, n % 2, :], scalar=bs[:, g:g + 1],
                                                 in1=kst[:, 0, c * 512:(c + 1) * 512], op0=ALU.add,
                                                 op1=ALU.subtract).then_inc(pro_kept, 1)
                    if key_mask is not None:
                        dve.wait_ge(mask_loaded[0], b * 16 + 16)
                        dve.tensor_scalar(kadd[:, :], km[:, :], 0.0, MASKED, ALU.is_equal, ALU.mult)\
                           .then_inc(mask_ready, 1)
                    for k in range(NKT):
                        n = HG * KC + k
                        dve.wait_ge(pro_made, b * PRO + (n + 1))
                        dve.tensor_tensor(V[:, k, :, :].rearrange("p h v -> p (h v)"), mb[:, n % 2, 0:H * VW],
                                          bs[:, HG + D:HG + D + H * VW], ALU.add).then_inc(pro_kept, 1)
                    for q in range(QT):
                        n = HG * KC + NKT + q
                        dve.wait_ge(pro_made, b * PRO + (n + 1))
                        dve.tensor_tensor(qf[:, q, :], mb[:, n % 2, 0:D], bs[:, HG:HG + D], ALU.add)\
                           .then_inc(pro_kept, 1)
                    blk = [Q[:, :, :, i * d:(i + 1) * d] for i in range(6)]
                    q4, r4 = (t[:, :, :].rearrange("p q (h f) -> p q h f", h=H) for t in (qf, qr))
                    dve.wait_ge(pro_kept, b * PRO + PRO)
                    dve.tensor_copy(blk[0], q4).then_inc(q_step, 1)
                    dve.wait_ge(q_step, b * 7 + 1)
                    dve.tensor_tensor(r4, q4, blk[0], ALU.subtract).then_inc(q_step, 1)
                    dve.tensor_copy(blk[3], blk[0]).then_inc(q_step, 1)
                    dve.tensor_copy(blk[5], blk[0]).then_inc(q_step, 1)
                    dve.wait_ge(q_step, b * 7 + 4)
                    dve.tensor_copy(blk[1], r4).then_inc(q_step, 1)
                    dve.wait_ge(q_step, b * 7 + 5)
                    dve.tensor_copy(blk[4], blk[1]).then_inc(q_step, 1)
                    dve.tensor_tensor(blk[2], r4, blk[1], ALU.subtract).then_inc(q_step, 1)
                    if masks is not None:
                        dve.wait_ge(mask_ready, b * 8 + 9)

                    def maxima(head, p, between=None):
                        for n in range(MU):
                            q, k = n // KC, n % KC
                            if n == WHEN[0] and between is not None:
                                between()
                            dve.wait_ge(m_made, head * MU + (n + 1))
                            if masks is not None:
                                if n >= 4:
                                    dve.wait_ge(m_read, head * MU + (n - 3 + 1))
                                dve.sem_inc(passed, 1)
                                dve.tensor_tensor_reduce(junk[n % 4], mb[:, n % 2, :],
                                                         mq[:, q * SK + k * 512:q * SK + (k + 1) * 512], 1.0, -3e38,
                                                         ALU.add, ALU.max, mx[:, q, k:k + 1]).then_inc(m_read, 1)
                            else:
                                dve.tensor_reduce(mx[:, q, k:k + 1], mb[:, n % 2, :], AX.X, ALU.max)\
                                   .then_inc(m_read, 1)
                        part = [Qh[p][:, :, M0 + i] for i in range(3)]
                        dve.wait_ge(m_read, head * MU + (MU + 1))
                        dve.tensor_reduce(nm[:, :], mx[:, :, :], AX.X, ALU.max, negate=True).then_inc(n_step, 1)
                        dve.wait_ge(n_step, head * 4 + 1)
                        dve.tensor_copy(part[0], nm[:, :]).then_inc(n_step, 1)
                        dve.wait_ge(n_step, head * 4 + 2)
                        dve.tensor_tensor(nr[:, :], nm[:, :], part[0], ALU.subtract).then_inc(n_step, 1)
                        dve.wait_ge(n_step, head * 4 + 3)
                        dve.tensor_copy(part[1], nr[:, :]).then_inc(n_step, 1)
                        dve.wait_ge(n_step, head * 4 + 4)
                        dve.tensor_tensor(part[2], nr[:, :], part[1], ALU.subtract).then_inc(negm, 1)

                    def keep_qe(head, p, bank):
                        dve.wait_ge(te_made, head + 1)
                        dve.tensor_copy(Qe[p][:, :], bank[:, 256:384].bitcast(BF16)).then_inc(qe_kept, 1)

                    maxima(b * H, 0)
                    keep_qe(b * H, 0, pb[0])

                    def normalise(h, u):
                        hi = b * H + h
                        both = pb[u % 2][:, 256:320].rearrange("p (q w) -> p q w", q=QT)
                        dve.wait_ge(fin, hi + 1)
                        dve.wait_ge(normed, hi + 2)
                        dve.reciprocal(rs[:, :], both[:, :, d]).then_inc(summed, 1)
                        dve.wait_ge(summed, hi + 1)
                        for q in range(QT):
                            ins = dve.tensor_scalar(
                                att[:, bass.ds(b * QT + q, 1), bass.ds(h * d, d)].rearrange("p o w -> p (o w)"),
                                both[:, q, 0:d], rs[:, q:q + 1], None, ALU.mult)
                        ins.then_inc(normed, 1)

                    def step(h, u, turn, more):
                        hi, p = b * H + h, u % 2
                        last_head = (lambda: normalise(h - 1, u - 1)) if u > 0 else None
                        if more:
                            maxima(hi + 1, 1 - p, last_head)
                            keep_qe(hi + 1, 1 - p, pb[1 - p])
                        else:
                            last_head()
                        if u == NX - 1:
                            normalise(h, u)

                    heads(dve, b, step)


def wide_context_stage(nc, R, att, pack, scale, ctxT, masks, half_sum):
    d, J = 64, 4
    G = 16 // J
    W4 = J * d
    NKT, KC = SK // P, SK // 512
    EU, EK = 8, 4
    MU = QT * KC
    NV, NQ = NKT // 2, J // 2
    LATE = 4
    units = [("v", n) for n in range(NV - LATE)] + [("q", n) for n in range(NQ)] + \
        [("k", n) for n in range(KC)] + [("v", n) for n in range(NV - LATE, NV)] + [("k", KC + n) for n in range(KC)]
    NU, at = len(units), {u: n for n, u in enumerate(units)}
    LATER = (3, 3, 2, 2, 2, 2, 2, 0)
    EXPS, MAXES = J * EU, J * MU
    with Stage(nc) as st:
        cx = st.sb("ctxT", [P, DC, SK])
        wt = st.sb("w_turn", [P, DC, 3 * W4])
        wk, wq, wv = (wt[:, :, i * W4:(i + 1) * W4] for i in range(3))
        V = st.sb("V", [P, NKT, W4])
        KT = [st.sb("KT", [d + 1, SK]) for _ in range(2)]
        X = [st.sb("key_parts", [P, SK], BF16) for _ in range(2)]
        QF = st.sb("QT", [d + 1, J, S])
        Qh, Qm = st.sb("QT_high", [P, J, S], BF16), st.sb("QT_middle", [P, J, S], BF16)
        PT = [st.sb("probsT", [P, EK * S]) for _ in range(3)]
        words = [x[:, :].bitcast(I32) for x in X]
        mq, mk = [st.sb("mask_add", [P, QT * SK], BF16) for _ in range(2)]
        junk = R.xn[:, :, :].rearrange("p t f -> p (t f)").bitcast(BF16).rearrange("p (i k) -> p i k", i=4)
        mx, nm, rs = st.sb("max_parts", [P, QT, KC]), st.sb("neg_max", [P, QT]), st.sb("sum_recip", [P, QT])
        part, tot = st.sb("part_sums", [P, EU // 2 + 1, S]), st.sb("key_sums", [P, S])
        osb, halves = st.sb("halves", [P, S]), st.sb("half_sum", [P, d])
        sT = st.ps("scoresT", [P, 2, EK * S])
        mb = st.ps("max_scores", [P, 2, 512])
        pb = [st.ps("weighted", [P, 512]) for _ in range(2)]

        w_loaded, const_loaded, ctx_loaded, mask_loaded = (st.sem(n) for n in (
            "w_loaded", "const_loaded", "ctx_loaded", "mask_loaded"))
        cleared, mask_ready, halfway = st.sem("cleared"), st.sem("mask_ready"), st.sem("half_totalled")
        passed = st.sem("wait_passed")
        pj_made, pj_kept, q_split = (st.sem(n) for n in ("proj_made", "proj_kept", "q_split"))
        k0_kept, k0_split, k1_high, k1_split = (st.sem(n) for n in ("k0_kept", "k0_split", "k1_high", "k1_split"))
        m_made, m_read, negm, turned, row_kept = (st.sem(n) for n in (
            "max_scores_made", "max_scores_read", "neg_max_ready", "neg_max_turned", "neg_max_kept"))
        st_made, exp_done, pv_done, sum_done = (st.sem(n) for n in (
            "scoresT_made", "exp_done", "weighted_done", "part_sum_done"))
        o_kept, totalled, fin, summed, normed = (st.sem(n) for n in (
            "halves_kept", "totalled", "halves_summed", "recip_done", "normalised"))
        PJ, MR, EX, PV, TO, FI, NO = 1, 2, 2, 4, 1, 1, 2

        with nc.Block() as block:

            @block.sync
            def _(sp):
                sp.dma_start(halves[:, :], half_sum).then_inc(const_loaded, 16)
                with sp.Fori(0, B) as b:
                    sp.wait_ge(pj_made, b * (G * NU) + PJ)
                    sp.dma_start(cx[:, :, :], ctxT[bass.ds(b, 1)].rearrange("o p c k -> (o p) c k"))\
                      .then_inc(ctx_loaded, 16)
                    with sp.Fori(0, G) as g:
                        sp.wait_ge(pj_made, (b * G + g) * NU + PJ)
                        sp.dma_start(wt[:, :, :], pack[bass.ds(g, 1)].rearrange("o p c w -> (o p) c w"))\
                          .then_inc(w_loaded, 16)

            @block.gpsimd
            def _(pool):
                with pool.Fori(0, B) as b:
                    pool.wait_ge(m_read, b * (G * MAXES) + MR)
                    pool.sem_inc(passed, 1)
                    for n in range(2):
                        pool.dma_start(words[n], masks[n][bass.ds(b, 1)].rearrange("o p k -> (o p) k"))\
                            .then_inc(mask_loaded, 16)
                    with pool.Fori(0, G) as g:
                        it = b * G + g
                        for n in range(J // 2 * KC):
                            c = slice(n % KC * 512, (n % KC + 1) * 512)
                            pool.wait_ge(pj_kept, it * NU + (at["k", n] + 1))
                            pool.tensor_tensor(X[1][0:d, c], KT[1][0:d, c], R.onesf[0:d, 0:1].broadcast_to([d, 512]),
                                               ALU.mult).then_inc(k1_high, 1)
                            pool.wait_ge(k1_high, it * (J // 2 * KC) + (n + 1))
                            pool.tensor_tensor(X[1][d:2 * d, c], KT[1][0:d, c], X[1][0:d, c], ALU.subtract)\
                                .then_inc(k1_split, 1)

            @block.tensor
            def _(pe):
                pe.sem_inc(pj_made, PJ)
                pe.sem_inc(pv_done, PV)
                pe.sem_inc(fin, FI)
                pe.wait_ge(const_loaded, 16)
                pe.wait_ge(cleared, 2)
                with pe.Fori(0, B) as b:
                    with pe.Fori(0, G) as g:
                        it = b * G + g

                        def project(n):
                            bank = sT[:, n % 2, 0:512]
                            if n >= 2:
                                pe.wait_ge(pj_kept, it * NU + (n - 1))
                                if units[n][0] == "q":
                                    pe.sem_inc(passed, 1)
                            what, m = units[n]
                            for i in range(1 if what == "k" else 2):
                                for c in range(DC):
                                    if what == "v":
                                        kt = m * 2 + i
                                        ops = bank[:, i * W4:(i + 1) * W4], cx[:, c, kt * P:(kt + 1) * P], wv[:, c, :]
                                    elif what == "q":
                                        j = m * 2 + i
                                        ops = (bank[0:d, i * S:(i + 1) * S], wq[:, c, j * d:(j + 1) * d],
                                               R.xnT[:, c, bass.ds(b * S, S)])
                                    else:
                                        pair, k = m // KC, m % KC
                                        ops = bank, wk[:, c, pair * P:(pair + 1) * P], cx[:, c, k * 512:(k + 1) * 512]
                                    last = pe.matmul(*ops, start=(c == 0), stop=(c == DC - 1))
                            last.then_inc(pj_made, 1)

                        def max_unit(j, n):
                            k, q = n // QT, n % QT
                            pe.wait_ge(m_read, it * MAXES + (j * MU + n - 1 + MR))
                            for i, part_q in enumerate((Qh, Qm)):
                                last = pe.matmul(mb[:, n % 2, :], part_q[:, j, q * P:(q + 1) * P],
                                                 X[j % 2][:, k * 512:(k + 1) * 512], start=(i == 0), stop=(i == 1))
                            last.then_inc(m_made, 1)

                        def turn_max(j):
                            pe.wait_ge(normed, it * J + (j - 1 + NO))
                            pe.wait_ge(negm, it * J + (j + 1))
                            for q in range(QT):
                                last = pe.transpose(pb[j % 2][0:1, 256 + q * P:256 + (q + 1) * P], nm[:, q:q + 1],
                                                    R.identf[:, :])
                            last.then_inc(turned, 1)

                        def weigh(j, e):
                            pe.wait_ge(exp_done, it * EXPS + (j * EU + e + 1 + EX))
                            probs = PT[(j * EU + e) % 3]
                            for i in range(EK):
                                kt, half = e * EK + i, i % 2
                                last = pe.matmul(pb[j % 2][half * d:(half + 1) * d, 0:S], V[:, kt, j * d:(j + 1) * d],
                                                 probs[:, i * S:(i + 1) * S],
                                                 start=(kt < 2), stop=(kt >= NKT - 2))
                            last.then_inc(pv_done, 1)

                        def add_halves(j):
                            pe.wait_ge(o_kept, it * J + (j + 1))
                            pe.wait_ge(totalled, it * J + (j + 1 + TO))
                            for q in range(QT):
                                cols = slice(q * P, (q + 1) * P)
                                pe.matmul(pb[j % 2][:, 256 + q * d:256 + (q + 1) * d], osb[:, cols], halves[:, :],
                                          start=True, stop=True)
                                last = pe.matmul(pb[j % 2][:, 384 + q:385 + q], tot[:, cols], R.onesf[:, 0:1],
                                                 start=True, stop=True)
                            last.then_inc(fin, 1)

                        pe.wait_ge(ctx_loaded, b * 16 + 16)
                        pe.wait_ge(w_loaded, it * 16 + 16)
                        pe.wait_ge(exp_done, it * EXPS + EX)
                        for n in range(at["k", 0]):
                            project(n)
                        pe.wait_ge(q_split, it * NQ + NQ)
                        for pair in range(J // 2):
                            j = 2 * pair
                            if pair:
                                pe.wait_ge(exp_done, it * EXPS + (j * EU + EX))

                            def max_bank(k):
                                pe.wait_ge(k0_split, it * (J // 2 * KC) + (pair * KC + k + 1))
                                for q in range(QT):
                                    max_unit(j, k * QT + q)

                            for k in range(KC):
                                project(at["k", pair * KC + k])
                                if k >= 2:
                                    max_bank(k - 2)
                            fill = [lambda n=n: project(at["v", n]) for n in range(NV - LATE, NV)] if pair == 0 else \
                                [lambda: weigh(j - 1, EU - 2), lambda: weigh(j - 1, EU - 1)]
                            max_bank(KC - 2)
                            fill[0]()
                            max_bank(KC - 1)
                            fill[1]()
                            turn_max(j)
                            for step in fill[2:]:
                                step()
                            if pair:
                                add_halves(j - 1)
                            pe.wait_ge(pj_kept, it * NU + (NU if pair else at["k", KC]))
                            pe.wait_ge(mask_ready, b * 2 + 2)
                            for j in (2 * pair, 2 * pair + 1):
                                pe.wait_ge(row_kept, it * J + (j + 1))
                                n = 0

                                def some_max(i):
                                    nonlocal n
                                    if j % 2 == 0 and i < LATER[e]:
                                        if n == 0:
                                            pe.wait_ge(k1_split, it * (J // 2 * KC) + (pair + 1) * KC)
                                        max_unit(j + 1, n)
                                        n += 1

                                for e in range(EU):
                                    pe.wait_ge(exp_done, it * EXPS + (j * EU + e - 1 + EX))
                                    for half in range(2):
                                        bank = sT[:, e % 2, half * 512:(half + 1) * 512]
                                        k0 = (e * EK + 2 * half) * S
                                        pe.matmul(bank, R.identb[:, :], mk[:, k0:k0 + 512], start=True, stop=False)
                                        for i in range(2):
                                            kt = e * EK + 2 * half + i
                                            last = pe.matmul(bank[:, i * S:(i + 1) * S], KT[j % 2][:, kt * P:(kt + 1) * P],
                                                             QF[0:d + 1, j, :], start=False, stop=(i == 1))
                                        if half == 1:
                                            last.then_inc(st_made, 1)
                                        some_max(half)
                                    if j % 2 and e == 0:
                                        add_halves(j - 1)
                                    if e >= 1 and not (j == 1 and e == EU - 1):
                                        weigh(j, e - 1)
                                    some_max(2)
                                if j % 2 == 0:
                                    turn_max(j + 1)
                                if j != 1:
                                    weigh(j, EU - 1)
                        add_halves(J - 1)

            @block.scalar
            def _(act):
                act.sem_inc(exp_done, EX)
                with act.Fori(0, B) as b:
                    with act.Fori(0, G) as g:
                        it = b * G + g
                        def keep(n):
                            what, m = units[n]
                            bank = sT[:, n % 2, 0:512]
                            act.wait_ge(pj_made, it * NU + (n + 1 + PJ))
                            if what == "v":
                                act.activation(V[:, 2 * m:2 * m + 2, :], bank.rearrange("p (k w) -> p k w", k=2),
                                               ACT.Copy).then_inc(pj_kept, 1)
                            elif what == "q":
                                two = slice(2 * m, 2 * m + 2)
                                src = bank[0:d, :].rearrange("p (j s) -> p j s", j=2)
                                for half in range(2):
                                    act.activation(Qh[half * d:(half + 1) * d, two, :], src, ACT.Copy)
                                act.activation(QF[0:d, two, :], src, ACT.Copy).then_inc(pj_kept, 1)
                            else:
                                c = slice(m % KC * 512, (m % KC + 1) * 512)
                                act.activation(X[0][0:d, c], bank[0:d, :], ACT.Copy)
                                act.activation(KT[0][0:d, c], bank[0:d, :], ACT.Copy).then_inc(k0_kept, 1)
                                act.activation(KT[1][0:d, c], bank[d:2 * d, :], ACT.Copy).then_inc(pj_kept, 1)

                        def keep_halves(j):
                            act.wait_ge(pv_done, it * EXPS + ((j + 1) * EU + PV))
                            act.wait_ge(fin, it * J + (j + FI))
                            act.activation(osb[:, :], pb[j % 2][:, 0:S], ACT.Copy).then_inc(o_kept, 1)

                        for n in range(at["k", 0]):
                            keep(n)
                        for pair in range(J // 2):
                            if pair == 0:
                                act.wait_ge(mask_ready, b * 2 + 2)
                            for n in range(at["k", 0], at["k", KC]) if pair == 0 else range(at["k", KC], NU):
                                keep(n)
                            if pair:
                                keep_halves(1)
                            for j in (2 * pair, 2 * pair + 1):
                                for e in range(EU):
                                    i = j * EU + e
                                    act.wait_ge(st_made, it * EXPS + (i + 1))
                                    used = it * EXPS + (max(i - 2, 0) + PV)
                                    act.wait_ge(pv_done, used)
                                    act.wait_ge(sum_done, used)
                                    act.activation(PT[i % 3][:, :], sT[:, e % 2, :], ACT.Exp, scale=scale).then_inc(exp_done, 1)
                                if j != 1:
                                    keep_halves(j)

            @block.vector
            def _(dve):
                for sem, start in ((m_read, MR), (sum_done, PV), (totalled, TO), (normed, NO)):
                    dve.sem_inc(sem, start)
                for k in KT:
                    dve.memset(k[d:d + 1, :], 1.0).then_inc(cleared, 1)
                with dve.Fori(0, B) as b:
                    dve.wait_ge(mask_loaded, b * 32 + 32)
                    dve.wait_ge(pv_done, b * (G * EXPS) + PV)
                    for src, add in zip(words, (mq, mk)):
                        dve.tensor_scalar(add[:, :], src.bitcast(U8), MASKED, None, ALU.mult).then_inc(mask_ready, 1)
                    dve.wait_ge(mask_ready, b * 2 + 1)
                    dve.sem_inc(passed, 1)
                    with dve.Fori(0, G) as g:
                        it = b * G + g

                        def maxima(j, n):
                            k, q = n // QT, n % QT
                            dve.wait_ge(m_made, it * MAXES + (j * MU + n + 1))
                            if n >= 4:
                                dve.wait_ge(m_read, it * MAXES + (j * MU + n - 3 + MR))
                            dve.sem_inc(passed, 1)
                            dve.tensor_tensor_reduce(junk[:, n % 4, :], mb[:, n % 2, :],
                                                     mq[:, q * SK + k * 512:q * SK + (k + 1) * 512], 1.0, -3e38,
                                                     ALU.add, ALU.max, mx[:, q, k:k + 1]).then_inc(m_read, 1)

                        def negate(j):
                            dve.wait_ge(m_read, it * MAXES + ((j + 1) * MU + MR))
                            dve.tensor_reduce(nm[:, :], mx[:, :, :], AX.X, ALU.max, negate=True).then_inc(negm, 1)
                            dve.wait_ge(turned, it * J + (j + 1))
                            dve.tensor_copy(QF[d:d + 1, j, :], pb[j % 2][0:1, 256:512]).then_inc(row_kept, 1)

                        def normalise(j):
                            dve.wait_ge(fin, it * J + (j + 1 + FI))
                            dve.wait_ge(normed, it * J + (j + NO))
                            dve.reciprocal(rs[:, :], pb[j % 2][:, 384:386]).then_inc(summed, 1)
                            dve.wait_ge(summed, it * J + (j + 1))
                            for q in range(QT):
                                o = att[:, bass.ds(b * QT + q, 1), bass.ds(g * W4 + j * d, d)]
                                ins = dve.tensor_scalar(o.rearrange("p o w -> p (o w)"),
                                                        pb[j % 2][:, 256 + q * d:256 + (q + 1) * d],
                                                        rs[:, q:q + 1], None, ALU.mult)
                            ins.then_inc(normed, 1)

                        for n in range(NQ):
                            two = slice(2 * n, 2 * n + 2)
                            dve.wait_ge(pj_kept, it * NU + (at["q", n] + 1))
                            for half in range(2):
                                last = dve.tensor_tensor(Qm[half * d:(half + 1) * d, two, :], QF[0:d, two, :],
                                                         Qh[0:d, two, :], ALU.subtract)
                            last.then_inc(q_split, 1)
                        dve.wait_ge(q_split, it * NQ + NQ)
                        for pair in range(J // 2):
                            j = 2 * pair
                            for k in range(KC + 2):
                                if k < KC:
                                    c = slice(k * 512, (k + 1) * 512)
                                    dve.wait_ge(k0_kept, it * (J // 2 * KC) + (pair * KC + k + 1))
                                    dve.tensor_tensor(X[0][d:2 * d, c], KT[0][0:d, c], X[0][0:d, c], ALU.subtract)\
                                       .then_inc(k0_split, 1)
                                if k >= 2:
                                    for q in range(QT):
                                        maxima(j, (k - 2) * QT + q)
                            negate(j)
                            if pair:
                                normalise(j - 1)
                            for j in (2 * pair, 2 * pair + 1):
                                n = 0
                                if j % 2:
                                    normalise(j - 1)
                                for e in range(EU):
                                    if j % 2 == 0:
                                        for _ in range(LATER[e]):
                                            maxima(j + 1, n)
                                            n += 1
                                        if e == EU - 1:
                                            negate(j + 1)
                                    if e == 0:
                                        dve.wait_ge(totalled, it * J + (j + TO))
                                    dve.wait_ge(exp_done, it * EXPS + (j * EU + e + 1 + EX))
                                    dve.tensor_reduce(part[:, (e if e < EU // 2 else (e + 1) % (EU // 2)), :], PT[(j * EU + e) % 3][:, :].rearrange(
                                        "p (k q) -> p q k", k=EK), AX.X, ALU.add).then_inc(sum_done, 1)
                                    if e == EU // 2 - 1:
                                        dve.wait_ge(sum_done, it * EXPS + (j * EU + EU // 2 + PV))
                                        dve.tensor_reduce(part[:, EU // 2, :], part[:, 0:EU // 2, :].rearrange(
                                            "p e q -> p q e"), AX.X, ALU.add).then_inc(halfway, 1)
                                        dve.wait_ge(halfway, it * (2 * J) + (2 * j + 1))
                                    elif e == EU - 2:
                                        dve.wait_ge(sum_done, it * EXPS + (j * EU + EU - 1 + PV))
                                        dve.tensor_reduce(tot[:, :], part[:, 1:EU // 2 + 1, :].rearrange("p e q -> p q e"),
                                                          AX.X, ALU.add).then_inc(halfway, 1)
                                dve.wait_ge(sum_done, it * EXPS + ((j + 1) * EU + PV))
                                dve.wait_ge(halfway, it * (2 * J) + (2 * j + 2))
                                dve.tensor_tensor(tot[:, :], tot[:, :], part[:, 0, :], ALU.add).then_inc(totalled, 1)
                        normalise(J - 1)


def context_stage(nc, R, att, ctxT_d, ctx_d):
    NKT, EK = SK // P, 4
    EU = NKT // EK
    parts = SK // 1024
    VW = D + 1
    with Stage(nc) as st:
        KT = [st.sb("ctxT", [P, DC, SK]) for _ in range(B)]
        V = [st.sb("ctx_ones", [P, NKT, VW]) for _ in range(B)]
        mx = st.sb("max_parts", [P, QT, parts])
        neg = st.sb("neg_max", [P, QT])
        rest, np3 = st.sb("neg_rest", [P, QT]), st.sb("neg_parts", [P, QT, 3], BF16)
        nrow, ones3 = st.sb("neg_max_rows", [3, 2, S], BF16), st.sb("ones3", [3, P], BF16)
        rsum = st.sb("sum_recip", [P, QT])
        PT = [st.sb("probsT", [P, EK * S]) for _ in range(3)]
        big = st.ps("scores", [P, 2, 1024])
        pv = st.ps("weighted", [P, QT, 512])
        rp = st.ps("row_ps", [3, S], BF16)
        k_loaded, v_loaded = ([st.sem(n) for _ in range(B)] for n in ("k_loaded", "v_loaded"))
        ones_set, split = st.sem("ones_set"), st.sem("split_step")
        s_made, s_read, maxed, turned, row_kept = (st.sem(n) for n in (
            "scores_made", "scores_read", "maxed", "turned", "row_kept"))
        st_made, exp_done, pv_done, summed, normed = (st.sem(n) for n in (
            "scoresT_made", "exp_done", "weighted_done", "summed", "normalised"))
        MU = QT * parts
        with nc.Block() as block:

            @block.sync
            def _(sp):
                for b in range(B):
                    for c in range(DC):
                        sp.dma_start(KT[b][:, c, :], ctxT_d[b][:, c, :]).then_inc(k_loaded[b], 16)
                    sp.dma_start(V[b][:, :, 0:D], ctx_d[b]).then_inc(v_loaded[b], 16)

            @block.gpsimd
            def _(pool):
                for b in range(B):
                    pool.memset(V[b][:, :, D:VW], 1.0).then_inc(ones_set, 1)
                pool.memset(ones3[:, :], 1.0).then_inc(ones_set, 1)

            @block.tensor
            def _(pe):
                pe.wait_ge(ones_set, B + 1)
                for b in range(B):
                    pe.wait_ge(k_loaded[b], 16 * DC)
                    u = b * MU
                    if b:
                        pe.wait_ge(exp_done, b * EU)
                    for q in range(QT):
                        for k in range(parts):
                            if u % MU >= 2:
                                pe.wait_ge(s_read, u - 1)
                            for h in range(2):
                                k0 = k * 1024 + h * 512
                                for c in range(DC):
                                    last = pe.matmul(big[:, u % 2, h * 512:(h + 1) * 512],
                                                     R.xnT[:, c, b * S + q * P:b * S + (q + 1) * P],
                                                     KT[b][:, c, k0:k0 + 512], start=(c == 0), stop=(c == DC - 1))
                            last.then_inc(s_made, 1)
                            u += 1
                    pe.wait_ge(maxed, b + 1)
                    for q in range(QT):
                        last = pe.transpose(rp[:, q * P:(q + 1) * P], np3[:, q, :], R.identb[:, :])
                    last.then_inc(turned, 1)
                    pe.wait_ge(row_kept, 2 * b + 2)

                    def weigh(e):
                        pe.wait_ge(exp_done, b * EU + e + 1)
                        if e == 0:
                            pe.wait_ge(v_loaded[b], 16)
                        if e == 0 and b:
                            pe.wait_ge(normed, b)
                        for i in range(EK):
                            kt = e * EK + i
                            for q in range(QT):
                                last = pe.matmul(pv[:, q, 0:VW], PT[e % 3][:, i * S + q * P:i * S + (q + 1) * P],
                                                 V[b][:, kt, :], start=(kt == 0), stop=(kt == NKT - 1))
                        last.then_inc(pv_done, 1)

                    for e in range(EU):
                        if e >= 2:
                            pe.wait_ge(exp_done, b * EU + e - 1)
                        for half in range(EK // 2):
                            pe.matmul(big[:, e % 2, half * 512:(half + 1) * 512], ones3[:, :],
                                      nrow[:, :, :].rearrange("r t s -> r (t s)"), start=True, stop=False)
                            for i in (2 * half, 2 * half + 1):
                                kt = e * EK + i
                                for c in range(DC):
                                    last = pe.matmul(big[:, e % 2, i * S:(i + 1) * S], KT[b][:, c, kt * P:(kt + 1) * P],
                                                     R.xnT[:, c, b * S:(b + 1) * S], start=False,
                                                     stop=(i % 2 == 1 and c == DC - 1))
                        last.then_inc(st_made, 1)
                        if e >= 1:
                            weigh(e - 1)
                    weigh(EU - 1)

            @block.scalar
            def _(act):
                for e in range(B * EU):
                    act.wait_ge(st_made, e + 1)
                    if e >= 3:
                        act.wait_ge(pv_done, e - 2)
                    act.activation(PT[e % EU % 3][:, :], big[:, e % 2, :], ACT.Exp).then_inc(exp_done, 1)

            @block.vector
            def _(dve):
                for b in range(B):
                    for u in range(MU):
                        dve.wait_ge(s_made, b * MU + u + 1)
                        dve.tensor_reduce(mx[:, u // parts, u % parts:u % parts + 1], big[:, u % 2, :],
                                          AX.X, ALU.max).then_inc(s_read, 1)
                    dve.wait_ge(s_read, (b + 1) * MU)
                    dve.tensor_reduce(neg[:, :], mx[:, :, :], AX.X, ALU.max, negate=True).then_inc(split, 1)
                    dve.wait_ge(split, b * 4 + 1)
                    dve.tensor_copy(np3[:, :, 0], neg[:, :]).then_inc(split, 1)
                    dve.wait_ge(split, b * 4 + 2)
                    dve.tensor_tensor(rest[:, :], neg[:, :], np3[:, :, 0], ALU.subtract).then_inc(split, 1)
                    dve.wait_ge(split, b * 4 + 3)
                    dve.tensor_copy(np3[:, :, 1], rest[:, :]).then_inc(split, 1)
                    dve.wait_ge(split, b * 4 + 4)
                    dve.tensor_tensor(np3[:, :, 2], rest[:, :], np3[:, :, 1], ALU.subtract).then_inc(maxed, 1)
                    dve.wait_ge(turned, b + 1)
                    for twice in range(2):
                        dve.tensor_copy(nrow[:, twice, :], rp[:, :]).then_inc(row_kept, 1)
                    dve.wait_ge(pv_done, (b + 1) * EU)
                    dve.reciprocal(rsum[:, :], pv[:, :, D]).then_inc(summed, 1)
                    dve.wait_ge(summed, b + 1)
                    for q in range(QT):
                        ins = dve.tensor_scalar(att[:, b * QT + q, :], pv[:, q, 0:D], rsum[:, q:q + 1], None, ALU.mult)
                    ins.then_inc(normed, 1)


def combine_stage(nc, R, att, dram):
    with Stage(nc) as st:
        w, rowp = st.sb("w_comb", [P, 2 * DC, D]), st.sb("b_gamma_beta", [P, 3, D])
        aT = st.sb("attT", [P, DC, NT * P])
        y = st.sb("y", [P, NT, D])
        stats, mv, rstd = st.sb("stats", [P, NT, 6]), st.sb("mean_var", [P, NT, 2]), st.sb("rstd", [P, NT])
        tp = [st.ps("tp", [P, NT * P]) for _ in range(DC)]
        acc = [st.ps("acc", [P, 512]) for _ in range(NT)]
        loaded, turned, kept, made, step, rooted = (st.sem(n) for n in (
            "loaded", "turned", "kept", "made", "dve_step", "rooted"))
        with nc.Block() as block:

            @block.sync
            def _(sp):
                sp.dma_start(w[:, :, :], dram["w9"]).then_inc(loaded, 16)
                sp.dma_start(rowp[:, :, :], dram["r9"]).then_inc(loaded, 16)

            @block.tensor
            def _(pe):
                for c in range(DC):
                    for t in range(NT):
                        last = pe.transpose(tp[c][:, t * P:(t + 1) * P], att[:, t, c * P:(c + 1) * P], R.identf[:, :])
                    last.then_inc(turned, 1)
                pe.wait_ge(kept, DC)
                pe.wait_ge(loaded, 32)
                for t in range(NT):
                    for c in range(2 * DC):
                        src = aT if c < DC else R.xnT
                        last = pe.matmul(acc[t][:, 0:D], src[:, c % DC, t * P:(t + 1) * P], w[:, c, :],
                                         start=(c == 0), stop=(c == 2 * DC - 1))
                    last.then_inc(made, 1)

            @block.scalar
            def _(act):
                for c in range(DC):
                    act.wait_ge(turned, c + 1)
                    act.activation(aT[:, c, :], tp[c][:, :], ACT.Copy).then_inc(kept, 1)
                act.wait_ge(step, 3 * NT + 1)
                act.activation(rstd[:, :], rstd[:, :], ACT.Sqrt).then_inc(rooted, 1)

            @block.vector
            def _(dve):
                dve.wait_ge(loaded, 32)
                for t in range(NT):
                    dve.wait_ge(made, t + 1)
                    dve.tensor_tensor(y[:, t, :], acc[t][:, 0:D], rowp[:, 0, :], ALU.add).then_inc(step, 1)
                for t in range(NT):
                    dve.wait_ge(step, t + 1)
                    dve.bn_stats(stats[:, t, :], y[:, t, :]).then_inc(step, 1)
                for t in range(NT):
                    dve.wait_ge(step, NT + t + 1)
                    dve.bn_aggr(mv[:, t, :], stats[:, t, :]).then_inc(step, 1)
                dve.wait_ge(step, 3 * NT)
                dve.tensor_scalar(rstd[:, :], mv[:, :, 1], EPS, None, ALU.add).then_inc(step, 1)
                dve.wait_ge(rooted, 1)
                dve.reciprocal(rstd[:, :], rstd[:, :]).then_inc(step, 1)
                n = 3 * NT + 2
                dve.wait_ge(step, n)
                for t in range(NT):
                    dve.tensor_scalar(y[:, t, :], y[:, t, :], mv[:, t, 0:1], rstd[:, t:t + 1],
                                      ALU.subtract, ALU.mult).then_inc(step, 1)
                for k, op in ((1, ALU.mult), (2, ALU.add)):
                    for t in range(NT):
                        n += 1
                        dve.wait_ge(step, n)
                        dve.tensor_tensor(y[:, t, :], y[:, t, :], rowp[:, k, :], op).then_inc(step, 1)
                for t in range(NT):
                    n += 1
                    dve.wait_ge(step, n)
                    dve.tensor_tensor(R.x[:, t, :], R.x[:, t, :], y[:, t, :], ALU.add)


def quantised_stage(nc, R, dram):
    HT = 8
    MAGIC = 1.5 * 2.0 ** 23
    SMALL = 1e-8
    with Stage(nc) as st:
        w1, w2 = st.sb("w1", [P, HT, D]), st.sb("w2", [P, DC, HT * P])
        b1, b2 = st.sb("b1", [P, HT]), st.sb("b2", [P, DC])
        w1q, w2q = st.sb("w1q", [P, HT, D], BF16), st.sb("w2q", [P, DC, HT * P], BF16)
        w1T, w2T = st.sb("w1qT", [P, DC, HT * P], BF16), st.sb("w2qT", [P, HT, D], BF16)
        s1, s2, i1, i2 = (st.sb(n, [P, w]) for n, w in (("s1", HT), ("s2", DC), ("i1", HT), ("i2", DC)))
        c1, c2 = st.sb("bq1", [P, HT]), st.sb("bq2", [P, DC])
        pm, gm, gs, gi = (st.sb(n, [P, 2]) for n in ("part_max", "all_max", "in_scale", "in_inverse"))
        grow = st.sb("max_row", [1, 2])
        xq = st.sb("xq", [P, DC, NT * P], BF16)
        h, hq = st.sb("h", [P, HT, NT * P]), st.sb("hq", [P, HT, NT * P], BF16)
        yT = st.sb("yT", [P, DC, NT * P])
        wp = [st.ps("w_turned", [P, 1024], BF16) for _ in range(2)]
        tp = st.ps("max_turned", [P, 512])
        ps = [st.ps("h_ps", [P, NT * P]) for _ in range(3)]
        yp = [st.ps("y_turned", [P, 512]) for _ in range(2)]
        loaded, step, wq_ready, w_turned, w_kept = (st.sem(n) for n in (
            "loaded", "dve_step", "w_quantised", "w_turned", "w_kept"))
        maxed, m_turned, row_ready, x_ready, made, kept, bias_ready = (st.sem(n) for n in (
            "maxed", "max_turned", "max_row_ready", "x_quantised", "made", "kept", "bias_ready"))
        out_turned, part = st.sem("out_turned"), st.sem("h_part_max")
        with nc.Block() as block:

            @block.sync
            def _(sp):
                sp.dma_start(w1[:, :, :], dram["w11_1"]).then_inc(loaded, 16)
                sp.dma_start(b1[:, :], dram["b11_1"]).then_inc(loaded, 16)
                sp.dma_start(w2[:, :, :], dram["w11_2"]).then_inc(loaded, 16)
                sp.dma_start(b2[:, :], dram["b11_2"]).then_inc(loaded, 16)

            @block.vector
            def _(dve):
                n = 0

                def did(ins):
                    nonlocal n
                    ins.then_inc(step, 1)
                    n += 1

                def round_to(out, src, inverse, low, high):
                    did(dve.tensor_scalar(src, src, inverse, MAGIC, ALU.mult, ALU.add))
                    dve.wait_ge(step, n)
                    did(dve.tensor_scalar(src, src, -MAGIC, low, ALU.add, ALU.max))
                    dve.wait_ge(step, n)
                    return dve.tensor_scalar(out, src, high, None, ALU.min)

                def weights(w, wq, s, inv, count):
                    did(dve.tensor_reduce(s[:, :], w[:, :, :], AX.X, ALU.max, apply_absolute_value=True))
                    dve.wait_ge(step, n)
                    did(dve.tensor_scalar(s[:, :], s[:, :], SMALL, 1.0 / 127.0, ALU.max, ALU.mult))
                    dve.wait_ge(step, n)
                    did(dve.reciprocal(inv[:, :], s[:, :]))
                    dve.wait_ge(step, n)
                    for f in range(count):
                        round_to(wq[:, f, :], w[:, f, :], inv[:, f:f + 1], -128.0, 127.0).then_inc(wq_ready, 1)

                def input_scale(k):
                    dve.wait_ge(m_turned, 2 * k + 1)
                    dve.tensor_reduce(grow[:, k:k + 1], tp[0:1, 0:P], AX.X, ALU.max).then_inc(row_ready, 1)
                    dve.wait_ge(m_turned, 2 * k + 2)
                    did(dve.tensor_scalar(gs[:, k:k + 1], tp[:, P:P + 1], SMALL, 1.0 / 255.0, ALU.max, ALU.mult))
                    dve.wait_ge(step, n)
                    did(dve.reciprocal(gi[:, k:k + 1], gs[:, k:k + 1]))
                    dve.wait_ge(step, n)

                def bias(s, inv, b, c, k):
                    did(dve.tensor_scalar(s[:, :], s[:, :], gs[:, k:k + 1], None, ALU.mult))
                    dve.wait_ge(step, n)
                    did(dve.reciprocal(inv[:, :], s[:, :]))
                    dve.wait_ge(step, n)
                    did(dve.tensor_tensor(c[:, :], b[:, :], inv[:, :], ALU.mult))
                    dve.wait_ge(step, n)
                    did(dve.tensor_scalar(c[:, :], c[:, :], MAGIC, -MAGIC, ALU.add, ALU.add))
                    dve.wait_ge(step, n)
                    dve.tensor_tensor(c[:, :], c[:, :], s[:, :], ALU.mult).then_inc(bias_ready, 1)

                dve.tensor_reduce(pm[:, 0:1], R.xnT[:, :, :], AX.XY, ALU.max).then_inc(maxed, 1)
                dve.wait_ge(loaded, 64)
                weights(w1, w1q, s1, i1, HT)
                input_scale(0)
                for c in range(DC):
                    round_to(xq[:, c, :], R.xnT[:, c, :], gi[:, 0:1], 0.0, 255.0).then_inc(x_ready, 1)
                bias(s1, i1, b1, c1, 0)
                weights(w2, w2q, s2, i2, DC)
                dve.wait_ge(kept, HT)
                dve.tensor_reduce(pm[:, 1:2], h[:, :, :], AX.XY, ALU.max).then_inc(maxed, 1)
                input_scale(1)
                for c in range(HT):
                    round_to(hq[:, c, :], h[:, c, :], gi[:, 1:2], 0.0, 255.0).then_inc(x_ready, 1)
                bias(s2, i2, b2, c2, 1)
                for t in range(NT):
                    dve.wait_ge(out_turned, t // 2 * 2 + 2)
                    dve.tensor_tensor(R.x[:, t, :], R.x[:, t, :], yp[t // 2][:, (t % 2) * D:(t % 2 + 1) * D], ALU.add)

            @block.tensor
            def _(pe):
                def all_max(k):
                    pe.wait_ge(maxed, k + 1)
                    pe.transpose(tp[0:1, 0:P], pm[:, k:k + 1], R.identf[:, :]).then_inc(m_turned, 1)
                    pe.wait_ge(row_ready, k + 1)
                    pe.matmul(tp[:, P:P + 1], R.onesf[0:1, :], grow[:, k:k + 1], start=True, stop=True)\
                      .then_inc(m_turned, 1)

                all_max(0)
                for c in range(DC):
                    pe.wait_ge(wq_ready, HT)
                    for f in range(HT):
                        last = pe.transpose(wp[c][:, f * P:(f + 1) * P], w1q[:, f, c * P:(c + 1) * P], R.identb[:, :])
                    last.then_inc(w_turned, 1)
                pe.wait_ge(w_kept, 2)
                pe.wait_ge(x_ready, DC)
                for f in range(HT):
                    if f >= 3:
                        pe.wait_ge(kept, f - 2)
                    for c in range(DC):
                        last = pe.matmul(ps[f % 3][:, :], w1T[:, c, f * P:(f + 1) * P], xq[:, c, :],
                                         start=(c == 0), stop=(c == DC - 1))
                    last.then_inc(made, 1)
                pe.wait_ge(wq_ready, HT + DC)
                for o in range(2):
                    for f in range(4):
                        for c in range(DC):
                            last = pe.transpose(wp[o][:, f * D + c * P:f * D + (c + 1) * P],
                                                w2q[:, c, (4 * o + f) * P:(4 * o + f + 1) * P], R.identb[:, :])
                    last.then_inc(w_turned, 1)
                pe.wait_ge(kept, HT)
                all_max(1)
                pe.wait_ge(w_kept, 4)
                pe.wait_ge(x_ready, DC + HT)
                for o in range(DC):
                    for f in range(HT):
                        last = pe.matmul(ps[o][:, :], w2T[:, f, o * P:(o + 1) * P], hq[:, f, :],
                                         start=(f == 0), stop=(f == HT - 1))
                    last.then_inc(made, 1)
                pe.wait_ge(kept, HT + DC)
                for t in range(NT):
                    for o in range(DC):
                        last = pe.transpose(yp[t // 2][:, (t % 2) * D + o * P:(t % 2) * D + (o + 1) * P],
                                            yT[:, o, t * P:(t + 1) * P], R.identf[:, :])
                    last.then_inc(out_turned, 1)

            @block.scalar
            def _(act):
                for c in range(DC):
                    act.wait_ge(w_turned, c + 1)
                    act.activation(w1T[:, c, :], wp[c][:, :], ACT.Copy).then_inc(w_kept, 1)
                act.wait_ge(bias_ready, 1)
                for f in range(HT):
                    act.wait_ge(made, f + 1)
                    act.activation(h[:, f, :], ps[f % 3][:, :], ACT.Relu, bias=c1[:, f:f + 1],
                                   scale=s1[:, f:f + 1]).then_inc(kept, 1)
                for o in range(2):
                    act.wait_ge(w_turned, 3 + o)
                    act.activation(w2T[:, 4 * o:4 * (o + 1), :], wp[o][:, :].rearrange("p (f m) -> p f m", f=4),
                                   ACT.Copy).then_inc(w_kept, 1)
                act.wait_ge(bias_ready, 2)
                for o in range(DC):
                    act.wait_ge(made, HT + o + 1)
                    act.activation(yT[:, o, :], ps[o][:, :], ACT.Identity, bias=c2[:, o:o + 1],
                                   scale=s2[:, o:o + 1]).then_inc(kept, 1)


def mamba_stages(nc, R, dram):
    CT, NS, K = 4, 16, 4
    T = NT * P
    bc_d = nc.dram_tensor("bc_rows", [2 * NS, T], F32, kind="Internal").ap()
    with ExitStack() as keep:
        def sb(name, shape, dt=F32):
            return keep.enter_context(nc.sbuf_tensor("ssm_" + name, shape, dt))

        actT, gate, delta, dx = (sb(n, [P, CT, T]) for n in ("act", "gate", "delta", "dx"))
        yT, A = sb("y", [P, CT, T]), sb("A", [P, CT, NS])
        cols = sb("cols", [P, CT, 9])
        BI, BG, CB, BD, DS, TAP = 0, 1, 2, 3, 4, 5
        wd = sb("w_delta", [P, CT, CT * P])
        wbc = sb("w_bc", [P, CT, 2 * NS])

        with Stage(nc) as st:
            win, wg = st.sb("w_in", [P, DC, CT * P]), st.sb("w_gate", [P, DC, CT * P])
            xz = st.sb("xz", [P, CT, B, K - 1 + S])
            cv = st.sb("conv", [P, CT, T])
            ps = [st.ps("ps", [P, T]) for _ in range(4)]
            loaded, made, xz_kept, conv, gate_kept, acted, zeroed = (st.sem(n) for n in (
                "loaded", "made", "xz_kept", "conv_step", "gate_kept", "acted", "zeroed"))
            with nc.Block() as block:

                @block.sync
                def _(sp):
                    sp.dma_start(cols[:, :, :], dram["s_cols"]).then_inc(loaded, 16)
                    sp.dma_start(win[:, :, :], dram["s_win"]).then_inc(loaded, 16)
                    sp.dma_start(wg[:, :, :], dram["s_wgate"]).then_inc(loaded, 16)
                    sp.dma_start(A[:, :, :], dram["s_alog"]).then_inc(loaded, 16)
                    sp.dma_start(wd[:, :, :], dram["s_wdelta"]).then_inc(loaded, 16)
                    sp.dma_start(wbc[:, :, :], dram["s_wbc"]).then_inc(loaded, 16)

                @block.gpsimd
                def _(pool):
                    pool.memset(xz[:, :, :, 0:K - 1], 0.0).then_inc(zeroed, 1)

                @block.tensor
                def _(pe):
                    pe.wait_ge(loaded, 96)
                    for n in range(2 * CT):
                        w, f = (win, n) if n < CT else (wg, n - CT)
                        if n >= 4:
                            pe.wait_ge(xz_kept, n - 3)
                        for c in range(DC):
                            last = pe.matmul(ps[n % 4][:, :], w[:, c, f * P:(f + 1) * P], R.xnT[:, c, :],
                                             start=(c == 0), stop=(c == DC - 1))
                        last.then_inc(made, 1)

                @block.vector
                def _(dve):
                    dve.wait_ge(zeroed, 1)
                    for f in range(CT):
                        dve.wait_ge(xz_kept, f + 1)
                        dst = cv[:, f, :].rearrange("p (b s) -> p b s", b=B)
                        for k in range(K):
                            src = xz[:, f, :, k:k + S]
                            tap = cols[:, f, TAP + k:TAP + k + 1]
                            if k == 0:
                                dve.tensor_scalar(dst, src, tap, None, ALU.mult).then_inc(conv, 1)
                            else:
                                dve.wait_ge(conv, f * K + k)
                                dve.scalar_tensor_tensor(out=dst, in0=src, scalar=tap, in1=dst,
                                                         op0=ALU.mult, op1=ALU.add).then_inc(conv, 1)

                @block.scalar
                def _(act):
                    for f in range(CT):
                        act.wait_ge(made, f + 1)
                        act.activation(xz[:, f, :, K - 1:K - 1 + S], ps[f][:, :].rearrange("p (b s) -> p b s", b=B),
                                       ACT.Identity, bias=cols[:, f, BI:BI + 1]).then_inc(xz_kept, 1)
                    for f in range(CT):
                        act.wait_ge(made, CT + f + 1)
                        act.activation(gate[:, f, :], ps[f][:, :], ACT.Silu, bias=cols[:, f, BG:BG + 1])
                    for f in range(CT):
                        act.wait_ge(conv, (f + 1) * K)
                        act.activation(actT[:, f, :], cv[:, f, :], ACT.Silu, bias=cols[:, f, CB:CB + 1])
                    act.activation(A[:, :, :], A[:, :, :], ACT.Exp).then_inc(acted, 1)

        with Stage(nc) as st:
            z, ez = st.sb("z", [P, CT, T]), st.sb("ez", [P, CT, T])
            bc = st.sb("bc", [2 * NS, T])
            ps = [st.ps("ps", [P, T]) for _ in range(CT)]
            bp = st.ps("bc_ps", [2 * NS, T])
            made, kept, lned, step, bc_made, stored = (st.sem(n) for n in (
                "made", "z_kept", "ln_done", "dve_step", "bc_kept", "bc_stored"))
            with nc.Block() as block:

                @block.tensor
                def _(pe):
                    for c in range(CT):
                        last = pe.matmul(bp[:, :], wbc[:, c, :], actT[:, c, :], start=(c == 0), stop=(c == CT - 1))
                    last.then_inc(made, 1)
                    for f in range(CT):
                        for c in range(CT):
                            last = pe.matmul(ps[f][:, :], wd[:, c, f * P:(f + 1) * P], actT[:, c, :],
                                             start=(c == 0), stop=(c == CT - 1))
                        last.then_inc(made, 1)

                @block.sync
                def _(sp):
                    sp.wait_ge(bc_made, 1)
                    sp.dma_start(bc_d, bc[:, :]).then_inc(stored, 16)
                    sp.wait_ge(stored, 16)

                @block.scalar
                def _(act):
                    act.wait_ge(made, 1)
                    act.activation(bc[:, :], bp[:, :], ACT.Copy).then_inc(bc_made, 1)
                    for f in range(CT):
                        act.wait_ge(made, f + 2)
                        act.activation(z[:, f, :], ps[f][:, :], ACT.Identity, bias=cols[:, f, BD:BD + 1])\
                           .then_inc(kept, 1)
                    act.wait_ge(kept, CT)
                    act.activation(ez[:, :, :], z[:, :, :], ACT.Abs).then_inc(kept, 1)
                    act.wait_ge(kept, CT + 1)
                    act.activation(ez[:, :, :], ez[:, :, :], ACT.Exp, scale=-1.0).then_inc(kept, 1)
                    act.wait_ge(kept, CT + 2)
                    act.activation(ez[:, :, :], ez[:, :, :], ACT.Ln, bias=1.0).then_inc(lned, 1)

                @block.vector
                def _(dve):
                    dve.tensor_scalar(A[:, :, :], A[:, :, :], -1.0, None, ALU.mult)
                    dve.wait_ge(lned, 1)
                    dve.tensor_scalar(delta[:, :, :], z[:, :, :], 0.0, None, ALU.max).then_inc(step, 1)
                    dve.wait_ge(step, 1)
                    dve.tensor_tensor(delta[:, :, :], delta[:, :, :], ez[:, :, :], ALU.add).then_inc(step, 1)
                    dve.wait_ge(step, 2)
                    dve.tensor_tensor(dx[:, :, :], delta[:, :, :], actT[:, :, :], ALU.mult)

        with Stage(nc) as st:
            bcb = st.sb("bc_all", [P, 2 * NS, T])
            dA, dB = ([st.sb(n, [P, T]) for _ in range(k)] for n, k in (("dA", 2), ("dBx", CT)))
            hh, hc = ([st.sb(n, [P, T]) for _ in range(2)] for n in ("h", "hC"))
            zero = st.sb("zero", [P, T])
            An = st.sb("A_now", [P, CT])
            yp = [st.ps("y_ps", [P, T]) for _ in range(CT)]
            loaded = [st.sem("bc_loaded") for _ in range(NS // 4)]
            a_ready, da, db, scanned, hc_ready, summed = (st.sem(n) for n in (
                "A_ready", "dA_ready", "dBx_ready", "scanned", "hC_ready", "summed"))
            cleared = st.sem("cleared")
            passed = st.sem("wait_passed")
            SC, HC, SU = 4, 2, 2
            with nc.Block() as block:

                @block.sync
                def _(sp):
                    for k in range(NS // 4):
                        for r in (4 * k, NS + 4 * k):
                            sp.dma_start(bcb[:, r:r + 4, :], bc_d[r:r + 4].partition_broadcast(P))\
                              .then_inc(loaded[k], 16)
                    for k in range(NS // 4):
                        sp.wait_ge(loaded[k], 32)

                @block.scalar
                def _(act):
                    act.sem_inc(a_ready, 1)
                    act.sem_inc(da, 1)
                    with act.Fori(0, NS) as n:
                        act.wait_ge(da, n * CT + 1)
                        act.activation(An[:, :], A[:, :, bass.ds(n, 1)].rearrange("p c o -> p (c o)"), ACT.Copy)\
                           .then_inc(a_ready, 1)
                        act.wait_ge(a_ready, n + 2)
                        for i in range(CT):
                            act.wait_ge(scanned, n * CT + (i - 1 + SC))
                            act.activation(dA[i % 2][:, :], delta[:, i, :], ACT.Exp, scale=An[:, i:i + 1])\
                               .then_inc(da, 1)

                @block.vector
                def _(dve):
                    dve.memset(zero[:, :], 0.0).then_inc(cleared, 1)
                    dve.sem_inc(scanned, SC)
                    dve.sem_inc(hc_ready, HC)
                    for k in range(NS // 4):
                        dve.wait_ge(loaded[k], 32)
                        with dve.Fori(4 * k, 4 * k + 4) as n:
                            for i in range(CT):
                                dve.wait_ge(da, n * CT + (i + 2))
                                dve.wait_ge(db, n * CT + (i + 1))
                                dve.wait_ge(hc_ready, n * CT + (i - 1 + HC))
                                for b in range(B):
                                    s = slice(b * S, (b + 1) * S)
                                    ins = dve.tensor_tensor_scan(hh[i % 2][:, s], dA[i % 2][:, s], dB[i][:, s],
                                                                 0.0, ALU.mult, ALU.add)
                                ins.then_inc(scanned, 1)
                                dve.wait_ge(scanned, n * CT + (i + 1 + SC))
                                dve.wait_ge(summed, n * CT + (i - 1 + SU))
                                dve.tensor_tensor(hc[i % 2][:, :], hh[i % 2][:, :],
                                                  bcb[:, bass.ds(n + NS, 1), :].rearrange("p o t -> p (o t)"),
                                                  ALU.mult).then_inc(hc_ready, 1)

                @block.gpsimd
                def _(pool):
                    for k in range(NS // 4):
                        pool.wait_ge(loaded[k], 32)
                        with pool.Fori(4 * k, 4 * k + 4) as n:
                            for i in range(CT):
                                pool.wait_ge(scanned, n * CT + (i - CT + 1 + SC))
                                pool.sem_inc(passed, 1)
                                pool.tensor_tensor(dB[i][:, :], dx[:, i, :],
                                                   bcb[:, bass.ds(n, 1), :].rearrange("p o t -> p (o t)"), ALU.mult)\
                                    .then_inc(db, 1)

                @block.tensor
                def _(pe):
                    pe.sem_inc(summed, SU - 1)
                    pe.wait_ge(cleared, 1)
                    for i in range(CT):
                        last = pe.matmul(yp[i][:, :], R.identf[:, :], zero[:, :], start=True, stop=False,
                                         skip_group_check=True)
                    last.then_inc(summed, 1)
                    with pe.Fori(0, NS) as n:
                        for i in range(CT):
                            pe.wait_ge(hc_ready, n * CT + (i + 1 + HC))
                            pe.matmul(yp[i][:, :], R.identf[:, :], hc[i % 2][:, :], start=False, stop=False,
                                      skip_group_check=True).then_inc(summed, 1)
                    for i in range(CT):
                        pe.matmul(yp[i][:, :], R.identf[:, :], zero[:, :], start=False, stop=True,
                                  skip_group_check=True).then_inc(summed, 1)

            with nc.Block() as block:

                @block.vector
                def _(dve):
                    for i in range(CT):
                        dve.scalar_tensor_tensor(out=yT[:, i, :], in0=actT[:, i, :], scalar=cols[:, i, DS:DS + 1],
                                                 in1=yp[i][:, :], op0=ALU.mult, op1=ALU.add).then_inc(cleared, 1)
                    for i in range(CT):
                        dve.wait_ge(cleared, i + 2)
                        dve.tensor_tensor(yT[:, i, :], yT[:, i, :], gate[:, i, :], ALU.mult)

        with Stage(nc) as st:
            wo, bo = st.sb("w_out", [P, CT, D]), st.sb("b_out", [P, D])
            ps = [st.ps("ps", [P, 512]) for _ in range(NT)]
            loaded, made, biased = st.sem("loaded"), st.sem("made"), st.sem("biased")
            with nc.Block() as block:

                @block.sync
                def _(sp):
                    sp.dma_start(wo[:, :, :], dram["s_wout"]).then_inc(loaded, 16)
                    sp.dma_start(bo[:, :], dram["s_bout"]).then_inc(loaded, 16)

                @block.tensor
                def _(pe):
                    pe.wait_ge(loaded, 32)
                    for t in range(NT):
                        for c in range(CT):
                            last = pe.matmul(ps[t][:, 0:D], yT[:, c, t * P:(t + 1) * P], wo[:, c, :],
                                             start=(c == 0), stop=(c == CT - 1))
                        last.then_inc(made, 1)

                @block.vector
                def _(dve):
                    dve.wait_ge(loaded, 32)
                    for t in range(NT):
                        dve.tensor_tensor(R.x[:, t, :], R.x[:, t, :], bo[:, :], ALU.add).then_inc(biased, 1)
                    for t in range(NT):
                        dve.wait_ge(biased, t + 1)
                        dve.wait_ge(made, t + 1)
                        dve.tensor_tensor(R.x[:, t, :], R.x[:, t, :], ps[t][:, 0:D], ALU.add)


class Resident:
    pass


def build(nc, dram, out):
    R = Resident()
    Stage.number = 0
    with ExitStack() as keep:
        def sb(name, shape, dt=F32):
            return keep.enter_context(nc.sbuf_tensor(name, shape, dt))

        R.x, R.xn = sb("x_res", [P, NT, D]), sb("xn", [P, NT, D])
        R.xnT = sb("xnT", [P, DC, NT * P])
        R.identf, R.identb, R.onesf = sb("identf", [P, P]), sb("identb", [P, P], BF16), sb("onesf", [P, P])
        R.stored = nc.alloc_semaphore("out_stored")
        setup_stage(nc, R, dram["x"])

        def attend_self(layer, scale, **how):
            norm_stage(nc, R)
            with nc.sbuf_tensor(f"att{layer}", [P, NT, D], F32) as att:
                self_attention_stage(nc, R, att, dram[f"w{layer}"], scale, (dram["causal_q"], dram["causal_k"]), **how)
                add_projected_stage(nc, R, att, D, dram[f"o{layer}"], None)

        parts_d = nc.dram_tensor("key_parts_rows", [3, D, SK], BF16, kind="Internal").ap()

        def attend_context(layer, out_bias, **how):
            norm_stage(nc, R)
            with nc.sbuf_tensor(f"att{layer}", [P, NT, D], F32) as att:
                split_context_stage(nc, R, att, (dram[f"w{layer}"], dram[f"b{layer}"], dram["group_sum"]), 0.25,
                                    dram["ctxT"], parts_d, **how)
                add_projected_stage(nc, R, att, D, dram[f"o{layer}"], dram[f"ob{layer}"] if out_bias else None)

        if 0 in LAYERS:
            attend_context(0, True, masks=(dram["m0q"], dram["m0k"]))
        if 1 in LAYERS:
            attend_self(1, 1.0 / 16, rope=dram["rope"])
        if 2 in LAYERS:
            norm_stage(nc, R)
            experts_stage(nc, R, dram, 2, 10, ACT.Gelu, 0.5)
        if 3 in LAYERS:
            norm_stage(nc, R)
            with nc.sbuf_tensor("att3", [P, NT, 1024], F32) as att:
                wide_context_stage(nc, R, att, dram["w3"], 0.125, dram["ctxT"], (dram["m3q"], dram["m3k"]),
                                   dram["half_sum"])
                add_projected_stage(nc, R, att, 1024, dram["o3"], dram["ob3"])
        if 4 in LAYERS:
            scratch = nc.dram_tensor("mixed_heads", [B, 16, S, 16], F32, kind="Internal").ap()
            norm_stage(nc, R)
            head_mix_stage(nc, R, dram, scratch)
            with nc.sbuf_tensor("att4", [P, NT, D], F32) as att:
                reload_stage(nc, att, scratch)
                add_projected_stage(nc, R, att, D, dram["o4"], dram["ob4"])
        if 5 in LAYERS:
            norm_stage(nc, R)
            experts_stage(nc, R, dram, 5, 9, ACT.Silu, 1.0)
        if 6 in LAYERS:
            attend_context(6, False, key_mask=dram["m6"])
        if 7 in LAYERS:
            norm_stage(nc, R)
            mamba_stages(nc, R, dram)
        if 8 in LAYERS:
            norm_stage(nc, R)
            signs_stage(nc, R, dram)
        if 9 in LAYERS:
            norm_stage(nc, R)
            with nc.sbuf_tensor("att9", [P, NT, D], F32) as att:
                context_stage(nc, R, att, dram["ctxT"], dram["ctx"])
                combine_stage(nc, R, att, dram)
        if 10 in LAYERS:
            attend_self(10, 0.25)
        if 11 in LAYERS:
            norm_stage(nc, R)
            quantised_stage(nc, R, dram)
        store_stage(nc, R, out)


def store_stage(nc, R, out):
    with nc.Block() as block:

        @block.sync
        def _(sp):
            sp.dma_start(out, R.x[:, :, :]).then_inc(R.stored, 16)
            sp.wait_ge(R.stored, 16)



def kernel(**inputs):
    import concourse.bacc as bacc
    from concourse.bass_utils import run_bass_kernel_spmd as run

    a = {k: np.asarray(v) for k, v in inputs.items()}
    nc = bacc.Bacc("TRN2", target_bir_lowering=False, num_devices=1)
    arrays, dram = {}, {}

    def give(name, v):
        v = np.ascontiguousarray(v)
        arrays["in_" + name] = v
        dram[name] = nc.dram_tensor("in_" + name, v.shape, mybir.dt.from_np(v.dtype), kind="ExternalInput").ap()

    def rows(w):
        return w.reshape(-1, P, w.shape[-1]).transpose(1, 0, 2)

    def spread(v):
        return np.broadcast_to(v.reshape(1, -1), (P, v.size))

    def words(m):
        return np.ascontiguousarray(m).view(np.int32)

    def both_masks(m):
        m = m.view(np.uint8)
        nk = m.shape[2]
        return (m.reshape(B, QT, P, nk).transpose(0, 2, 1, 3).reshape(B, P, QT * nk),
                m.reshape(B, S, nk // P, P).transpose(0, 3, 2, 1).reshape(B, P, nk // P * S))

    def rope_tables():
        inv = (np.float32(1.0) / np.float32(10000.0) ** (np.arange(0, 16, 2, dtype=np.float32) / np.float32(16))).astype(np.float32)
        freq = (np.arange(S, dtype=np.float32)[:, None] * inv[None, :]).astype(np.float32)
        cos, sin = np.zeros((S, 16, 8, 2), np.float32), np.zeros((S, 16, 8, 2), np.float32)
        cos[:] = np.cos(freq)[:, None, :, None]
        sin[:] = np.sin(freq)[:, None, :, None] * np.array([-1, 1], np.float32)
        return np.stack([rows(cos.reshape(S, D)), rows(sin.reshape(S, D))], 2)

    give("x", rows(a["x"].reshape(B * S, D)))
    ctx = a["ctx_1024"]
    give("ctxT", ctx.reshape(B, SK, DC, P).transpose(0, 3, 2, 1))
    for n, m in zip(("m0q", "m0k"), both_masks(a["mask_BxSxS2_bf0"])):
        give(n, words(m))
    for n, m in zip(("m3q", "m3k"), both_masks(a["mask_BxSxS2_bk1"])):
        give(n, words(m))
    later = np.arange(S)[None, :] > np.arange(S)[:, None]
    for n, m in zip(("causal_q", "causal_k"), both_masks(np.broadcast_to(later, (B, S, S)).copy())):
        give(n, words(m))
    give("m6", a["mask_BxS2_ik1"])
    give("rope", rope_tables())

    def ones_after(v):
        out = np.zeros((v.shape[0], 16, 17), np.float32)
        out[:, :, :16] = v.reshape(-1, 16, 16)
        return out

    def kqv(name):
        return rows(np.concatenate([a[name + "Wk"], a[name + "Wq"], ones_after(a[name + "Wv"]).reshape(D, -1)], 1))

    def kqv_bias(bk, bq, bv):
        vb = ones_after(bv[None])
        vb[:, :, 16] = 1.0
        return np.concatenate([bk.reshape(2, P).T, spread(bq), spread(vb)], 1)

    give("w0", kqv("L0_xattn_"))
    give("b0", kqv_bias(a["L0_xattn_bk"], a["L0_xattn_bq"], a["L0_xattn_bv"]))
    group_sum = np.zeros((P, 32), np.float32)
    group_sum[np.arange(P), np.arange(P) % 32] = 1.0
    give("group_sum", group_sum)
    give("o0", rows(a["L0_xattn_Wo"]))
    give("ob0", spread(a["L0_xattn_bo"]))
    swap = np.arange(D) ^ 1
    give("w1", rows(np.concatenate([a["L0_attn_qw"], a["L0_attn_kw"], a["L0_attn_qw"][:, swap],
                                    a["L0_attn_kw"][:, swap], a["L0_attn_vw"]], 1)))
    give("o1", rows(a["L0_attn_ow"]))
    def by_fours(w):
        return w.reshape(DC, P, 4, 256).transpose(2, 1, 0, 3)

    give("w3", np.concatenate([by_fours(a["L1_xattn_" + n]) for n in ("Wk", "Wq", "Wv")], 3))
    half_sum = np.zeros((P, 64), np.float32)
    half_sum[np.arange(P), np.arange(P) % 64] = 1.0
    give("half_sum", half_sum)
    give("o3", rows(a["L1_xattn_Wo"]))
    give("ob3", spread(a["L1_xattn_bo"]))
    give("w4", rows(np.concatenate([a["L1_attn_" + n].T for n in ("Wq", "Wk", "Wv")], 1)))
    give("b4", spread(np.concatenate([a["L1_attn_" + n] for n in ("bq", "bk", "bv")])))
    give("o4", rows(a["L1_attn_Wo"].T))
    give("ob4", spread(a["L1_attn_bo"]))
    give("w6", kqv("L2_xattn_"))
    give("b6", kqv_bias(*[np.zeros(D, np.float32)] * 3))
    give("o6", rows(a["L2_xattn_Wo"]))
    give("w10", rows(a["L3_attn_in_proj_weight"].T))
    give("o10", rows(a["L3_attn_out_proj_weight"].T))

    def all_experts(routed, shared):
        w = np.concatenate([routed, shared], 0)
        return w.reshape(len(w), -1, P, w.shape[2]).transpose(0, 2, 1, 3)

    give("descending", spread(np.arange(8, 0, -1).astype(np.float32)))
    give("rw2", rows(a["L0_ffn_router_w"]))
    give("rb2", spread(a["L0_ffn_router_b"]))
    give("e1_2", all_experts(a["L0_ffn_w1"], a["L0_ffn_sw1"]))
    give("e2_2", all_experts(a["L0_ffn_w2"], a["L0_ffn_sw2"]))
    give("b1_2", np.concatenate([a["L0_ffn_b1"], a["L0_ffn_sb1"]]).reshape(10, 4, P).transpose(0, 2, 1))
    give("b2_2", np.concatenate([a["L0_ffn_b2"], a["L0_ffn_sb2"]]))
    give("rw5", rows(a["L1_ffn_router_w"].T))
    give("rb5", spread(a["L1_ffn_experts_bias"]))
    give("e1_5", all_experts(a["L1_ffn_w1"], a["L1_ffn_sw1"]))
    give("e3_5", all_experts(a["L1_ffn_w3"], a["L1_ffn_sw3"]))
    give("e2_5", all_experts(a["L1_ffn_w2"], a["L1_ffn_sw2"]))

    for k in ("k0", "k1", "k2"):
        give(k, words(rows(a["L2_ffn_" + k].view(np.uint8))))
    give("signs_scales", spread(np.stack([a["L2_ffn_s0"], a["L2_ffn_s1"], a["L2_ffn_s2"]])))

    give("ctx", ctx.reshape(B, SK // P, P, D).transpose(0, 2, 1, 3))
    give("w9", rows(a["L3_xattn_W"].T))
    r9 = np.stack([a["L3_xattn_b"], a["L3_xattn_gamma"], a["L3_xattn_beta"]])
    give("r9", np.broadcast_to(r9[None], (P, 3, D)))

    give("w11_1", rows(a["L3_ffn_w1"]))
    give("w11_2", rows(a["L3_ffn_w2"]))
    give("b11_1", a["L3_ffn_b1"].reshape(8, P).T)
    give("b11_2", a["L3_ffn_b2"].reshape(DC, P).T)

    m = {k[8:]: v for k, v in a.items() if k.startswith("L2_attn_")}
    tiles = [m[k].reshape(4, P).T for k in ("b_in", "b_gate", "conv_b", "b_delta", "D_skip")]
    taps = m["conv_w"].reshape(4, P, 4).transpose(1, 0, 2)
    give("s_cols", np.concatenate([np.stack(tiles, 2), taps], 2))
    give("s_win", rows(m["W_in"]))
    give("s_wgate", rows(m["W_gate"]))
    give("s_alog", rows(m["A_log"]))
    give("s_wdelta", rows(m["W_delta"]))
    give("s_wbc", rows(np.concatenate([m["W_B"], m["W_C"]], 1)))
    give("s_wout", rows(m["W_out"]))
    give("s_bout", spread(m["b_out"]))

    out = nc.dram_tensor("out_x", (P, NT, D), F32, kind="ExternalOutput").ap()
    build(nc, dram, out)
    r = run(nc, [arrays], core_ids=[0])
    got = r.results[0]["out_x"]
    return got.transpose(1, 0, 2).reshape(B, S, D)
```
